# Optimizing a Trainium2 kernel written in Bass

```python
import numpy as np
import jax
import jax.numpy as jnp

def _softmax(x, axis=-1):
    return jax.nn.softmax(x, axis=axis)

def _gelu(x):
    return jax.nn.gelu(x, approximate=True)

def _silu(x):
    return jax.nn.silu(x)

def _sigmoid(x):
    return jax.nn.sigmoid(x)

def _layernorm(x, axis=-1, eps=1e-05):
    m = jnp.mean(x, axis=axis, keepdims=True)
    v = jnp.var(x, axis=axis, keepdims=True)
    return (x - m) / jnp.sqrt(v + eps)

def _scatter_add(tgt, idx, src, axis=0):
    return tgt.at[idx].add(src)

def _segment_sum(src, seg, n):
    return jax.ops.segment_sum(src, seg, n)
kernel_name = 'mk_xattn_ffn_d2_seqx_r8_2da4b2'

def setup_inputs(seed: int=0):
    np.random.seed(seed)
    _w = jnp.asarray

    def _rec_inputs():
        import jax
        import jax.numpy as jnp
        _rk = jax.random.key(seed)
        x = -0.0005207 + 1.001 * jax.random.normal(jax.random.fold_in(_rk, 1), (8, 256, 128), jnp.float32)
        _lenS = 256 - jax.random.randint(jax.random.fold_in(_rk, 7), (8,), 0, max(1, 256 // 4) + 1, jnp.int32)
        _lenS2 = 512 - jax.random.randint(jax.random.fold_in(_rk, 8), (8,), 0, max(1, 512 // 4) + 1, jnp.int32)
        _ctx_1024P = jax.random.normal(jax.random.fold_in(_rk, 11), (8, 16, 128), jnp.float32)
        _ctx_1024c = jax.random.dirichlet(jax.random.fold_in(_rk, 511), 0.3 * jnp.ones((16,), jnp.float32), (8, 512))
        _ctx_1024t = jnp.einsum('bsk,bkd->bsd', _ctx_1024c, _ctx_1024P)
        _ctx_1024t = _ctx_1024t * jax.lax.rsqrt(jnp.mean(jnp.square(_ctx_1024t)) + 1e-12) * 0.953939
        ctx_1024 = -1.39393e-06 + 0.999914 * (_ctx_1024t + 0.3 * jax.random.normal(jax.random.fold_in(_rk, 611), (8, 512, 128), jnp.float32))
        itok_BxS_0_1023 = jax.random.randint(jax.random.fold_in(_rk, 12), (8, 256), 0, 128, jnp.int32)
        itok_BxS2_0_2047 = jax.random.randint(jax.random.fold_in(_rk, 13), (8, 512), 0, 256, jnp.int32)
        _validS = jnp.arange(256)[None, :] < _lenS[:, None]
        _validS2 = jnp.arange(512)[None, :] < _lenS2[:, None]
        _causal = jnp.tril(jnp.ones((256, 256), dtype=bool))
        mask_Bx1x1xS2_bf0 = jnp.logical_not(jnp.ones((8, 1, 1, 512), dtype=bool))
        return (x, ctx_1024, itok_BxS_0_1023, itok_BxS2_0_2047, mask_Bx1x1xS2_bf0)
    x, ctx_1024, itok_BxS_0_1023, itok_BxS2_0_2047, mask_Bx1x1xS2_bf0 = _rec_inputs()

    def _L0_xattn_setup():
        import jax, jax.numpy as jnp
        import numpy as np
        DIM = 128
        H = 16
        HD = DIM // H
        SCALE = HD ** (-0.5)
        LAMBDA_INIT = 0.1
        EPS = 1e-06

        def _split_heads(x, B, N):
            return x.reshape(B, N, H, HD).transpose(0, 2, 1, 3)
        key0 = jax.random.key(seed)
        ks = jax.random.split(key0, 12)
        B, Nq, Nk = (2, 128, 256)
        w = 0.02
        inp = {'query': jax.random.normal(ks[0], (B, Nq, DIM), jnp.float32), 'key': jax.random.normal(ks[1], (B, Nk, DIM), jnp.float32), 'value': jax.random.normal(ks[2], (B, Nk, DIM), jnp.float32), 'qpos': jax.random.randint(ks[3], (B, Nq), 0, Nq, jnp.int32), 'kpos': jax.random.randint(ks[4], (B, Nk), 0, Nk, jnp.int32), 'q1_w': jax.random.normal(ks[5], (DIM, DIM), jnp.float32) * w, 'q2_w': jax.random.normal(ks[6], (DIM, DIM), jnp.float32) * w, 'kv1_w': jax.random.normal(ks[7], (2 * DIM, DIM), jnp.float32) * w, 'kv2_w': jax.random.normal(ks[8], (2 * DIM, DIM), jnp.float32) * w, 'proj_w': jax.random.normal(ks[9], (DIM, DIM), jnp.float32) * w, 'proj_b': jnp.zeros((DIM,), jnp.float32), 'norm_w': jnp.ones((DIM,), jnp.float32), 'lambda_1': jnp.ones((1, H, 1, 1), jnp.float32), 'lambda_2': jnp.full((1, H, 1, 1), 1.0 - LAMBDA_INIT * (1.0 / 12.0), jnp.float32)}
        return inp
    _L0_xattn_all = _L0_xattn_setup()
    _L0_xattn_in = {k: v for k, v in _L0_xattn_all.items() if k in ('q1_w', 'q2_w', 'kv1_w', 'kv2_w', 'proj_w', 'proj_b', 'norm_w', 'lambda_1', 'lambda_2')}
    del _L0_xattn_all

    def _L0_ffn_setup():
        import jax, jax.numpy as jnp
        import numpy as np
        B, S, H = (4, 256, 128)
        F = 512
        E = 8
        JITTER_EPS = 0.01

        def _sparse_mixer_top2(scores, jitter_eps):
            vals, idx = jax.lax.top_k(scores, 2)
            neg_inf = -jnp.inf
            m1 = vals[:, :1]
            factor1 = jnp.maximum(jnp.abs(scores), m1)
            mask1 = (m1 - scores) / factor1 > 2 * jitter_eps
            p1 = jax.nn.softmax(jnp.where(mask1, neg_inf, scores), axis=-1)
            mult1 = jnp.take_along_axis(p1, idx[:, :1], axis=-1)[:, 0]
            m2 = vals[:, 1:2]
            factor2 = jnp.maximum(jnp.abs(scores), m2)
            mask2 = (m2 - scores) / factor2 > 2 * jitter_eps
            top1_onehot = jnp.arange(scores.shape[-1])[None, :] == idx[:, :1]
            s2 = jnp.where(top1_onehot, neg_inf, scores)
            p2 = jax.nn.softmax(jnp.where(mask2, neg_inf, s2), axis=-1)
            mult2 = jnp.take_along_axis(p2, idx[:, 1:2], axis=-1)[:, 0]
            return (mult1, mult2, idx)
        key = jax.random.key(seed)
        k0, k1, k2, k3, k4 = jax.random.split(key, 5)
        hidden_states = jax.random.normal(k0, (B, S, H), dtype=jnp.float32)
        gate_w = jax.random.normal(k1, (E, H), dtype=jnp.float32) * 0.02
        w1 = jax.random.normal(k2, (E, F, H), dtype=jnp.float32) * 0.02
        w2 = jax.random.normal(k3, (E, H, F), dtype=jnp.float32) * 0.02
        w3 = jax.random.normal(k4, (E, F, H), dtype=jnp.float32) * 0.02
        return {'hidden_states': hidden_states, 'gate_w': gate_w, 'w1': w1, 'w2': w2, 'w3': w3}
    _L0_ffn_all = _L0_ffn_setup()
    _L0_ffn_in = {k: v for k, v in _L0_ffn_all.items() if k in ('gate_w', 'w1', 'w2', 'w3')}
    del _L0_ffn_all

    def _L1_xattn_setup():
        import jax, jax.numpy as jnp
        import numpy as np
        D_MODEL = 128
        NUM_HEADS = 16
        D_K = D_MODEL // NUM_HEADS
        key = jax.random.key(seed)
        ks = jax.random.split(key, 12)
        B, L = (2, 256)
        s = 1.0 / np.sqrt(D_MODEL)
        inp = {'q': jax.random.normal(ks[0], (B, L, D_MODEL), jnp.float32), 'k': jax.random.normal(ks[1], (B, L, D_MODEL), jnp.float32), 'v': jax.random.normal(ks[2], (B, L, D_MODEL), jnp.float32), 'mask': jnp.zeros((B, 1, 1, L), dtype=bool), 'W_q': jax.random.normal(ks[3], (D_MODEL, D_MODEL), jnp.float32) * s, 'b_q': jnp.zeros((D_MODEL,), jnp.float32), 'W_k': jax.random.normal(ks[4], (D_MODEL, D_MODEL), jnp.float32) * s, 'b_k': jnp.zeros((D_MODEL,), jnp.float32), 'W_v': jax.random.normal(ks[5], (D_MODEL, D_MODEL), jnp.float32) * s, 'b_v': jnp.zeros((D_MODEL,), jnp.float32), 'W_o': jax.random.normal(ks[6], (D_MODEL, D_MODEL), jnp.float32) * s, 'b_o': jnp.zeros((D_MODEL,), jnp.float32)}
        return inp
    _L1_xattn_all = _L1_xattn_setup()
    _L1_xattn_in = {k: v for k, v in _L1_xattn_all.items() if k in ('W_q', 'b_q', 'W_k', 'b_k', 'W_v', 'b_v', 'W_o', 'b_o')}
    del _L1_xattn_all

    def _L1_ffn_setup():
        import jax, jax.numpy as jnp
        import numpy as np
        E = 8
        TOPK = 2
        D = 128
        F = 512
        B, S = (2, 64)

        def _gmm(x, W, expert_onehot):
            return jnp.einsum('te,td,edf->tf', expert_onehot, x, W)
        key = jax.random.key(seed)
        k1, k2, k3, k4, k5 = jax.random.split(key, 5)
        scale_d = 1.0 / np.sqrt(D)
        scale_f = 1.0 / np.sqrt(F)
        return {'inputs': jax.random.normal(k1, (B, S, D), jnp.float32), 'gate_kernel': jax.random.normal(k2, (D, E), jnp.float32) * scale_d, 'w0': jax.random.normal(k3, (E, D, F), jnp.float32) * scale_d, 'w1': jax.random.normal(k4, (E, D, F), jnp.float32) * scale_d, 'wo': jax.random.normal(k5, (E, F, D), jnp.float32) * scale_f}
    _L1_ffn_all = _L1_ffn_setup()
    _L1_ffn_in = {k: v for k, v in _L1_ffn_all.items() if k in ('gate_kernel', 'w0', 'w1', 'wo')}
    del _L1_ffn_all
    return {'x': x, 'ctx_1024': ctx_1024, 'itok_BxS_0_1023': itok_BxS_0_1023, 'itok_BxS2_0_2047': itok_BxS2_0_2047, 'mask_Bx1x1xS2_bf0': mask_Bx1x1xS2_bf0, 'L0_xattn_q1_w': _L0_xattn_in['q1_w'], 'L0_xattn_q2_w': _L0_xattn_in['q2_w'], 'L0_xattn_kv1_w': _L0_xattn_in['kv1_w'], 'L0_xattn_kv2_w': _L0_xattn_in['kv2_w'], 'L0_xattn_proj_w': _L0_xattn_in['proj_w'], 'L0_xattn_proj_b': _L0_xattn_in['proj_b'], 'L0_xattn_norm_w': _L0_xattn_in['norm_w'], 'L0_xattn_lambda_1': _L0_xattn_in['lambda_1'], 'L0_xattn_lambda_2': _L0_xattn_in['lambda_2'], 'L0_ffn_gate_w': _L0_ffn_in['gate_w'], 'L0_ffn_w1': _L0_ffn_in['w1'], 'L0_ffn_w2': _L0_ffn_in['w2'], 'L0_ffn_w3': _L0_ffn_in['w3'], 'L1_xattn_W_q': _L1_xattn_in['W_q'], 'L1_xattn_b_q': _L1_xattn_in['b_q'], 'L1_xattn_W_k': _L1_xattn_in['W_k'], 'L1_xattn_b_k': _L1_xattn_in['b_k'], 'L1_xattn_W_v': _L1_xattn_in['W_v'], 'L1_xattn_b_v': _L1_xattn_in['b_v'], 'L1_xattn_W_o': _L1_xattn_in['W_o'], 'L1_xattn_b_o': _L1_xattn_in['b_o'], 'L1_ffn_gate_kernel': _L1_ffn_in['gate_kernel'], 'L1_ffn_w0': _L1_ffn_in['w0'], 'L1_ffn_w1': _L1_ffn_in['w1'], 'L1_ffn_wo': _L1_ffn_in['wo']}

def reference(x, ctx_1024, itok_BxS_0_1023, itok_BxS2_0_2047, mask_Bx1x1xS2_bf0, L0_xattn_q1_w, L0_xattn_q2_w, L0_xattn_kv1_w, L0_xattn_kv2_w, L0_xattn_proj_w, L0_xattn_proj_b, L0_xattn_norm_w, L0_xattn_lambda_1, L0_xattn_lambda_2, L0_ffn_gate_w, L0_ffn_w1, L0_ffn_w2, L0_ffn_w3, L1_xattn_W_q, L1_xattn_b_q, L1_xattn_W_k, L1_xattn_b_k, L1_xattn_W_v, L1_xattn_b_v, L1_xattn_W_o, L1_xattn_b_o, L1_ffn_gate_kernel, L1_ffn_w0, L1_ffn_w1, L1_ffn_wo):
    import jax
    import jax.numpy as jnp

    def _L0_xattn_ref(query, key, value, qpos, kpos, q1_w, q2_w, kv1_w, kv2_w, proj_w, proj_b, norm_w, lambda_1, lambda_2):
        import jax, jax.numpy as jnp
        import numpy as np
        DIM = 128
        H = 16
        HD = DIM // H
        SCALE = HD ** (-0.5)
        LAMBDA_INIT = 0.1
        EPS = 1e-06

        def _split_heads(x, B, N):
            return x.reshape(B, N, H, HD).transpose(0, 2, 1, 3)
        B, Nq, C = query.shape
        Nk = key.shape[1]
        q1 = _split_heads(query @ q1_w.T, B, Nq)
        q2 = _split_heads(query @ q2_w.T, B, Nq)
        kv1 = (key @ kv1_w.T).reshape(B, Nk, 2, H, HD).transpose(2, 0, 3, 1, 4)
        k1, v1 = (kv1[0], kv1[1])
        kv2 = (key @ kv2_w.T).reshape(B, Nk, 2, H, HD).transpose(2, 0, 3, 1, 4)
        k2 = kv2[0]
        attn1 = jax.nn.softmax(jnp.einsum('bhqd,bhkd->bhqk', q1, k1) * SCALE, axis=-1)
        attn2 = jax.nn.softmax(jnp.einsum('bhqd,bhkd->bhqk', q2, k2) * SCALE, axis=-1)
        lambda_full = lambda_1 - lambda_2 + LAMBDA_INIT
        diff_attn = attn1 - lambda_full * attn2
        x = jnp.einsum('bhqk,bhkd->bhqd', diff_attn, v1)
        x = x.transpose(0, 2, 1, 3).reshape(B, Nq, C)
        xf = x.astype(jnp.float32)
        xf = xf * jax.lax.rsqrt(jnp.mean(xf * xf, axis=-1, keepdims=True) + EPS) * norm_w
        x = xf.astype(x.dtype)
        return x @ proj_w.T + proj_b

    def _L0_ffn_ref(hidden_states, gate_w, w1, w2, w3):
        import jax, jax.numpy as jnp
        import numpy as np
        B, S, H = (4, 256, 128)
        F = 512
        E = 8
        JITTER_EPS = 0.01

        def _sparse_mixer_top2(scores, jitter_eps):
            vals, idx = jax.lax.top_k(scores, 2)
            neg_inf = -jnp.inf
            m1 = vals[:, :1]
            factor1 = jnp.maximum(jnp.abs(scores), m1)
            mask1 = (m1 - scores) / factor1 > 2 * jitter_eps
            p1 = jax.nn.softmax(jnp.where(mask1, neg_inf, scores), axis=-1)
            mult1 = jnp.take_along_axis(p1, idx[:, :1], axis=-1)[:, 0]
            m2 = vals[:, 1:2]
            factor2 = jnp.maximum(jnp.abs(scores), m2)
            mask2 = (m2 - scores) / factor2 > 2 * jitter_eps
            top1_onehot = jnp.arange(scores.shape[-1])[None, :] == idx[:, :1]
            s2 = jnp.where(top1_onehot, neg_inf, scores)
            p2 = jax.nn.softmax(jnp.where(mask2, neg_inf, s2), axis=-1)
            mult2 = jnp.take_along_axis(p2, idx[:, 1:2], axis=-1)[:, 0]
            return (mult1, mult2, idx)
        Bv, Sv, Hv = hidden_states.shape
        x = hidden_states.reshape(-1, Hv)
        scores = x @ gate_w.T
        mult1, mult2, idx = _sparse_mixer_top2(scores, JITTER_EPS)
        out = jnp.zeros_like(x)
        for e in range(E):
            w_tok = mult1 * (idx[:, 0] == e) + mult2 * (idx[:, 1] == e)
            h = jax.nn.silu(x @ w1[e].T) * (x @ w3[e].T)
            out = out + w_tok[:, None] * (h @ w2[e].T)
        return out.reshape(Bv, Sv, Hv)

    def _L1_xattn_ref(q, k, v, mask, W_q, b_q, W_k, b_k, W_v, b_v, W_o, b_o):
        import jax, jax.numpy as jnp
        import numpy as np
        D_MODEL = 128
        NUM_HEADS = 16
        D_K = D_MODEL // NUM_HEADS
        B, Lq, _ = q.shape
        Lk = k.shape[1]
        scale = jnp.sqrt(jnp.asarray(D_K, q.dtype))
        Q = (q @ W_q.T + b_q).reshape(B, Lq, NUM_HEADS, D_K).transpose(0, 2, 1, 3)
        K = (k @ W_k.T + b_k).reshape(B, Lk, NUM_HEADS, D_K).transpose(0, 2, 1, 3)
        V = (v @ W_v.T + b_v).reshape(B, Lk, NUM_HEADS, D_K).transpose(0, 2, 1, 3)
        scores = jnp.einsum('bhqd,bhkd->bhqk', Q, K) / scale
        scores = jnp.where(mask, -jnp.inf, scores)
        attn = jax.nn.softmax(scores, axis=-1)
        out = jnp.einsum('bhqk,bhkd->bhqd', attn, V)
        out = out.transpose(0, 2, 1, 3).reshape(B, Lq, D_MODEL)
        return out @ W_o.T + b_o

    def _L1_ffn_ref(inputs, gate_kernel, w0, w1, wo):
        import jax, jax.numpy as jnp
        import numpy as np
        E = 8
        TOPK = 2
        D = 128
        F = 512
        B, S = (2, 64)

        def _gmm(x, W, expert_onehot):
            return jnp.einsum('te,td,edf->tf', expert_onehot, x, W)
        dtype = inputs.dtype
        gate_logits = jnp.einsum('bsd,de->bse', inputs, gate_kernel)
        weights, selected_experts = jax.lax.top_k(gate_logits, TOPK)
        weights = jax.nn.softmax(weights.astype(jnp.float32), axis=-1).astype(dtype)
        inputs_2d = jnp.reshape(inputs, (-1, D))
        flat_sel = jnp.ravel(selected_experts)
        sort_idx = jnp.argsort(flat_sel)
        rep = jnp.repeat(inputs_2d, TOPK, axis=0)
        sorted_hidden = jnp.take(rep, sort_idx, axis=0)
        T = flat_sel.shape[0]
        group_sizes = jnp.zeros((E,), jnp.int32).at[flat_sel].add(1)
        expert_ids = jnp.repeat(jnp.arange(E), group_sizes, total_repeat_length=T)
        onehot = jax.nn.one_hot(expert_ids, E, dtype=dtype)
        layer_1 = _gmm(sorted_hidden, w0, onehot)
        layer_2 = _gmm(sorted_hidden, w1, onehot)
        intermediate = jax.nn.silu(layer_1) * layer_2
        layer_3 = _gmm(intermediate, wo, onehot)
        unsort = jnp.take(layer_3, jnp.argsort(sort_idx), axis=0)
        combined = unsort * jnp.ravel(weights)[:, None]
        out = jnp.sum(combined.reshape(-1, TOPK, D), axis=1)
        return out.reshape(inputs.shape).astype(dtype)
    x = x + _L0_xattn_ref(_layernorm(x, axis=-1), ctx_1024, ctx_1024, itok_BxS_0_1023, itok_BxS2_0_2047, L0_xattn_q1_w, L0_xattn_q2_w, L0_xattn_kv1_w, L0_xattn_kv2_w, L0_xattn_proj_w, L0_xattn_proj_b, L0_xattn_norm_w, L0_xattn_lambda_1, L0_xattn_lambda_2)
    x = x + _L0_ffn_ref(_layernorm(x, axis=-1), L0_ffn_gate_w, L0_ffn_w1, L0_ffn_w2, L0_ffn_w3)
    x = x + _L1_xattn_ref(_layernorm(x, axis=-1), ctx_1024, ctx_1024, mask_Bx1x1xS2_bf0, L1_xattn_W_q, L1_xattn_b_q, L1_xattn_W_k, L1_xattn_b_k, L1_xattn_W_v, L1_xattn_b_v, L1_xattn_W_o, L1_xattn_b_o)
    x = x + _L1_ffn_ref(_layernorm(x, axis=-1), L1_ffn_gate_kernel, L1_ffn_w0, L1_ffn_w1, L1_ffn_wo)
    return x

_drawn_inputs = setup_inputs


def setup_inputs(seed=0):
    import zlib

    import numpy as np

    out = dict(_drawn_inputs(seed))
    spreads = {'L0_xattn_proj_b': (0.0, 0.1),
     'L0_xattn_norm_w': (1.0, 0.2),
     'L0_xattn_lambda_1': (1.0, 0.2),
     'L0_xattn_lambda_2': (0.9916666746139526, 0.2),
     'L1_xattn_b_q': (0.0, 0.1),
     'L1_xattn_b_k': (0.0, 2.0),
     'L1_xattn_b_v': (0.0, 0.1),
     'L1_xattn_b_o': (0.0, 0.1)}
    factors = {'L0_xattn_q2_w': 4.781, 'L0_xattn_kv2_w': 8.0, 'L0_xattn_q1_w': 3.501}
    for name, (base, spread) in spreads.items():
        noise = np.random.default_rng([zlib.crc32(name.encode()), seed]).standard_normal(out[name].shape)
        drawn = base * np.exp(spread * noise) if base else spread * noise
        out[name] = jnp.asarray(drawn.astype(out[name].dtype))
    for name, factor in factors.items():
        out[name] = (out[name] * factor).astype(out[name].dtype)
    return out
```

```python
from contextlib import ExitStack

import concourse.bass as bass
from concourse import mybir

ALU = mybir.AluOpType
ACT = mybir.ActivationFunctionType
AX = mybir.AxisListType
F32 = mybir.dt.float32
BF16 = mybir.dt.bfloat16
I32 = mybir.dt.int32
U32 = mybir.dt.uint32

P = 128
B, NQ, NK, D = 8, 256, 512, 128
H, HD = 16, 8
HH = H // 2
KT, QT = NK // P, NQ // P
SCALE = HD ** -0.5
LN_EPS, RMS_EPS, LAMBDA_INIT = 1e-5, 1e-6, 0.1
E, F = 8, 512
FC = F // P
TOK = B * NQ
TT = TOK // P
SLOTS = TT * 2 + E
BIG = 3.0e38
UNIT = 16
PAIR = 2 * UNIT
KQ = NK + NQ

TERMS = [(0, 0), (1, 1), (0, 1), (1, 0), (0, 2), (2, 0)]
TROWS = len(TERMS) * HD
MROW = 96
STACK_DMAS = 10

W_LOAD, W_CT, W_K, W_XT, W_Q, W_V = 0, 3, 5, 6, 7, 9
P_O, P_OT, P_ON, P_PROJ = 18, 20, 24, 27
M_T = 6


class Layer:

    def __init__(self, n):
        self.n = n
        self.diff = n == 0
        self.units = 2 * B if self.diff else B
        self.pairs = self.units // 2
        self.steps = self.units * UNIT
        self.order = {}
        for g in range(-PAIR, self.steps + PAIR):
            for job in self.jobs(g):
                if 0 <= job[1] < (2 * self.units if job[0] == "mt" else self.units):
                    self.order[job] = len(self.order)

    def leads(self, u):
        return not self.diff or u % 2 == 0

    def ends(self, u):
        return not self.diff or u % 2 == 1

    def jobs(self, g):
        w = g % UNIT
        v = (g - w) // UNIT + 2
        out = []
        if w == W_CT and self.leads(v):
            out.append(("ct", v))
        if w == W_K:
            out.append(("k", v))
        if w == W_XT and self.leads(v):
            out.append(("xt", v))
        if w == W_Q:
            out.append(("q", v))
        if w == W_V and self.leads(v):
            out.append(("v", v))
        if (g + M_T) % 8 == 0:
            out.append(("mt", (g + M_T) // 8))
        for name, p in (("ot", P_OT), ("on", P_ON), ("proj", P_PROJ)):
            if (g - p) % UNIT == 0 and (name == "ot" or self.ends((g - p) // UNIT)):
                out.append((name, (g - p) // UNIT))
        return out

    def lead_no(self, v):
        return v // 2 if self.diff else v


class Block:

    def __init__(self, layer, j=None, it=None):
        self.layer, self.j, self.it = layer, j, it

    def at(self, f):
        if self.it is None:
            return f(self.j)
        return f(1) + (f(2) - f(1)) * self.it

    def live(self, f, n):
        return self.it is not None or 0 <= f(self.j) < n

    def some(self, f, least):
        return (f(1) if self.it is not None else f(self.j)) >= least

    def jobs(self, s):
        j0 = 1 if self.it is not None else self.j
        out = []
        for name, v in self.layer.jobs(PAIR * j0 + s):
            per = 4 if name == "mt" else 2
            if (name, v) in self.layer.order:
                unit = lambda j, v=v, per=per: v + per * (j - j0)
                out.append((name, unit, lambda j, name=name, unit=unit: self.layer.order[(name, unit(j))]))
        return out


def run_blocks(eng, layer, emit):
    emit(Block(layer, j=-1))
    emit(Block(layer, j=0))
    with eng.Fori(0, layer.pairs - 2) as it:
        emit(Block(layer, it=it))
    emit(Block(layer, j=layer.pairs - 1))
    emit(Block(layer, j=layer.pairs))


def build(nc, a, out):
    L = [Layer(0), Layer(1)]
    with ExitStack() as ctx:
        def sb(name, shape, dt=F32):
            return ctx.enter_context(nc.sbuf_tensor(name, shape, dt))

        def sem(name):
            return ctx.enter_context(nc.semaphore(name))

        def dram(name, shape, dt=F32):
            return nc.dram_tensor(name, shape, dt).ap()

        x_att = [dram("x_att0", (B, NQ, D)), dram("x_att1", (B, NQ, D))]
        x_ffn = [dram("x_ffn0", (B, NQ, D)), out]
        rows_in = dram("rows_in", (SLOTS * P, D))
        rows_out = dram("rows_out", (SLOTS * P, D))
        x_src = [a["x"], x_ffn[0]]

        ident = sb("ident", [P, P])
        identb = sb("identb", [P, P], BF16)
        stack = sb("stack", [P, 4, HH, KQ], BF16)
        parts = sb("parts", [P, 2, 3, KQ], BF16)
        rest_k = sb("rest_k", [P, NK])
        rest_q = sb("rest_q", [P, NQ])
        probs = sb("probs", [P, 4, 4, NQ])
        vpad = sb("vpad", [P, 2, 2, KT, 4, 32])
        vals = sb("vals", [P, 2, KT, D])
        ctx_sb = sb("ctx_sb", [P, KT, D])
        ctxT = sb("ctxT", [P, NK])
        x_in = sb("x_in", [P, QT, D])
        x_stat = sb("x_stat", [P, QT, 6])
        x_mv = sb("x_mv", [P, QT, 2])
        x_rstd = sb("x_rstd", [P, QT])
        xn = sb("xn", [P, QT, D])
        xnT = sb("xnT", [P, NQ])
        row_max = sb("row_max", [P, 2, QT, HH])
        max_rest = sb("max_rest", [P, QT, HH])
        max_parts = sb("max_parts", [P, 2, QT, 3, HH], BF16)
        max_rows = sb("max_rows", [3 * HH, 2, NQ], BF16)
        outT = sb("outT", [P, 2, NQ])
        r_den = sb("r_den", [P, QT, H])
        o_first = sb("o_first", [P, QT * H, HD])
        o_second = sb("o_second", [P, QT * H, HD])
        o_diff = sb("o_diff", [P, QT, D])
        o_sq = sb("o_sq", [P, D])
        o_ss = sb("o_ss", [P, QT])
        o_rr = sb("o_rr", [P, QT])
        o_norm = sb("o_norm", [P, QT, D])
        onT = sb("onT", [P, NQ])
        x_res = sb("x_res", [P, QT, D])
        x_new = sb("x_new", [P, QT, D])
        half_neg = sb("half_neg", [P, TT])
        raw = sb("raw", [P, 10, D])
        raw_perm = sb("raw_perm", [P, 2, D])
        w_all = sb("w_all", [P, 10, D])
        bias_k = sb("bias_k", [P, 2])
        bias_q = sb("bias_q", [P, 2])
        bias_v = sb("bias_v", [P, 2, D])
        bias_o = sb("bias_o", [P, 2, D])
        norm_col = sb("norm_col", [P, 1])
        lam_in = sb("lam_in", [P, 2, H])
        lam_d = sb("lam_d", [P, H])
        lam = sb("lam", [P, H])

        zero_row = sb("zero_row", [P, D])
        place_f = sb("place_f", [P, 2, TT])
        w_exp = sb("w_exp", [P, 3, E, F])
        gate_raw = sb("gate_raw", [E, D])
        w_gate = sb("w_gate", [P, 2, E])
        x_all = sb("x_all", [P, TT, D])
        xT_all = probs[:].rearrange("p a i n -> p (a i n)")[:, 0:TOK]
        y_all = probs[:].rearrange("p a i (n c) -> p (a i n) c", c=D)
        t_stat = sb("t_stat", [P, TT, 6])
        t_mv = sb("t_mv", [P, TT, 2])
        t_rstd = sb("t_rstd", [P, TT])
        tri = sb("tri", [P, P], BF16)
        ones = sb("ones", [P, P], BF16)
        i_rev = sb("i_rev", [P, E], I32)
        rev = sb("rev", [P, E])
        i_slot = sb("i_slot", [P, SLOTS], I32)
        slot_no = sb("slot_no", [P, SLOTS])
        i_full = sb("i_full", [P, TT], I32)
        full_rows = sb("full_rows", [P, TT])
        carry = sb("carry", [P, E, TT])
        gate_s = sb("gate_s", [P, TT, E])
        gate_s2 = sb("gate_s2", [P, TT, E])
        gate_abs = sb("gate_abs", [P, TT, E])
        top = sb("top", [P, 2, TT])
        rt_a = sb("rt_a", [P, TT, E])
        rt_b = sb("rt_b", [P, TT, E])
        rt_k = sb("rt_k", [P, TT])
        hot = sb("hot", [P, 2, TT, E])
        picked = sb("picked", [P, TT, E], BF16)
        share = sb("share", [P, 2, TT])
        share_d = sb("share_d", [P, TT])
        total = sb("total", [P, E, TT])
        upto = sb("upto", [P, E, TT])
        more = sb("more", [P, E, TT])
        n_tiles = sb("n_tiles", [P, E])
        tile_end = sb("tile_end", [P, E])
        tile_at = sb("tile_at", [P, E])
        place = sb("place", [P, TT, E])
        done_e = sb("done_e", [P, SLOTS, E])
        tile_e = sb("tile_e", [P, SLOTS])
        expert_of = sb("expert_of", [P, SLOTS], I32)
        position = sb("position", [P, 2, TT], U32)
        s_rows = sb("s_rows", [P, 2, D])
        s_rowsT = sb("s_rowsT", [P, 2, P])
        s_act = sb("s_act", [P, 2, F])
        s_hid = sb("s_hid", [P, 2, F])
        s_hidT = sb("s_hidT", [P, 2, F])
        s_out = sb("s_out", [P, 2, D])

        ps = ctx.enter_context(nc.psum_tensor("ps", [P, 8, 512], F32))
        score = [ps[:, 0:2, :].rearrange("p b (i n) -> p (b i) n", i=2),
                 ps[:, 2:4, :].rearrange("p b (i n) -> p (b i) n", i=2)]
        maxs = [ps[:, 4, :], ps[:, 5, :]]
        oacc = ps[:, 6, :].rearrange("p (f n) -> p f n", f=2)
        misc = ps[:, 7, :]
        misc_bf = misc.bitcast(BF16)

        w_in = sem("w_in")
        gp_init = sem("gp_init")
        raw_perm_ready = sem("raw_perm_ready")
        wt_ready = sem("wt_ready")
        wt_taken = sem("wt_taken")
        zero_done = sem("zero_done")
        const_step = sem("const_step")
        rows_zero = sem("rows_zero")
        w_exp_in = sem("w_exp_in")
        lam_step = sem("lam_step")
        gate_ready = sem("gate_ready")
        carrier = sem("carrier")

        WQ = [[0, 1], [6, 6]]
        WK = [[2, 3], [7, 7]]
        WV = [4, 8]
        WO = [5, 9]

        def heads_last(ap):
            return ap.rearrange("p (f h d) -> p f d h", f=2, h=HH)

        block = ctx.enter_context(nc.Block())

        def att_sems(n):
            names = ("ctx_in x_in qk_done exp_done pv_done mx_ready mx_taken job_ready job_taken a1_done "
                     "split_step vpad_ready ln_step rstd_step xn_ready mp_step o_taken den_step on_ready "
                     "rr_step res_in res_ready x_out").split()
            d = {k: sem(f"{k}{n}") for k in names}
            d["stack_in"] = [sem(f"stack_in{n}_{i}") for i in range(4)]
            d["mrow_in"] = [sem(f"mrow_in{n}_{i}") for i in range(2)]
            return d

        S = [att_sems(0), att_sems(1)]
        phase = [sem(f"phase{i}") for i in range(3)]

        def start_sync(sp):
            q = [(0, a["L0_xattn_q1_w"]), (1, a["L0_xattn_q2_w"]), (2, a["L0_xattn_kv1_w"][0:D, :]),
                 (3, a["L0_xattn_kv2_w"][0:D, :]), (4, a["L0_xattn_kv1_w"][D:2 * D, :]), (5, a["L0_xattn_proj_w"]),
                 (6, a["L1_xattn_W_q"]), (7, a["L1_xattn_W_k"]), (8, a["L1_xattn_W_v"]), (9, a["L1_xattn_W_o"])]
            for i, src in q:
                sp.dma_start(raw[:, i, :], src).then_inc(w_in, 16)
            for f in range(2):
                r = slice(f * 64, f * 64 + 64)
                for col, src in ((bias_q, a["L1_xattn_b_q"]), (bias_k, a["L1_xattn_b_k"])):
                    sp.dma_start(col[r, 1:2], src[r].rearrange("(h d o) -> d h o", h=HH, o=1),
                                 allow_slow_non_contiguous=True).then_inc(w_in, 16)
                for i in range(4):
                    sp.dma_start(norm_col[64 * f + 16 * i:64 * f + 16 * i + 16, :],
                                 a["L0_xattn_norm_w"][r].rearrange("(q i d o) -> i q d o", q=2, i=4, o=1)[i],
                                 allow_slow_non_contiguous=True).then_inc(w_in, 16)
            for tile, src in ((bias_o[:, 0, :], a["L0_xattn_proj_b"]), (bias_o[:, 1, :], a["L1_xattn_b_o"]),
                              (bias_v[:, 1, :], a["L1_xattn_b_v"])):
                sp.dma_start(tile, src.partition_broadcast(P)).then_inc(w_in, 16)
            for i, name in enumerate(("L0_xattn_lambda_1", "L0_xattn_lambda_2")):
                sp.dma_start(lam_in[:, i, :], a[name].rearrange("a h b c -> (a h b c)").partition_broadcast(P)
                             ).then_inc(w_in, 16)

        def load_experts(sp, n):
            up = w_exp[:, 0].rearrange("p e (c h) -> p e c h", c=FC)
            gate = w_exp[:, 1].rearrange("p e (c h) -> p e c h", c=FC)
            down = w_exp[:, 2].rearrange("p e (c h) -> p e c h", c=FC)
            if n == 0:
                sp.dma_start(gate_raw[:], a["L0_ffn_gate_w"]).then_inc(w_exp_in, 16)
                for e in range(E):
                    sp.dma_start(up[:, e], a["L0_ffn_w1"][e].rearrange("(c p) h -> p c h", p=P)).then_inc(w_exp_in, 16)
                    sp.dma_start(gate[:, e], a["L0_ffn_w3"][e].rearrange("(c p) h -> p c h", p=P)
                                 ).then_inc(w_exp_in, 16)
                sp.dma_start(w_exp[:, 2], a["L0_ffn_w2"].rearrange("e h f -> h e f")).then_inc(w_exp_in, 16)
            else:
                sp.dma_start(w_gate[:, 1, :], a["L1_ffn_gate_kernel"]).then_inc(w_exp_in, 16)
                sp.dma_start(w_exp[:, 0], a["L1_ffn_w0"].rearrange("e d f -> d e f")).then_inc(w_exp_in, 16)
                sp.dma_start(w_exp[:, 1], a["L1_ffn_w1"].rearrange("e d f -> d e f")).then_inc(w_exp_in, 16)
                for e in range(E):
                    sp.dma_start(down[:, e], a["L1_ffn_wo"][e].rearrange("(c p) d -> p c d", p=P)
                                 ).then_inc(w_exp_in, 16)

        W_EXP_DMAS = [2 + 2 * E, 2 + 2 * E + 3 + E]

        W_DMAS = 10 + 2 * (2 + 4) + 3 + 2

        def zero_view(c):
            return stack[:, c, :, :].bitcast(F32)

        def start_gpsimd(pool):
            for c in range(2, 4):
                nc.gpsimd.memset(zero_view(c), 0.0).then_inc(zero_done, 1)
            nc.gpsimd.memset(ident[:], 1.0).then_inc(gp_init, 1)
            pool.wait_ge(gp_init, 1)
            nc.gpsimd.affine_select(out=ident[:], in_=ident[:], compare_op=ALU.is_equal, fill=0.0, base=0,
                                    pattern=[[-1, P]], channel_multiplier=1).then_inc(gp_init, 1)
            pool.wait_ge(gp_init, 2)
            nc.gpsimd.tensor_copy(identb[:], ident[:]).then_inc(gp_init, 1)
            nc.gpsimd.memset(half_neg[:], -0.5).then_inc(gp_init, 1)
            nc.gpsimd.memset(vpad[:], 0.0).then_inc(gp_init, 1)
            pool.wait_ge(gp_init, 5)
            for pp in range(2):
                nc.gpsimd.memset(vpad[:, :, pp, :, :, 16 * pp + HD:16 * pp + HD + 1], 1.0).then_inc(gp_init, 1)
            nc.gpsimd.memset(bias_k[:, 0:1], 0.0).then_inc(gp_init, 1)
            nc.gpsimd.memset(bias_q[:, 0:1], 0.0).then_inc(gp_init, 1)
            nc.gpsimd.memset(bias_v[:, 0, :], 0.0).then_inc(gp_init, 1)
            nc.gpsimd.memset(ones[:], 1.0).then_inc(gp_init, 1)
            nc.gpsimd.iota(i_rev[:], pattern=[[-1, E]], base=E, channel_multiplier=0).then_inc(gp_init, 1)
            nc.gpsimd.iota(i_slot[:], pattern=[[1, SLOTS]], base=0, channel_multiplier=0).then_inc(gp_init, 1)
            nc.gpsimd.iota(i_full[:], pattern=[[P, TT]], base=0, channel_multiplier=0).then_inc(gp_init, 1)
            nc.gpsimd.memset(carry[:], 1.0).then_inc(const_step, 1)
            pool.wait_ge(gp_init, 14)
            nc.gpsimd.tensor_copy(rev[:], i_rev[:]).then_inc(gp_init, 1)
            nc.gpsimd.tensor_copy(slot_no[:], i_slot[:]).then_inc(gp_init, 1)
            nc.gpsimd.tensor_copy(full_rows[:], i_full[:]).then_inc(gp_init, 1)
            pool.wait_ge(const_step, 1)
            for e in range(E):
                nc.gpsimd.memset(carry[:, e, 0:1], 0.0).then_inc(gp_init, 1)
            nc.gpsimd.affine_select(out=tri[:], in_=ones[:], compare_op=ALU.is_gt, fill=0.0, base=0,
                                    pattern=[[1, P]], channel_multiplier=-1).then_inc(const_step, 1)
            nc.gpsimd.memset(zero_row[:], 0.0).then_inc(const_step, 1)

        GP_INIT = 10 + 4 + 3 + E

        def start_vector(dve):
            for c in range(2):
                nc.vector.memset(zero_view(c), 0.0).then_inc(zero_done, 1)
            dve.wait_ge(zero_done, 4)
            nc.vector.memset(stack[MROW:P, :, :, 0:NK], 1.0).then_inc(zero_done, 1)
            dve.wait_ge(w_in, 16 * W_DMAS)
            for n in range(2):
                for f in range(2):
                    r = slice(f * 64, f * 64 + 64)
                    nc.vector.tensor_copy(raw_perm[:, n, r].rearrange("p (i q d) -> p q i d", i=4, q=2),
                                          raw[:, WO[n], r].rearrange("p (q i d) -> p q i d", q=2, i=4)
                                          ).then_inc(raw_perm_ready, 1)
            nc.vector.tensor_tensor(lam_d[:], lam_in[:, 0, :], lam_in[:, 1, :], ALU.subtract).then_inc(lam_step, 1)
            dve.wait_ge(lam_step, 1)
            for f in range(2):
                nc.vector.tensor_scalar(lam[:, f * 8:f * 8 + 8].rearrange("p (i q) -> p q i", i=4),
                                        lam_d[:, f * 8:f * 8 + 8].rearrange("p (q i) -> p q i", q=2),
                                        LAMBDA_INIT, None, ALU.add).then_inc(lam_step, 1)
            for i in range(10):
                dve.wait_ge(wt_ready, i // 2 + 1)
                src = ps[:, i // 2 % 4, (i % 2) * D:(i % 2) * D + D]
                if i in WQ[0] + WK[0] + WQ[1][:1] + WK[1][:1]:
                    ins = nc.vector.tensor_copy(w_all[:, i, :].rearrange("p (f d h) -> p f d h", f=2, d=HD),
                                                heads_last(src))
                elif i == WO[0]:
                    ins = nc.vector.tensor_scalar(w_all[:, i, :], src, norm_col[:, 0:1], None, ALU.mult)
                else:
                    ins = nc.vector.tensor_copy(w_all[:, i, :], src)
                ins.then_inc(wt_taken, 1)

        def start_tensor(pe):
            pe.wait_ge(gp_init, GP_INIT)
            pe.wait_ge(w_in, 16 * W_DMAS)
            pe.wait_ge(raw_perm_ready, 4)
            for i in range(10):
                src = raw_perm[:, WO.index(i), :] if i in WO else raw[:, i, :]
                if i == 8:
                    pe.wait_ge(wt_taken, 2)
                ins = nc.tensor.transpose(ps[:, i // 2 % 4, (i % 2) * D:(i % 2) * D + D], src, ident[:])
                if i % 2:
                    ins.then_inc(wt_ready, 1)
            pe.wait_ge(wt_taken, 10)
            pe.wait_ge(zero_done, 5)

        def apart(eng):
            eng.sem_inc(carrier, 1)

        def att_sync(sp, layer):
            n, z = layer.n, S[layer.n]
            xs = x_src[n].rearrange("b (t p) c -> p b t c", p=P)
            xo = x_att[n].rearrange("b (t p) c -> p b t c", p=P)
            cs = a["ctx_1024"].rearrange("b (t p) c -> p b t c", p=P)

            def emit(blk):
                at, live, some = blk.at, blk.live, blk.some
                for s in range(PAIR):
                    w = s % UNIT
                    v = lambda j: 2 * j + s // UNIT + 2
                    lead = layer.leads(s // UNIT)
                    if w == W_LOAD and lead and live(v, layer.units):
                        b = lambda j: layer.lead_no(v(j))
                        if some(b, 1):
                            prev = lambda j: v(j) - (2 if layer.diff else 1)
                            sp.wait_ge(z["job_ready"], at(lambda j: layer.order[("ct", prev(j))] + 1))
                            apart(sp)
                            sp.wait_ge(z["xn_ready"], at(lambda j: 2 * b(j)))
                        sp.dma_start(ctx_sb[:], cs[:, bass.ds(at(b), 1), :, :].rearrange("p b t c -> p (b t) c")
                                     ).then_inc(z["ctx_in"], 16)
                        sp.dma_start(x_in[:], xs[:, bass.ds(at(b), 1), :, :].rearrange("p b t c -> p (b t) c")
                                     ).then_inc(z["x_in"], 16)
                    for c_half, w_key, w_query in ((0, 8, 9), (1, 0, 0)):
                        for group, w_g in (("key", w_key), ("query", w_query)):
                            if w != w_g:
                                continue
                            u = v if c_half == 0 else (lambda j: 2 * j + s // UNIT + 1)
                            if not live(u, layer.units):
                                continue
                            c = lambda j: 2 * u(j) + c_half
                            par = (s // UNIT + (0 if c_half == 0 else 1)) % 2
                            slot = 2 * par + c_half
                            sp.wait_ge(z["split_step"], at(lambda j: 4 * u(j) + (2 if group == "key" else 4)))
                            apart(sp)
                            if group == "key" and some(c, 4):
                                sp.wait_ge(z["qk_done"], at(lambda j: 8 * (c(j) - 3)))
                            for t, (qp, kp) in enumerate(TERMS):
                                src = parts[64 * c_half:64 * c_half + 64, par]
                                dst = stack[8 * t:8 * t + 8, slot]
                                if group == "key" and qp != kp:
                                    sp.dma_start(dst[:, :, 0:NK], src[:, kp, 0:NK]).then_inc(z["stack_in"][slot], 16)
                                if group == "query" and qp == kp:
                                    sp.dma_start(dst[:, :, :], src[:, kp, :]).then_inc(z["stack_in"][slot], 16)
                                if group == "query" and qp != kp:
                                    sp.dma_start(dst[:, :, NK:KQ], src[:, qp, NK:KQ]).then_inc(z["stack_in"][slot], 16)
                    for name, u, no in blk.jobs(s):
                        if name == "mt":
                            slot = (s + M_T) // 8 % 4
                            sp.wait_ge(z["job_taken"], at(lambda j: no(j) + 1))
                            sp.dma_start(stack[MROW:MROW + 3, slot, :, NK:KQ], max_rows[:, slot % 2, :]
                                         ).then_inc(z["mrow_in"][slot % 2], 16)
                        if name == "ot" and layer.ends(s // UNIT + 1):
                            b = lambda j: u(j) // 2 if layer.diff else u(j)
                            if some(b, 1):
                                prev = lambda j: u(j) - (2 if layer.diff else 1)
                                sp.wait_ge(z["job_taken"], at(lambda j: layer.order[("proj", prev(j))] + 1))
                            sp.dma_start(x_res[:], xs[:, bass.ds(at(b), 1), :, :].rearrange("p b t c -> p (b t) c")
                                         ).then_inc(z["res_in"], 16)
                        if name == "proj":
                            b = lambda j: u(j) // 2 if layer.diff else u(j)
                            sp.wait_ge(z["job_taken"], at(lambda j: no(j) + 1))
                            sp.dma_start(xo[:, bass.ds(at(b), 1), :, :].rearrange("p b t c -> p (b t) c"), x_new[:]
                                         ).then_inc(z["x_out"], 16)
            run_blocks(sp, layer, emit)
            sp.wait_ge(z["x_out"], 16 * B)

        def att_tensor(pe, layer):
            n, z = layer.n, S[layer.n]

            def job(blk, s, name, u, no):
                at = blk.at
                if name != "first":
                    if blk.some(no, 1):
                        pe.wait_ge(z["job_taken"], at(no))
                if name == "ct":
                    pe.wait_ge(z["ctx_in"], at(lambda j: 16 * (layer.lead_no(u(j)) + 1)))
                    for t in range(KT):
                        ins = nc.tensor.transpose(misc[:, t * P:(t + 1) * P], ctx_sb[:, t, :], ident[:])
                elif name == "k":
                    ins = nc.tensor.matmul(misc, w_all[:, WK[n][s // UNIT], :], ctxT[:], start=True, stop=True)
                elif name == "xt":
                    pe.wait_ge(z["xn_ready"], at(lambda j: 2 * (layer.lead_no(u(j)) + 1)))
                    for t in range(QT):
                        ins = nc.tensor.transpose(misc[:, t * P:(t + 1) * P], xn[:, t, :], ident[:])
                elif name == "q":
                    ins = nc.tensor.matmul(misc[:, 0:NQ], w_all[:, WQ[n][s // UNIT], :], xnT[:], start=True, stop=True)
                elif name == "v":
                    for t in range(KT):
                        ins = nc.tensor.matmul(misc[:, t * P:(t + 1) * P], ctxT[:, t * P:(t + 1) * P],
                                               w_all[:, WV[n], :], start=True, stop=True)
                elif name == "mt":
                    pe.wait_ge(z["mp_step"], at(lambda j: 4 * (u(j) + 1)))
                    for t in range(QT):
                        src = max_parts[:, (s + M_T) // 8 % 2, t].rearrange("p a h -> p (a h)")
                        ins = nc.tensor.transpose(misc_bf[0:3 * HH, t * P:(t + 1) * P], src, identb[:])
                elif name == "ot":
                    pe.wait_ge(z["o_taken"], at(lambda j: u(j) + 1))
                    for t in range(QT):
                        for f in range(2):
                            ins = nc.tensor.transpose(misc[:, (2 * t + f) * P:(2 * t + f + 1) * P],
                                                      outT[:, f, t * P:(t + 1) * P], ident[:])
                elif name == "on":
                    if layer.diff:
                        pe.wait_ge(z["on_ready"], at(lambda j: QT * (layer.lead_no(u(j)) + 1)))
                    for t in range(QT):
                        ins = nc.tensor.transpose(misc[:, t * P:(t + 1) * P], o_norm[:, t, :], ident[:])
                elif name == "proj":
                    for t in range(QT):
                        ins = nc.tensor.matmul(misc[:, t * P:(t + 1) * P], onT[:, t * P:(t + 1) * P],
                                               w_all[:, WO[n], :], start=True, stop=True)
                ins.then_inc(z["job_ready"], 1)

            def emit(blk):
                at, live, some = blk.at, blk.live, blk.some
                for s in range(PAIR):
                    g = lambda j: PAIR * j + s
                    if live(g, layer.steps):
                        slot, pp, kt = s // 8, s // 4 % 2, s % 4
                        if s % 8 == 0:
                            pe.wait_ge(z["mrow_in"][slot % 2], at(lambda j: 16 * (2 * j + slot // 2 + 1)))
                        if some(g, 2):
                            pe.wait_ge(z["exp_done"], at(lambda j: g(j) - 1))
                        for i in range(4):
                            ins = nc.tensor.matmul(score[s % 2][:, i, :],
                                                   stack[:, slot, 4 * pp + i, kt * P:(kt + 1) * P],
                                                   stack[:, slot, 4 * pp + i, NK:KQ], start=True, stop=True)
                        ins.then_inc(z["qk_done"], 1)
                    for name, u, no in blk.jobs(s):
                        job(blk, s, name, u, no)
                    gm = lambda j: PAIR * j + s + UNIT
                    if live(gm, layer.steps):
                        slot = (s + UNIT) // 8 % 4
                        if s % 8 == 0:
                            cyc = lambda j: j + (s + UNIT) // PAIR
                            pe.wait_ge(z["stack_in"][slot], at(lambda j: 16 * STACK_DMAS * (cyc(j) + 1)))
                        for t in range(QT):
                            if some(gm, 1):
                                pe.wait_ge(z["mx_taken"], at(lambda j: 2 * gm(j) + t - 1))
                            nc.tensor.matmul(maxs[t], stack[0:MROW, slot, s % 8, NK + t * P:NK + (t + 1) * P],
                                             stack[0:MROW, slot, s % 8, 0:NK], start=True, stop=True
                                             ).then_inc(z["mx_ready"], 1)
                    gp = lambda j: PAIR * j + s - 2
                    if live(gp, layer.steps):
                        sp_ = (s - 2) % PAIR
                        f, pp, kt = sp_ // 8 % 2, sp_ // 4 % 2, sp_ % 4
                        if sp_ % UNIT == 0 and some(gp, 1):
                            pe.wait_ge(z["o_taken"], at(lambda j: gp(j) // UNIT))
                        if sp_ % 8 == 0 and layer.leads(sp_ // UNIT):
                            pe.wait_ge(z["vpad_ready"], at(lambda j: 4 * layer.lead_no(gp(j) // UNIT) + 2 * f + 2))
                        pe.wait_ge(z["exp_done"], at(lambda j: gp(j) + 1))
                        for i in range(4):
                            ins = nc.tensor.matmul(oacc[32 * i:32 * i + 32, f, :], vpad[:, f, pp, kt, i, :],
                                                   probs[:, sp_ % 4, i, :], start=(sp_ % UNIT == 0),
                                                   stop=(sp_ % 8 == 7), skip_group_check=True)
                        ins.then_inc(z["pv_done"], 1)
            run_blocks(pe, layer, emit)

        def att_scalar(act, layer):
            n, z = layer.n, S[layer.n]

            def emit(blk):
                at, live, some = blk.at, blk.live, blk.some
                for s in range(PAIR):
                    g = lambda j: PAIR * j + s
                    if live(g, layer.steps):
                        act.wait_ge(z["qk_done"], at(lambda j: g(j) + 1))
                        if some(g, 4):
                            act.wait_ge(z["pv_done"], at(lambda j: g(j) - 3))
                        nc.scalar.activation(probs[:, s % 4], score[s % 2], ACT.Exp, scale=SCALE
                                             ).then_inc(z["exp_done"], 1)
                    uo = lambda j: 2 * j + (s - P_O) // UNIT
                    if (s - P_O) % UNIT == 0 and live(uo, layer.units):
                        act.wait_ge(z["pv_done"], at(lambda j: UNIT * (uo(j) + 1)))
                        if some(uo, 1):
                            act.wait_ge(z["job_ready"], at(lambda j: layer.order[("ot", uo(j) - 1)] + 1))
                        nc.scalar.copy(outT[:], oacc).then_inc(z["o_taken"], 1)
                    for name, u, no in blk.jobs(s):
                        if name in ("v", "ot", "proj"):
                            continue
                        act.wait_ge(z["job_ready"], at(lambda j: no(j) + 1))
                        par = s // UNIT
                        if name == "ct":
                            nc.scalar.copy(ctxT[:], misc).then_inc(z["job_taken"], 1)
                        elif name == "xt":
                            nc.scalar.copy(xnT[:], misc[:, 0:NQ]).then_inc(z["job_taken"], 1)
                        elif name == "on":
                            nc.scalar.copy(onT[:], misc[:, 0:NQ]).then_inc(z["job_taken"], 1)
                        elif name == "mt":
                            q = (s + M_T) // 8 % 2
                            if some(u, 2):
                                act.wait_ge(z["mrow_in"][q], at(lambda j: 16 * (u(j) // 2)))
                            nc.scalar.copy(max_rows[:, q, :], misc_bf[0:3 * HH, 0:NQ]).then_inc(z["job_taken"], 1)
                        else:
                            cols, bias = ((slice(0, NK), bias_k) if name == "k" else (slice(NK, KQ), bias_q))
                            if some(u, 2):
                                for slot in (2 * par, 2 * par + 1):
                                    act.wait_ge(z["stack_in"][slot], at(lambda j: 16 * STACK_DMAS * (u(j) // 2)))
                            nc.scalar.activation(parts[:, par, 0, cols], misc[:, 0:cols.stop - cols.start],
                                                 ACT.Identity, bias=bias[:, n:n + 1]).then_inc(z["a1_done"], 1)
            run_blocks(act, layer, emit)

        def att_vector(dve, layer):
            n, z = layer.n, S[layer.n]

            def emit(blk):
                at, live, some = blk.at, blk.live, blk.some
                for s in range(PAIR):
                    w, par = s % UNIT, s // UNIT
                    gm = lambda j: PAIR * j + s + UNIT
                    if live(gm, layer.steps):
                        c2 = s // 8 % 2
                        for t in range(QT):
                            dve.wait_ge(z["mx_ready"], at(lambda j: 2 * gm(j) + t + 1))
                            if s % 8 == 0 and t == 0 and some(lambda j: gm(j) // 8, 2):
                                dve.wait_ge(z["mp_step"], at(lambda j: 4 * (gm(j) // 8 - 1)))
                            nc.vector.tensor_reduce(row_max[:, c2, t, s % 8:s % 8 + 1], maxs[t], axis=AX.X,
                                                    op=ALU.max, negate=True).then_inc(z["mx_taken"], 1)
                    v = lambda j: 2 * j + s // UNIT + 2
                    if w in (2, 4) and layer.leads(par) and live(v, layer.units):
                        b = lambda j: layer.lead_no(v(j))
                        if w == 2:
                            dve.wait_ge(z["x_in"], at(lambda j: 16 * (b(j) + 1)))
                            for t in range(QT):
                                nc.vector.bn_stats(x_stat[:, t, :], x_in[:, t, :]).then_inc(z["ln_step"], 1)
                            dve.wait_ge(z["ln_step"], at(lambda j: 4 * b(j) + 2))
                            if some(b, 1):
                                dve.wait_ge(z["rstd_step"], at(lambda j: 2 * b(j)))
                            for t in range(QT):
                                apart(dve)
                                nc.vector.bn_aggr(x_mv[:, t, :], x_stat[:, t, :]).then_inc(z["ln_step"], 1)
                        else:
                            dve.wait_ge(z["rstd_step"], at(lambda j: 2 * b(j) + 2))
                            if some(b, 1):
                                prev = lambda j: v(j) - (2 if layer.diff else 1)
                                dve.wait_ge(z["job_ready"], at(lambda j: layer.order[("xt", prev(j))] + 1))
                            for t in range(QT):
                                nc.vector.tensor_scalar(xn[:, t, :], x_in[:, t, :], x_mv[:, t, 0:1],
                                                        x_rstd[:, t:t + 1], ALU.subtract, ALU.mult
                                                        ).then_inc(z["xn_ready"], 1)
                    if (s - P_OT - 2) % UNIT == 0 and layer.diff and layer.ends((s - P_OT - 2) // UNIT):
                        uu = lambda j: 2 * j + (s - P_OT - 2) // UNIT
                        if live(uu, layer.units):
                            bb = lambda j: uu(j) // 2
                            dve.wait_ge(z["rr_step"], at(lambda j: 2 * bb(j) + 2))
                            if some(bb, 1):
                                dve.wait_ge(z["job_ready"], at(lambda j: layer.order[("on", uu(j) - 2)] + 1))
                            for t in range(QT):
                                nc.vector.tensor_scalar(o_norm[:, t, :], o_diff[:, t, :], o_rr[:, t:t + 1], None,
                                                        ALU.mult).then_inc(z["on_ready"], 1)
                    for name, u, no in blk.jobs(s):
                        if name in ("k", "q"):
                            cols, bias, rest = ((slice(0, NK), bias_k, rest_k) if name == "k"
                                                else (slice(NK, KQ), bias_q, rest_q))
                            k = 1 if name == "k" else 2
                            dve.wait_ge(z["a1_done"], at(lambda j: 2 * u(j) + k))
                            if some(u, 1):
                                dve.wait_ge(z["split_step"], at(lambda j: 4 * (u(j) - 1) + 2 * k))
                            nc.vector.scalar_tensor_tensor(
                                out=rest[:], in0=misc[:, 0:cols.stop - cols.start], scalar=bias[:, n:n + 1],
                                in1=parts[:, par, 0, cols], op0=ALU.add, op1=ALU.subtract
                            ).then_inc(z["job_taken"], 1)
                        elif name == "v":
                            dve.wait_ge(z["job_ready"], at(lambda j: no(j) + 1))
                            if some(u, 2):
                                dve.wait_ge(z["vpad_ready"], at(lambda j: 4 * (layer.lead_no(u(j) - 2) + 1)))
                            nc.vector.tensor_tensor(vals[:, par], misc.rearrange("p (t c) -> p t c", t=KT),
                                                    bias_v[:, n:n + 1, :].broadcast_to([P, KT, D]), ALU.add
                                                    ).then_inc(z["job_taken"], 1)
                        elif name == "ot":
                            second = layer.diff and layer.ends((s - P_OT) // UNIT)
                            got = misc.rearrange("p (m c) -> p m c", c=16)
                            den = got[:, :, HD:HD + 1].rearrange("p (t m) c -> p t (m c)", t=QT)
                            rd = r_den[:].rearrange("p t m -> p (t m)")
                            dve.wait_ge(z["job_ready"], at(lambda j: no(j) + 1))
                            base = (lambda j: 4 * (u(j) // 2) + (u(j) % 2)) if layer.diff else (lambda j: u(j))
                            nc.vector.reciprocal(r_den[:], den).then_inc(z["den_step"], 1)
                            dve.wait_ge(z["den_step"], at(lambda j: base(j) + 1))
                            if second:
                                nc.vector.tensor_tensor(r_den[:], r_den[:],
                                                        lam[:].rearrange("p (o m) -> p o m", o=1).broadcast_to([P, QT, H]),
                                                        ALU.mult).then_inc(z["den_step"], 1)
                                dve.wait_ge(z["den_step"], at(lambda j: base(j) + 2))
                            dst = o_first if layer.diff and not second else o_second
                            if not layer.diff:
                                dst = o_norm[:].rearrange("p t (m d) -> p (t m) d", d=HD)
                                if some(u, 1):
                                    dve.wait_ge(z["job_ready"], at(lambda j: layer.order[("on", u(j) - 1)] + 1))
                            else:
                                dst = dst[:]
                            ins = nc.vector.tensor_tensor(dst, got[:, :, 0:HD],
                                                          rd.rearrange("p (m o) -> p m o", o=1).broadcast_to([P, QT * H, HD]),
                                                          ALU.mult)
                            ins.then_inc(z["job_taken"], 1)
                            if second:
                                dve.wait_ge(z["job_taken"], at(lambda j: no(j) + 1))
                                od = o_diff[:].rearrange("p t (m d) -> p (t m) d", d=HD)
                                nc.vector.tensor_tensor(od, o_first[:], o_second[:], ALU.subtract
                                                        ).then_inc(z["den_step"], 1)
                                dve.wait_ge(z["den_step"], at(lambda j: base(j) + 3))
                                if some(u, 2):
                                    dve.wait_ge(z["rr_step"], at(lambda j: 2 * (u(j) // 2)))
                                for t in range(QT):
                                    nc.vector.tensor_tensor_reduce(out=o_sq[:], in0=o_diff[:, t, :], in1=o_diff[:, t, :],
                                                                   scale=1.0, scalar=0.0, op0=ALU.mult, op1=ALU.add,
                                                                   accum_out=o_ss[:, t:t + 1]).then_inc(z["ss_step"], 1)
                                    dve.wait_ge(z["ss_step"], at(lambda j: 2 * (u(j) // 2) + t + 1))
                        elif name == "proj":
                            b = (lambda j: u(j) // 2) if layer.diff else u
                            dve.wait_ge(z["job_ready"], at(lambda j: no(j) + 1))
                            dve.wait_ge(z["res_ready"], at(lambda j: b(j) + 1))
                            if some(b, 1):
                                dve.wait_ge(z["x_out"], at(lambda j: 16 * b(j)))
                            nc.vector.tensor_tensor(x_new[:].rearrange("p t c -> p (t c)"), misc[:, 0:NQ],
                                                    x_res[:].rearrange("p t c -> p (t c)"), ALU.add
                                                    ).then_inc(z["job_taken"], 1)
            run_blocks(dve, layer, emit)

        def att_gpsimd(pool, layer):
            n, z = layer.n, S[layer.n]

            def emit(blk):
                at, live, some = blk.at, blk.live, blk.some
                for s in range(PAIR):
                    w, par = s % UNIT, s // UNIT
                    if s % 8 == 1:
                        c = lambda j: 4 * j + (s + 7) // 8
                        q = (s + 7) // 8 % 2
                        if live(c, 2 * layer.units):
                            pool.wait_ge(z["mx_taken"], at(lambda j: 16 * (c(j) + 1)))
                            if some(c, 2):
                                pool.wait_ge(z["job_ready"], at(lambda j: layer.order[("mt", c(j) - 2)] + 1))
                            part = [max_parts[:, q, :, k, :] for k in range(3)]
                            apart(pool)
                            nc.gpsimd.tensor_copy(part[0], row_max[:, q]).then_inc(z["mp_step"], 1)
                            pool.wait_ge(z["mp_step"], at(lambda j: 4 * c(j) + 1))
                            nc.gpsimd.tensor_tensor(max_rest[:], row_max[:, q], part[0], ALU.subtract
                                                    ).then_inc(z["mp_step"], 1)
                            pool.wait_ge(z["mp_step"], at(lambda j: 4 * c(j) + 2))
                            apart(pool)
                            nc.gpsimd.tensor_copy(part[1], max_rest[:]).then_inc(z["mp_step"], 1)
                            pool.wait_ge(z["mp_step"], at(lambda j: 4 * c(j) + 3))
                            nc.gpsimd.tensor_tensor(part[2], max_rest[:], part[1], ALU.subtract
                                                    ).then_inc(z["mp_step"], 1)
                    v = lambda j: 2 * j + s // UNIT + 2
                    if w == 3 and layer.leads(par) and live(v, layer.units):
                        b = lambda j: layer.lead_no(v(j))
                        pool.wait_ge(z["ln_step"], at(lambda j: 4 * b(j) + 4))
                        if some(b, 1):
                            pool.wait_ge(z["xn_ready"], at(lambda j: 2 * b(j)))
                        var = x_mv[:, :, 1:2].rearrange("p t o -> p (t o)")
                        apart(pool)
                        nc.gpsimd.tensor_scalar(x_rstd[:], var, LN_EPS, None, ALU.add).then_inc(z["rstd_step"], 1)
                        pool.wait_ge(z["rstd_step"], at(lambda j: 2 * b(j) + 1))
                        nc.gpsimd.tensor_tensor(x_rstd[:], x_rstd[:], half_neg[:, 0:QT], ALU.pow
                                                ).then_inc(z["rstd_step"], 1)
                    for f, sc in ((0, 11), (1, 3)):
                        vu = lambda j: 2 * j + s // UNIT + (1 if f == 0 else 0)
                        if w == sc and layer.leads(s // UNIT + (1 if f == 0 else 0)) and live(vu, layer.units):
                            pool.wait_ge(z["job_taken"], at(lambda j: layer.order[("v", vu(j))] + 1))
                            if some(vu, 1):
                                pool.wait_ge(z["pv_done"], at(lambda j: UNIT * vu(j) - (8 if f == 0 else 0)))
                            vp = (s // UNIT + (1 if f == 0 else 0)) % 2
                            for pp in range(2):
                                apart(pool)
                                nc.gpsimd.tensor_copy(
                                    vpad[:, f, pp, :, :, 16 * pp:16 * pp + HD],
                                    vals[:, vp, :, 64 * f + 32 * pp:64 * f + 32 * pp + 32].rearrange("p t (i d) -> p t i d", i=4)
                                ).then_inc(z["vpad_ready"], 1)
                    if (s - P_OT - 1) % UNIT == 0 and layer.diff and layer.ends((s - P_OT - 1) // UNIT):
                        uu = lambda j: 2 * j + (s - P_OT - 1) // UNIT
                        if live(uu, layer.units):
                            bb = lambda j: uu(j) // 2
                            pool.wait_ge(z["ss_step"], at(lambda j: 2 * bb(j) + 2))
                            if some(bb, 1):
                                pool.wait_ge(z["on_ready"], at(lambda j: 2 * bb(j)))
                            apart(pool)
                            nc.gpsimd.tensor_scalar(o_rr[:], o_ss[:], 1.0 / D, RMS_EPS, ALU.mult, ALU.add
                                                    ).then_inc(z["rr_step"], 1)
                            pool.wait_ge(z["rr_step"], at(lambda j: 2 * bb(j) + 1))
                            nc.gpsimd.tensor_tensor(o_rr[:], o_rr[:], half_neg[:, 0:QT], ALU.pow
                                                    ).then_inc(z["rr_step"], 1)
                    for name, u, no in blk.jobs(s):
                        if name in ("k", "q"):
                            cols, rest = ((slice(0, NK), rest_k) if name == "k" else (slice(NK, KQ), rest_q))
                            k = 0 if name == "k" else 2
                            pool.wait_ge(z["job_taken"], at(lambda j: no(j) + 1))
                            apart(pool)
                            nc.gpsimd.tensor_copy(parts[:, par, 1, cols], rest[:]).then_inc(z["split_step"], 1)
                            pool.wait_ge(z["split_step"], at(lambda j: 4 * u(j) + k + 1))
                            nc.gpsimd.tensor_tensor(parts[:, par, 2, cols], rest[:], parts[:, par, 1, cols],
                                                    ALU.subtract).then_inc(z["split_step"], 1)
                        if name == "on":
                            b = (lambda j: u(j) // 2) if layer.diff else u
                            pool.wait_ge(z["res_in"], at(lambda j: 16 * (b(j) + 1)))
                            nc.gpsimd.tensor_tensor(x_res[:], x_res[:], bias_o[:, n:n + 1, :].broadcast_to([P, QT, D]),
                                                    ALU.add).then_inc(z["res_ready"], 1)
            run_blocks(pool, layer, emit)

        for n in range(2):
            S[n]["ss_step"] = sem(f"ss_step{n}")

        def ffn_sems(n):
            names = ("x_all_in stat_step stat_rstd xn_all xt_bank xt_copied scored expd counted route_step "
                     "placed scattered wt_done wt_copied rows_t rows_taken up_done act_done hid_done hid_t "
                     "hidT_taken down_done out_taken x_again mixed stored").split()
            d = {k: sem(f"f_{k}{n}") for k in names}
            d["gathered"] = [sem(f"f_gathered{n}_{i}") for i in range(4)]
            d["rows_in"] = [sem(f"f_rows_in{n}_{i}") for i in range(2)]
            d["rows_out"] = [sem(f"f_rows_out{n}_{i}") for i in range(2)]
            return d

        Z = [ffn_sems(0), ffn_sems(1)]

        class Tiles:
            pairs = SLOTS // 2

        up_ps = [ps[:, 0, :], ps[:, 1, :]]
        gate_ps = [ps[:, 2, :], ps[:, 3, :]]
        hidT_ps = ps[:, 4, :]
        rowsT_ps = ps[:, 5, 0:P]
        down_ps = [ps[:, 6, 0:D], ps[:, 7, 0:D]]

        def x_tiles(ap):
            return ap.rearrange("b (t p) c -> p (b t) c", p=P)

        def ffn_sync(sp, n):
            z = Z[n]
            sp.dma_start(x_all[:], x_tiles(x_att[n])).then_inc(z["x_all_in"], 16)
            sp.wait_ge(z["scattered"], 16 * 2 * TT)
            sp.dma_start(x_all[:], x_tiles(x_att[n])).then_inc(z["x_again"], 16)
            src = rows_in.rearrange("(s p) c -> p s c", p=P)
            dst = rows_out.rearrange("(s p) c -> p s c", p=P)

            def emit(blk):
                at, live, some = blk.at, blk.live, blk.some
                for q in range(2):
                    t = lambda j: 2 * j + q + 2
                    if live(t, SLOTS):
                        if some(t, 2):
                            sp.wait_ge(z["rows_t"], at(lambda j: t(j) - 1))
                        sp.dma_start(s_rows[:, q:q + 1, :], src[:, bass.ds(at(t), 1), :]).then_inc(z["rows_in"][q], 16)
                    t2 = lambda j: 2 * j + q - 2
                    if live(t2, SLOTS):
                        sp.wait_ge(z["out_taken"], at(lambda j: t2(j) + 1))
                        sp.dma_start(dst[:, bass.ds(at(t2), 1), :], s_out[:, q:q + 1, :]).then_inc(z["rows_out"][q], 16)
            run_blocks(sp, Tiles, emit)
            for k in range(4):
                sp.wait_ge(z["mixed"], 2 * (4 * k + 4))
                sp.dma_start(x_tiles(x_ffn[n])[:, 4 * k:4 * k + 4, :], x_all[:, 4 * k:4 * k + 4, :]
                             ).then_inc(z["stored"], 16)
            sp.wait_ge(z["stored"], 64)

        def ffn_gpsimd(pool, n):
            z = Z[n]
            pool.wait_ge(z["stat_step"], 2 * TT)
            nc.gpsimd.tensor_scalar(t_rstd[:], t_mv[:, :, 1:2].rearrange("p t o -> p (t o)"), LN_EPS, None, ALU.add
                                    ).then_inc(z["stat_rstd"], 1)
            pool.wait_ge(z["stat_rstd"], 1)
            nc.gpsimd.tensor_tensor(t_rstd[:], t_rstd[:], half_neg[:], ALU.pow).then_inc(z["stat_rstd"], 1)
            pool.wait_ge(z["placed"], 2)
            pool.wait_ge(z["xn_all"], TT)
            pool.wait_ge(rows_zero, 16)
            for t in range(TT):
                for k in range(2):
                    nc.gpsimd.indirect_dma_start(
                        out=rows_in, out_offset=bass.IndirectOffsetOnAxis(ap=position[:, k, t:t + 1], axis=0),
                        in_=x_all[:, t, :], in_offset=None).then_inc(z["scattered"], 16)
            for q in range(2):
                pool.wait_ge(z["rows_out"][q], 16 * (SLOTS // 2))
            for t in range(TT):
                for k in range(2):
                    nc.gpsimd.indirect_dma_start(
                        out=y_all[:, 2 * t + k, :], out_offset=None, in_=rows_out,
                        in_offset=bass.IndirectOffsetOnAxis(ap=position[:, k, t:t + 1], axis=0)
                    ).then_inc(z["gathered"][t // 4], 16)

        def ffn_scalar(act, n):
            z = Z[n]
            for k in range(TT // 4):
                act.wait_ge(z["xt_bank"], k + 1)
                nc.scalar.copy(xT_all[:, 512 * k:512 * k + 512], ps[:, k, :]).then_inc(z["xt_copied"], 1)
            act.wait_ge(z["route_step"], EXP_AT[n][0])
            if n == 0:
                nc.scalar.activation(rt_b[:], rt_a[:], ACT.Exp, scale=-1.0).then_inc(z["expd"], 1)
                act.wait_ge(z["route_step"], EXP_AT[n][1])
                nc.scalar.activation(rt_b[:], rt_a[:], ACT.Exp, scale=-1.0).then_inc(z["expd"], 1)
            else:
                nc.scalar.activation(rt_k[:], share_d[:], ACT.Exp, scale=-1.0).then_inc(z["expd"], 1)
            if n == 0:
                for k in range(3 * E):
                    act.wait_ge(z["wt_done"], k + 1)
                    nc.scalar.copy(w_exp[:, k // E, k % E, :], ps[:, 6 + k % 2, :]).then_inc(z["wt_copied"], 1)

            def emit(blk):
                at, live, some = blk.at, blk.live, blk.some
                for q in range(2):
                    t = lambda j: 2 * j + q + 1
                    if live(t, SLOTS):
                        act.wait_ge(z["rows_t"], at(lambda j: t(j) + 1))
                        if some(t, 2):
                            act.wait_ge(z["up_done"], at(lambda j: t(j) - 1))
                        nc.scalar.copy(s_rowsT[:, 1 - q, :], rowsT_ps).then_inc(z["rows_taken"], 1)
                    t1 = lambda j: 2 * j + q - 1
                    if live(t1, SLOTS):
                        act.wait_ge(z["hid_t"], at(lambda j: t1(j) + 1))
                        if some(t1, 2):
                            act.wait_ge(z["down_done"], at(lambda j: t1(j) - 1))
                        nc.scalar.copy(s_hidT[:, 1 - q, :], hidT_ps).then_inc(z["hidT_taken"], 1)
                    t0 = lambda j: 2 * j + q
                    if live(t0, SLOTS):
                        act.wait_ge(z["up_done"], at(lambda j: t0(j) + 1))
                        if some(t0, 2):
                            act.wait_ge(z["hid_done"], at(lambda j: t0(j) - 1))
                        nc.scalar.activation(s_act[:, q, :], up_ps[q], ACT.Silu).then_inc(z["act_done"], 1)
            run_blocks(act, Tiles, emit)

        def ffn_tensor(pe, n):
            z = Z[n]
            pe.wait_ge(w_exp_in, 16 * W_EXP_DMAS[n])
            if n == 0:
                nc.tensor.transpose(ps[:, 7, 0:E], gate_raw[:], ident[0:E, 0:E]).then_inc(z["counted"], 1)
            for k in range(TT // 4):
                pe.wait_ge(z["xn_all"], 4 * k + 4)
                for i in range(4):
                    ins = nc.tensor.transpose(ps[:, k, i * P:(i + 1) * P], x_all[:, 4 * k + i, :], ident[:])
                ins.then_inc(z["xt_bank"], 1)
            if n == 0:
                pe.wait_ge(gate_ready, 1)
            for k in range(TT // 4):
                pe.wait_ge(z["xt_copied"], k + 1)
                for i in range(4):
                    t = 4 * k + i
                    ins = nc.tensor.matmul(ps[:, 4, t * E:(t + 1) * E], xT_all[:, t * P:(t + 1) * P], w_gate[:, n, :],
                                           start=True, stop=True)
            ins.then_inc(z["scored"], 1)
            pe.wait_ge(const_step, 3)
            pe.wait_ge(z["route_step"], PICK_AT[n])
            flat = picked[:].rearrange("p t e -> p (t e)")
            nc.tensor.matmul(ps[:, 5, 0:P], tri[:], flat, start=True, stop=True)
            nc.tensor.matmul(ps[:, 5, P:2 * P], ones[:], flat, start=True, stop=True).then_inc(z["counted"], 1)
            if n == 0:
                for k in range(3 * E):
                    if k >= 2:
                        pe.wait_ge(z["wt_copied"], k - 1)
                    for c in range(FC):
                        ins = nc.tensor.transpose(ps[:, 6 + k % 2, c * P:(c + 1) * P],
                                                  w_exp[:, k // E, k % E, c * P:(c + 1) * P], ident[:])
                    ins.then_inc(z["wt_done"], 1)
                pe.wait_ge(z["wt_copied"], 3 * E)
            pe.wait_ge(z["placed"], 2)

            def emit(blk):
                at, live, some = blk.at, blk.live, blk.some
                for q in range(2):
                    t = lambda j: 2 * j + q + 1
                    if live(t, SLOTS):
                        cyc = lambda j: t(j) // 2 + 1
                        pe.wait_ge(z["rows_in"][1 - q], at(lambda j: 16 * cyc(j)))
                        if some(t, 1):
                            pe.wait_ge(z["rows_taken"], at(t))
                        nc.tensor.transpose(rowsT_ps, s_rows[:, 1 - q, :], ident[:]).then_inc(z["rows_t"], 1)
                    t0 = lambda j: 2 * j + q
                    if live(t0, SLOTS):
                        e = pe.value_load(expert_of[0:1, bass.ds(at(t0), 1)], min_val=0, max_val=E - 1)
                        pe.wait_ge(z["rows_taken"], at(lambda j: t0(j) + 1))
                        if some(t0, 2):
                            pe.wait_ge(z["act_done"], at(lambda j: t0(j) - 1))
                            pe.wait_ge(z["hid_done"], at(lambda j: t0(j) - 1))
                        for k, dst in ((0, up_ps[q]), (1, gate_ps[q])):
                            ins = nc.tensor.matmul(dst, s_rowsT[:, q, :],
                                                   w_exp[:, k, bass.ds(e, 1), :].rearrange("p e f -> p (e f)"),
                                                   start=True, stop=True)
                        ins.then_inc(z["up_done"], 1)
                    t1 = lambda j: 2 * j + q - 1
                    if live(t1, SLOTS):
                        pe.wait_ge(z["hid_done"], at(lambda j: t1(j) + 1))
                        if some(t1, 1):
                            pe.wait_ge(z["hidT_taken"], at(t1))
                        for c in range(FC):
                            ins = nc.tensor.transpose(hidT_ps[:, c * P:(c + 1) * P],
                                                      s_hid[:, 1 - q, c * P:(c + 1) * P], ident[:])
                        ins.then_inc(z["hid_t"], 1)
                    t2 = lambda j: 2 * j + q - 2
                    if live(t2, SLOTS):
                        e = pe.value_load(expert_of[0:1, bass.ds(at(t2), 1)], min_val=0, max_val=E - 1)
                        pe.wait_ge(z["hidT_taken"], at(lambda j: t2(j) + 1))
                        if some(t2, 2):
                            pe.wait_ge(z["out_taken"], at(lambda j: t2(j) - 1))
                        for c in range(FC):
                            ins = nc.tensor.matmul(down_ps[q], s_hidT[:, q, c * P:(c + 1) * P],
                                                   w_exp[:, 2, bass.ds(e, 1), c * P:(c + 1) * P
                                                         ].rearrange("p e f -> p (e f)"),
                                                   start=(c == 0), stop=(c == FC - 1))
                        ins.then_inc(z["down_done"], 1)
            run_blocks(pe, Tiles, emit)

        EXP_AT, PICK_AT = [[None, None], [None]], [None, None]

        def route(dve, n, dry=False):
            z = Z[n]
            count = [0]

            def step(make):
                count[0] += 1
                if not dry:
                    make().then_inc(z["route_step"], 1)
                    dve.wait_ge(z["route_step"], count[0])

            V = nc.vector
            by_token = lambda ap: ap.rearrange("p (t o) -> p t o", o=1).broadcast_to([P, TT, E])
            by_expert = lambda ap: ap.rearrange("p (o e) -> p o e", o=1).broadcast_to([P, TT, E])
            if not dry:
                dve.wait_ge(z["scored"], 1)
            step(lambda: V.tensor_copy(gate_s[:].rearrange("p t e -> p (t e)"), ps[:, 4, 0:TT * E]))
            for k, src in ((0, gate_s), (1, gate_s2)):
                step(lambda: V.tensor_reduce(top[:, k, :], src[:], axis=AX.X, op=ALU.max))
                step(lambda: V.tensor_tensor(rt_a[:], src[:], by_token(top[:, k, :]), ALU.is_equal))
                step(lambda: V.tensor_tensor(rt_a[:], rt_a[:], by_expert(rev[:]), ALU.mult))
                step(lambda: V.tensor_reduce(rt_k[:], rt_a[:], axis=AX.X, op=ALU.max))
                step(lambda: V.tensor_tensor(hot[:, k], by_expert(rev[:]), by_token(rt_k[:]), ALU.is_equal))
                if k == 0:
                    step(lambda: V.scalar_tensor_tensor(out=gate_s2[:], in0=hot[:, 0], scalar=-BIG, in1=gate_s[:],
                                                        op0=ALU.mult, op1=ALU.add))
            step(lambda: V.tensor_tensor(picked[:], hot[:, 0], hot[:, 1], ALU.add))
            PICK_AT[n] = count[0]
            if n == 0:
                step(lambda: V.scalar_tensor_tensor(out=gate_abs[:], in0=gate_s[:], scalar=-1.0, in1=gate_s[:],
                                                    op0=ALU.mult, op1=ALU.max))
                for k, src in ((0, gate_s), (1, gate_s2)):
                    step(lambda: V.tensor_tensor(rt_a[:], by_token(top[:, k, :]), src[:], ALU.subtract))
                    EXP_AT[0][k] = count[0]
                    step(lambda: V.tensor_tensor(place[:], gate_abs[:], by_token(top[:, k, :]), ALU.max))
                    step(lambda: V.scalar_tensor_tensor(out=place[:], in0=place[:], scalar=0.02, in1=rt_a[:],
                                                        op0=ALU.mult, op1=ALU.is_ge))
                    if not dry:
                        dve.wait_ge(z["expd"], k + 1)
                    step(lambda: V.tensor_tensor(place[:], place[:], rt_b[:], ALU.mult))
                    step(lambda: V.tensor_reduce(share_d[:], place[:], axis=AX.X, op=ALU.add))
                    step(lambda: V.reciprocal(share[:, k, :], share_d[:]))
            else:
                step(lambda: V.tensor_tensor(share_d[:], top[:, 0, :], top[:, 1, :], ALU.subtract))
                EXP_AT[1][0] = count[0]
                if not dry:
                    dve.wait_ge(z["expd"], 1)
                step(lambda: V.tensor_scalar(share_d[:], rt_k[:], 1.0, None, ALU.add))
                step(lambda: V.reciprocal(share[:, 0, :], share_d[:]))
                step(lambda: V.tensor_tensor(share[:, 1, :], share[:, 0, :], rt_k[:], ALU.mult))
            if not dry:
                dve.wait_ge(z["counted"], 2 if n == 0 else 1)
            step(lambda: V.tensor_copy(total[:], ps[:, 5, P:2 * P].rearrange("p (t e) -> p e t", e=E)))
            step(lambda: V.tensor_tensor_scan(upto[:].rearrange("p e t -> p (e t)"), carry[:].rearrange("p e t -> p (e t)"),
                                              total[:].rearrange("p e t -> p (e t)"), 0.0, ALU.mult, ALU.add))
            step(lambda: V.tensor_tensor(more[:], upto[:, :, TT - 1:TT].broadcast_to([P, E, TT]),
                                         full_rows[:].rearrange("p (o t) -> p o t", o=1).broadcast_to([P, E, TT]),
                                         ALU.is_gt))
            step(lambda: V.tensor_reduce(n_tiles[:], more[:], axis=AX.X, op=ALU.add))
            step(lambda: V.tensor_tensor_scan(tile_end[:], carry[:, 0:1, 1:1 + E].rearrange("p o t -> p (o t)"),
                                              n_tiles[:], 0.0, ALU.mult, ALU.add))
            step(lambda: V.tensor_tensor(tile_at[:], tile_end[:], n_tiles[:], ALU.subtract))
            step(lambda: V.tensor_tensor(done_e[:], tile_end[:].rearrange("p (o e) -> p o e", o=1).broadcast_to([P, SLOTS, E]),
                                         slot_no[:].rearrange("p (s o) -> p s o", o=1).broadcast_to([P, SLOTS, E]),
                                         ALU.is_le))
            step(lambda: V.tensor_reduce(tile_e[:], done_e[:], axis=AX.X, op=ALU.add))
            if not dry:
                V.tensor_scalar(expert_of[:], tile_e[:], float(E - 1), None, ALU.min).then_inc(z["placed"], 1)
            step(lambda: V.tensor_tensor(upto[:], upto[:], total[:], ALU.subtract))
            step(lambda: V.tensor_tensor(place[:], ps[:, 5, 0:P].rearrange("p (t e) -> p t e", e=E),
                                         upto[:].rearrange("p e t -> p t e"), ALU.add))
            step(lambda: V.scalar_tensor_tensor(out=place[:], in0=by_expert(tile_at[:]), scalar=float(P), in1=place[:],
                                                op0=ALU.mult, op1=ALU.add))
            step(lambda: V.tensor_tensor(hot[:], hot[:], place[:].rearrange("p (o t) e -> p o t e", o=1
                                                                          ).broadcast_to([P, 2, TT, E]), ALU.mult))
            step(lambda: V.tensor_reduce(place_f[:], hot[:], axis=AX.X, op=ALU.add))
            if not dry:
                V.tensor_copy(position[:], place_f[:]).then_inc(z["placed"], 1)

        for n in range(2):
            route(None, n, dry=True)

        def ffn_vector(dve, n):
            z = Z[n]
            dve.wait_ge(z["x_all_in"], 16)
            for t in range(TT):
                nc.vector.bn_stats(t_stat[:, t, :], x_all[:, t, :]).then_inc(z["stat_step"], 1)
            for t in range(TT):
                dve.wait_ge(z["stat_step"], TT)
                nc.vector.bn_aggr(t_mv[:, t, :], t_stat[:, t, :]).then_inc(z["stat_step"], 1)
            if n == 0:
                dve.wait_ge(z["counted"], 1)
                nc.vector.tensor_copy(w_gate[:, 0, :], ps[:, 7, 0:E]).then_inc(gate_ready, 1)
            dve.wait_ge(z["stat_rstd"], 2)
            for t in range(TT):
                nc.vector.tensor_scalar(x_all[:, t, :], x_all[:, t, :], t_mv[:, t, 0:1], t_rstd[:, t:t + 1],
                                        ALU.subtract, ALU.mult).then_inc(z["xn_all"], 1)
            route(dve, n)

            def emit(blk):
                at, live, some = blk.at, blk.live, blk.some
                for q in range(2):
                    t0 = lambda j: 2 * j + q
                    t2 = lambda j: 2 * j + q - 2
                    if live(t2, SLOTS):
                        dve.wait_ge(z["down_done"], at(lambda j: t2(j) + 1))
                        if some(t2, 2):
                            dve.wait_ge(z["rows_out"][q], at(lambda j: 16 * (t2(j) // 2)))
                        nc.vector.tensor_copy(s_out[:, q, :], down_ps[q]).then_inc(z["out_taken"], 1)
                    if live(t0, SLOTS):
                        dve.wait_ge(z["act_done"], at(lambda j: t0(j) + 1))
                        if some(t0, 2):
                            dve.wait_ge(z["hid_t"], at(lambda j: t0(j) - 1))
                        nc.vector.tensor_tensor(s_hid[:, q, :], gate_ps[q], s_act[:, q, :], ALU.mult
                                                ).then_inc(z["hid_done"], 1)
            run_blocks(dve, Tiles, emit)
            dve.wait_ge(z["x_again"], 16)
            for k in range(4):
                dve.wait_ge(z["gathered"][k], 16 * 8)
                for e in range(2):
                    if e:
                        dve.wait_ge(z["mixed"], 2 * 4 * k + 4)
                    for t in range(4 * k, 4 * k + 4):
                        nc.vector.scalar_tensor_tensor(out=x_all[:, t, :], in0=y_all[:, 2 * t + e, :],
                                                       scalar=share[:, e, t:t + 1], in1=x_all[:, t, :],
                                                       op0=ALU.mult, op1=ALU.add).then_inc(z["mixed"], 1)

        def next_phase(eng, k):
            eng.drain().then_inc(phase[k], 1)
            eng.wait_ge(phase[k], 5)

        @block.sync
        def _(sp):
            start_sync(sp)
            load_experts(sp, 0)
            sp.wait_ge(const_step, 3)
            sp.dma_start(rows_in.rearrange("(s p) c -> p s c", p=P),
                         zero_row[:].rearrange("p (o c) -> p o c", o=1).broadcast_to([P, SLOTS, D])
                         ).then_inc(rows_zero, 16)
            att_sync(sp, L[0])
            next_phase(sp, 0)
            ffn_sync(sp, 0)
            next_phase(sp, 1)
            load_experts(sp, 1)
            att_sync(sp, L[1])
            next_phase(sp, 2)
            ffn_sync(sp, 1)

        @block.gpsimd
        def _(pool):
            start_gpsimd(pool)
            att_gpsimd(pool, L[0])
            next_phase(pool, 0)
            ffn_gpsimd(pool, 0)
            next_phase(pool, 1)
            att_gpsimd(pool, L[1])
            next_phase(pool, 2)
            ffn_gpsimd(pool, 1)

        @block.scalar
        def _(act):
            act.wait_ge(wt_taken, 10)
            act.wait_ge(zero_done, 5)
            act.wait_ge(gp_init, GP_INIT)
            act.wait_ge(w_in, 16 * W_DMAS)
            att_scalar(act, L[0])
            next_phase(act, 0)
            ffn_scalar(act, 0)
            next_phase(act, 1)
            att_scalar(act, L[1])
            next_phase(act, 2)
            ffn_scalar(act, 1)

        @block.vector
        def _(dve):
            start_vector(dve)
            dve.wait_ge(gp_init, GP_INIT)
            att_vector(dve, L[0])
            next_phase(dve, 0)
            ffn_vector(dve, 0)
            next_phase(dve, 1)
            att_vector(dve, L[1])
            next_phase(dve, 2)
            ffn_vector(dve, 1)

        @block.tensor
        def _(pe):
            start_tensor(pe)
            att_tensor(pe, L[0])
            next_phase(pe, 0)
            ffn_tensor(pe, 0)
            next_phase(pe, 1)
            att_tensor(pe, L[1])
            next_phase(pe, 2)
            ffn_tensor(pe, 1)


_INS = ["x", "ctx_1024",
        "L0_xattn_q1_w", "L0_xattn_q2_w", "L0_xattn_kv1_w", "L0_xattn_kv2_w", "L0_xattn_proj_w", "L0_xattn_proj_b",
        "L0_xattn_norm_w", "L0_xattn_lambda_1", "L0_xattn_lambda_2",
        "L0_ffn_gate_w", "L0_ffn_w1", "L0_ffn_w2", "L0_ffn_w3",
        "L1_xattn_W_q", "L1_xattn_b_q", "L1_xattn_W_k", "L1_xattn_b_k", "L1_xattn_W_v", "L1_xattn_b_v",
        "L1_xattn_W_o", "L1_xattn_b_o",
        "L1_ffn_gate_kernel", "L1_ffn_w0", "L1_ffn_w1", "L1_ffn_wo"]


def kernel(**inputs):
    import numpy as np
    import concourse.bacc as bacc
    from concourse.bass_utils import run_bass_kernel_spmd

    nc = bacc.Bacc("TRN2", target_bir_lowering=False, num_devices=1)
    arrays, aps = {}, {}
    for name in _INS:
        x = np.ascontiguousarray(inputs[name])
        arrays[f"in_{name}_dram"] = x
        aps[name] = nc.dram_tensor(f"in_{name}_dram", x.shape, mybir.dt.from_np(x.dtype), kind="ExternalInput").ap()
    out = nc.dram_tensor("out_dram", (B, NQ, D), F32, kind="ExternalOutput").ap()
    build(nc, aps, out)
    return run_bass_kernel_spmd(nc, [arrays], core_ids=[0]).results[0]["out_dram"]
```

```python
from contextlib import ExitStack

import concourse.bass as bass
from concourse import mybir

ALU = mybir.AluOpType
ACT = mybir.ActivationFunctionType
AX = mybir.AxisListType
F32 = mybir.dt.float32
BF16 = mybir.dt.bfloat16
I32 = mybir.dt.int32
U32 = mybir.dt.uint32

P = 128
B, NQ, NK, D = 8, 256, 512, 128
H, HD = 16, 8
HH = H // 2
KT, QT = NK // P, NQ // P
SCALE = HD ** -0.5
LN_EPS, RMS_EPS, LAMBDA_INIT = 1e-5, 1e-6, 0.1
E, F = 8, 512
FC = F // P
TOK = B * NQ
TT = TOK // P
SLOTS = TT * 2 + E
BIG = 3.0e38
TWO_ONES = 1.0 + 0x3F80 / 2.0 ** 23
UNIT = 16
PAIR = 2 * UNIT
KQ = NK + NQ

TERMS = [(0, 0), (1, 1), (0, 1), (1, 0), (0, 2), (2, 0)]
TROWS = len(TERMS) * HD
MROW = 96
STACK_DMAS = 10

W_LOAD, W_CT, W_K, W_XT, W_Q, W_V = 0, 2, 3, 6, 7, 12
P_O, P_OT, P_ON, P_PROJ = 18, 25, 30, 32
P_DIFF, P_SUMS, P_RMS, P_NORM = P_OT + 1, P_OT + 2, P_OT + 2, P_OT + 4
M_T = 3


class Layer:
    loops = 1

    def __init__(self, n):
        self.n = n
        self.diff = n == 0
        self.units = 2 * B if self.diff else B
        self.pairs = self.units // 2
        self.steps = self.units * UNIT
        self.order = {}
        for g in range(-PAIR, self.steps + PAIR):
            for job in self.jobs(g):
                if 0 <= job[1] < (2 * self.units if job[0] == "mt" else self.units):
                    self.order[job] = len(self.order)

    def leads(self, u):
        return not self.diff or u % 2 == 0

    def ends(self, u):
        return not self.diff or u % 2 == 1

    def jobs(self, g):
        w = g % UNIT
        v = (g - w) // UNIT + 2
        out = []
        if w == W_CT and self.leads(v):
            out.append(("ct", v))
        if w == W_K:
            out.append(("k", v))
        if w == W_XT and self.leads(v):
            out.append(("xt", v))
        if w == W_Q:
            out.append(("q", v))
        if w == W_V and self.leads(v):
            out.append(("v", v))
        if (g + M_T) % 8 == 0:
            out.append(("mt", (g + M_T) // 8))
        for name, p in (("ot", P_OT), ("on", P_ON), ("proj", P_PROJ)):
            if (g - p) % UNIT == 0 and (name == "ot" or self.ends((g - p) // UNIT)):
                out.append((name, (g - p) // UNIT))
        return out

    def lead_no(self, v):
        return v // 2 if self.diff else v


class Block:

    def __init__(self, layer, j=None, it=None):
        self.layer, self.j, self.it = layer, j, it

    def at(self, f):
        if self.it is None:
            return f(self.j)
        j = self.layer.loops
        return f(j) + (f(j + 1) - f(j)) * self.it

    def live(self, f, n):
        return self.it is not None or 0 <= f(self.j) < n

    def some(self, f, least):
        return f(self.layer.loops if self.it is not None else self.j) >= least

    def jobs(self, s):
        j0 = self.layer.loops if self.it is not None else self.j
        out = []
        for name, v in self.layer.jobs(PAIR * j0 + s):
            per = 4 if name == "mt" else 2
            if (name, v) in self.layer.order:
                unit = lambda j, v=v, per=per: v + per * (j - j0)
                out.append((name, unit, lambda j, name=name, unit=unit: self.layer.order[(name, unit(j))]))
        return out


def run_blocks(eng, layer, emit):
    for j in range(-1, layer.loops):
        emit(Block(layer, j=j))
    with eng.Fori(0, layer.pairs - 1 - layer.loops) as it:
        emit(Block(layer, it=it))
    emit(Block(layer, j=layer.pairs - 1))
    emit(Block(layer, j=layer.pairs))


def build(nc, a, out):
    L = [Layer(0), Layer(1)]
    with ExitStack() as ctx:
        def sb(name, shape, dt=F32):
            return ctx.enter_context(nc.sbuf_tensor(name, shape, dt))

        def sem(name):
            return ctx.enter_context(nc.semaphore(name))

        def dram(name, shape, dt=F32):
            return nc.dram_tensor(name, shape, dt).ap()

        rows_in = dram("rows_in", (SLOTS * P, D))
        rows_out = dram("rows_out", (SLOTS * P, D))

        ident = sb("ident", [P, P])
        identb = sb("identb", [P, P], BF16)
        stack = sb("stack", [P, 4, HH, KQ], BF16)
        parts = sb("parts", [P, 2, 3, KQ], BF16)
        rest_k = sb("rest_k", [P, NK])
        rest_q = sb("rest_q", [P, NQ])
        probs = sb("probs", [P, 4, 4, NQ])
        vpad = sb("vpad", [P, 2, 2, KT, 4, 32])
        vals = sb("vals", [P, 2, KT, D])
        ctx_sb = sb("ctx_sb", [P, KT, D])
        ctxT = sb("ctxT", [P, NK])
        x_all = sb("x_all", [P, TT, D])
        x_stat = sb("x_stat", [P, QT, 6])
        x_mv = sb("x_mv", [P, QT, 2])
        x_rstd = sb("x_rstd", [P, QT])
        xn = sb("xn", [P, QT, D])
        xnT = sb("xnT", [P, NQ])
        row_max = sb("row_max", [P, 2, QT, HH])
        max_rest = sb("max_rest", [P, QT, HH])
        max_parts = sb("max_parts", [P, 2, QT, 3, HH], BF16)
        max_rows = sb("max_rows", [3 * HH, 2, NQ], BF16)
        outT = sb("outT", [P, 2, NQ])
        r_den = sb("r_den", [P, QT, H])
        o_first = sb("o_first", [P, QT * H, HD])
        o_second = sb("o_second", [P, QT * H, HD])
        o_diff = sb("o_diff", [P, QT, D])
        o_sq = sb("o_sq", [P, D])
        o_ss = sb("o_ss", [P, QT])
        o_rr = sb("o_rr", [P, QT])
        o_norm = sb("o_norm", [P, QT, D])
        onT = sb("onT", [P, NQ])
        half_neg = sb("half_neg", [P, TT])
        raw = sb("raw", [P, 10, D])
        raw_perm = sb("raw_perm", [P, 2, D])
        w_all = sb("w_all", [P, 10, D])
        bias_k = sb("bias_k", [P, 2])
        bias_q = sb("bias_q", [P, 2])
        bias_v = sb("bias_v", [P, 2, D])
        bias_o = sb("bias_o", [P, 2, D])
        norm_col = sb("norm_col", [P, 1])
        lam_in = sb("lam_in", [P, 2, H])
        lam_d = sb("lam_d", [P, H])
        lam = sb("lam", [P, H])

        zero_row = sb("zero_row", [P, D])
        place_f = sb("place_f", [P, 2, TT])
        w_exp = sb("w_exp", [P, 3, E, F])
        gate_raw = sb("gate_raw", [E, D])
        w_gate = sb("w_gate", [P, 2, E])
        xn_all = sb("xn_all", [P, TT, D])
        xT_all = probs[:].rearrange("p a i n -> p (a i n)")[:, 0:TOK]
        y_all = probs[:].rearrange("p a i (n c) -> p (a i n) c", c=D)
        t_stat = sb("t_stat", [P, TT, 6])
        t_mv = sb("t_mv", [P, TT, 2])
        t_rstd = sb("t_rstd", [P, TT])
        tri = sb("tri", [P, P], BF16)
        ones = sb("ones", [P, P], BF16)
        i_rev = sb("i_rev", [P, E], I32)
        rev = sb("rev", [P, E])
        i_slot = sb("i_slot", [P, SLOTS], I32)
        slot_no = sb("slot_no", [P, SLOTS])
        i_full = sb("i_full", [P, TT], I32)
        full_rows = sb("full_rows", [P, TT])
        carry = sb("carry", [P, E, TT])
        gate_s = sb("gate_s", [P, TT, E])
        gate_s2 = sb("gate_s2", [P, TT, E])
        gate_abs = sb("gate_abs", [P, TT, E])
        top = sb("top", [P, 2, TT])
        rt_a = sb("rt_a", [P, TT, E])
        rt_b = sb("rt_b", [P, TT, E])
        rt_k = sb("rt_k", [P, TT])
        hot = sb("hot", [P, 2, TT, E])
        picked = sb("picked", [P, TT, E], BF16)
        share = sb("share", [P, 2, TT])
        share_d = sb("share_d", [P, TT])
        total = sb("total", [P, E, TT])
        upto = sb("upto", [P, E, TT])
        more = sb("more", [P, E, TT])
        n_tiles = sb("n_tiles", [P, E])
        tile_end = sb("tile_end", [P, E])
        tile_at = sb("tile_at", [P, E])
        place = sb("place", [P, TT, E])
        done_e = sb("done_e", [P, SLOTS, E])
        tile_e = sb("tile_e", [P, SLOTS])
        expert_of = sb("expert_of", [P, SLOTS], I32)
        position = sb("position", [P, 2, TT], U32)
        s_rows = sb("s_rows", [P, 2, D])
        s_rowsT = sb("s_rowsT", [P, 2, P])
        s_act = sb("s_act", [P, 2, F])
        s_hid = sb("s_hid", [P, 2, F])
        s_hidT = sb("s_hidT", [P, 2, F])
        s_out = sb("s_out", [P, 2, D])

        ps = ctx.enter_context(nc.psum_tensor("ps", [P, 8, 512], F32))
        score = [ps[:, 0:2, :].rearrange("p b (i n) -> p (b i) n", i=2),
                 ps[:, 2:4, :].rearrange("p b (i n) -> p (b i) n", i=2)]
        maxs = [ps[:, 4, :], ps[:, 5, :]]
        oacc = ps[:, 6, :].rearrange("p (f n) -> p f n", f=2)
        misc = ps[:, 7, :]
        misc_bf = misc.bitcast(BF16)

        w_in = sem("w_in")
        bias_in = sem("bias_in")
        x_start = sem("x_start")
        ones_done = sem("ones_done")
        gp_init = sem("gp_init")
        late_init = sem("late_init")
        raw_perm_ready = sem("raw_perm_ready")
        wt_ready = sem("wt_ready")
        wt_taken = sem("wt_taken")
        zero_done = sem("zero_done")
        const_step = sem("const_step")
        rows_zero = sem("rows_zero")
        w_exp_in = sem("w_exp_in")
        lam_step = sem("lam_step")
        gate_ready = sem("gate_ready")
        carrier = sem("carrier")

        WQ = [[0, 1], [6, 6]]
        WK = [[2, 3], [7, 7]]
        WV = [4, 8]
        WO = [5, 9]

        def heads_last(ap):
            return ap.rearrange("p (f h d) -> p f d h", f=2, h=HH)

        block = ctx.enter_context(nc.Block())

        def att_sems(n):
            names = ("ctx_in qk_done exp_done pv_done mx_ready mx_taken job_ready job_taken a1_done "
                     "split_step vpad_ready ln_step rstd_step xn_ready mp_step o_taken den_step on_ready "
                     "rr_step res_ready x_added").split()
            d = {k: sem(f"{k}{n}") for k in names}
            d["stack_in"] = [sem(f"stack_in{n}_{i}") for i in range(4)]
            d["mrow_in"] = [sem(f"mrow_in{n}_{i}") for i in range(2)]
            return d

        S = [att_sems(0), att_sems(1)]
        phase = [sem(f"phase{i}") for i in range(3)]

        def start_sync(sp):
            sp.dma_start(ctx_sb[:], a["ctx_1024"][0].rearrange("(t p) c -> p t c", p=P)).then_inc(S[0]["ctx_in"], 16)
            xs = a["x"].rearrange("b (t p) c -> p (b t) c", p=P)
            sp.dma_start(x_all[:, 0:QT, :], xs[:, 0:QT, :]).then_inc(x_start, 16)
            for i, src in ((0, a["L0_xattn_q1_w"]), (1, a["L0_xattn_q2_w"]), (2, a["L0_xattn_kv1_w"][0:D, :]),
                           (3, a["L0_xattn_kv2_w"][0:D, :]), (4, a["L0_xattn_kv1_w"][D:2 * D, :]),
                           (5, a["L0_xattn_proj_w"]), (6, a["L1_xattn_W_q"]), (7, a["L1_xattn_W_k"]),
                           (8, a["L1_xattn_W_v"]), (9, a["L1_xattn_W_o"])):
                sp.dma_start(raw[:, i, :], src).then_inc(w_in, 16)
            for f in range(2):
                r = slice(f * 64, f * 64 + 64)
                for i in range(4):
                    sp.dma_start(norm_col[64 * f + 16 * i:64 * f + 16 * i + 16, :],
                                 a["L0_xattn_norm_w"][r].rearrange("(q i d o) -> i q d o", q=2, i=4, o=1)[i],
                                 allow_slow_non_contiguous=True).then_inc(w_in, 16)
            for i, name in enumerate(("L0_xattn_lambda_1", "L0_xattn_lambda_2")):
                sp.dma_start(lam_in[:, i, :], a[name].rearrange("a h b c -> (a h b c)").partition_broadcast(P)
                             ).then_inc(w_in, 16)
            sp.dma_start(x_all[:, QT:TT, :], xs[:, QT:TT, :]).then_inc(x_start, 16)
            sp.dma_start(bias_o[:, 0, :], a["L0_xattn_proj_b"].partition_broadcast(P)).then_inc(bias_in, 16)

        def load_biases(sp):
            for f in range(2):
                r = slice(f * 64, f * 64 + 64)
                for col, src in ((bias_q, a["L1_xattn_b_q"]), (bias_k, a["L1_xattn_b_k"])):
                    sp.dma_start(col[r, 1:2], src[r].rearrange("(h d o) -> d h o", h=HH, o=1),
                                 allow_slow_non_contiguous=True).then_inc(bias_in, 16)
            for tile, src in ((bias_o[:, 1, :], a["L1_xattn_b_o"]), (bias_v[:, 1, :], a["L1_xattn_b_v"])):
                sp.dma_start(tile, src.partition_broadcast(P)).then_inc(bias_in, 16)

        def load_expert(pool, n, e):
            up, gate, down = w_exp[:, 0, e, :], w_exp[:, 1, e, :], w_exp[:, 2, e, :]
            chunks = lambda ap: ap.rearrange("p (c h) -> p c h", c=FC)
            if n == 0:
                if e == 0:
                    pool.dma_start(gate_raw[:], a["L0_ffn_gate_w"]).then_inc(w_exp_in, 16)
                pool.dma_start(chunks(up), a["L0_ffn_w1"][e].rearrange("(c p) h -> p c h", p=P)).then_inc(w_exp_in, 16)
                pool.dma_start(chunks(gate), a["L0_ffn_w3"][e].rearrange("(c p) h -> p c h", p=P)
                               ).then_inc(w_exp_in, 16)
                pool.dma_start(down, a["L0_ffn_w2"][e]).then_inc(w_exp_in, 16)
            else:
                if e == 0:
                    pool.dma_start(w_gate[:, 1, :], a["L1_ffn_gate_kernel"]).then_inc(w_exp_in, 16)
                pool.dma_start(up, a["L1_ffn_w0"][e]).then_inc(w_exp_in, 16)
                pool.dma_start(gate, a["L1_ffn_w1"][e]).then_inc(w_exp_in, 16)
                pool.dma_start(chunks(down), a["L1_ffn_wo"][e].rearrange("(c p) d -> p c d", p=P)
                               ).then_inc(w_exp_in, 16)

        W_EXP_DMAS = [1 + 3 * E, 2 * (1 + 3 * E)]

        W_DMAS = 10 + 2 * 4 + 2

        def zero_view(c):
            return stack[:, c, :, :].bitcast(F32)

        def start_gpsimd(pool):
            for c in range(2, 4):
                nc.gpsimd.memset(zero_view(c), 0.0).then_inc(zero_done, 1)
            nc.gpsimd.memset(ident[:], 1.0).then_inc(gp_init, 1)
            pool.wait_ge(gp_init, 1)
            nc.gpsimd.affine_select(out=ident[:], in_=ident[:], compare_op=ALU.is_equal, fill=0.0, base=0,
                                    pattern=[[-1, P]], channel_multiplier=1).then_inc(gp_init, 1)
            pool.wait_ge(gp_init, 2)
            nc.gpsimd.tensor_copy(identb[:], ident[:]).then_inc(gp_init, 1)
            nc.gpsimd.memset(half_neg[:], -0.5).then_inc(gp_init, 1)
            nc.gpsimd.memset(vpad[:], 0.0).then_inc(gp_init, 1)
            pool.wait_ge(gp_init, 5)
            for pp in range(2):
                nc.gpsimd.memset(vpad[:, :, pp, :, :, 16 * pp + HD:16 * pp + HD + 1], 1.0).then_inc(gp_init, 1)
            nc.gpsimd.memset(bias_k[:, 0:1], 0.0).then_inc(gp_init, 1)
            nc.gpsimd.memset(bias_q[:, 0:1], 0.0).then_inc(gp_init, 1)
            nc.gpsimd.memset(bias_v[:, 0, :], 0.0).then_inc(gp_init, 1)

        GP_INIT = 10

        def ones_rows(c):
            nc.vector.memset(stack[MROW:P, c, :, 0:NK].bitcast(F32), TWO_ONES).then_inc(ones_done, 1)

        def late_gpsimd(pool):
            nc.gpsimd.memset(ones[:], 1.0).then_inc(late_init, 1)
            nc.gpsimd.iota(i_rev[:], pattern=[[-1, E]], base=E, channel_multiplier=0).then_inc(late_init, 1)
            nc.gpsimd.iota(i_slot[:], pattern=[[1, SLOTS]], base=0, channel_multiplier=0).then_inc(late_init, 1)
            nc.gpsimd.iota(i_full[:], pattern=[[P, TT]], base=0, channel_multiplier=0).then_inc(late_init, 1)
            nc.gpsimd.memset(carry[:], 1.0).then_inc(const_step, 1)
            pool.wait_ge(late_init, 4)
            nc.gpsimd.tensor_copy(rev[:], i_rev[:]).then_inc(late_init, 1)
            nc.gpsimd.tensor_copy(slot_no[:], i_slot[:]).then_inc(late_init, 1)
            nc.gpsimd.tensor_copy(full_rows[:], i_full[:]).then_inc(late_init, 1)
            pool.wait_ge(const_step, 1)
            for e in range(E):
                nc.gpsimd.memset(carry[:, e, 0:1], 0.0).then_inc(late_init, 1)
            nc.gpsimd.affine_select(out=tri[:], in_=ones[:], compare_op=ALU.is_gt, fill=0.0, base=0,
                                    pattern=[[1, P]], channel_multiplier=-1).then_inc(const_step, 1)
            nc.gpsimd.memset(zero_row[:], 0.0).then_inc(const_step, 1)

        def start_vector(dve):
            for c in range(2):
                nc.vector.memset(zero_view(c), 0.0).then_inc(zero_done, 1)
            dve.wait_ge(zero_done, 4)
            for c in range(2):
                ones_rows(c)
            dve.wait_ge(w_in, 16 * W_DMAS)
            for n in range(2):
                for f in range(2):
                    r = slice(f * 64, f * 64 + 64)
                    nc.vector.tensor_copy(raw_perm[:, n, r].rearrange("p (i q d) -> p q i d", i=4, q=2),
                                          raw[:, WO[n], r].rearrange("p (q i d) -> p q i d", q=2, i=4)
                                          ).then_inc(raw_perm_ready, 1)
            nc.vector.tensor_tensor(lam_d[:], lam_in[:, 0, :], lam_in[:, 1, :], ALU.subtract).then_inc(lam_step, 1)
            dve.wait_ge(lam_step, 1)
            for f in range(2):
                nc.vector.tensor_scalar(lam[:, f * 8:f * 8 + 8].rearrange("p (i q) -> p q i", i=4),
                                        lam_d[:, f * 8:f * 8 + 8].rearrange("p (q i) -> p q i", q=2),
                                        LAMBDA_INIT, None, ALU.add).then_inc(lam_step, 1)
            for i in range(10):
                dve.wait_ge(wt_ready, i // 2 + 1)
                src = ps[:, i // 2 % 4, (i % 2) * D:(i % 2) * D + D]
                if i in WQ[0] + WK[0] + WQ[1][:1] + WK[1][:1]:
                    ins = nc.vector.tensor_copy(w_all[:, i, :].rearrange("p (f d h) -> p f d h", f=2, d=HD),
                                                heads_last(src))
                elif i == WO[0]:
                    ins = nc.vector.tensor_scalar(w_all[:, i, :], src, norm_col[:, 0:1], None, ALU.mult)
                else:
                    ins = nc.vector.tensor_copy(w_all[:, i, :], src)
                ins.then_inc(wt_taken, 1)

        def start_tensor(pe):
            pe.wait_ge(gp_init, GP_INIT)
            pe.wait_ge(w_in, 16 * W_DMAS)
            pe.wait_ge(raw_perm_ready, 4)
            for i in range(10):
                src = raw_perm[:, WO.index(i), :] if i in WO else raw[:, i, :]
                if i == 8:
                    pe.wait_ge(wt_taken, 2)
                ins = nc.tensor.transpose(ps[:, i // 2 % 4, (i % 2) * D:(i % 2) * D + D], src, ident[:])
                if i % 2:
                    ins.then_inc(wt_ready, 1)
            pe.wait_ge(wt_taken, 10)
            pe.wait_ge(zero_done, 4)

        def apart(eng):
            eng.sem_inc(carrier, 1)

        GATHER_AT = {0: [0], W_Q + 2: [1, 2], W_V: [3], 21: [4], 26: [5], 28: [6], 30: [7]}
        MIX_AT = {1: [0], 17: [1], 21: [2, 3], 27: [4], 29: [5], 31: [6]}

        def gather(pool, n, b):
            for t in range(QT * b, QT * b + QT):
                for k in range(2):
                    nc.gpsimd.indirect_dma_start(
                        out=y_all[:, 2 * t + k, :], out_offset=None, in_=rows_out,
                        in_offset=bass.IndirectOffsetOnAxis(ap=position[:, k, t:t + 1], axis=0)
                    ).then_inc(Z[n]["gathered"][b], 16)

        def mix(dve, n, b):
            dve.wait_ge(Z[n]["gathered"][b], 16 * 2 * QT)
            for e in range(2):
                if e:
                    dve.wait_ge(Z[n]["mixed"], 4 * b + 2)
                for t in range(QT * b, QT * b + QT):
                    nc.vector.scalar_tensor_tensor(out=x_all[:, t, :], in0=y_all[:, 2 * t + e, :],
                                                   scalar=share[:, e, t:t + 1], in1=x_all[:, t, :],
                                                   op0=ALU.mult, op1=ALU.add).then_inc(Z[n]["mixed"], 1)

        def att_sync(sp, layer):
            n, z = layer.n, S[layer.n]
            cs = a["ctx_1024"].rearrange("b (t p) c -> p b t c", p=P)

            def emit(blk):
                at, live, some = blk.at, blk.live, blk.some
                for s in range(PAIR):
                    w = s % UNIT
                    v = lambda j: 2 * j + s // UNIT + 2
                    lead = layer.leads(s // UNIT)
                    first = n == 0 and blk.j == -1 and s == 0
                    if w == W_LOAD and lead and live(v, layer.units) and not first:
                        b = lambda j: layer.lead_no(v(j))
                        if some(b, 1):
                            prev = lambda j: v(j) - (2 if layer.diff else 1)
                            sp.wait_ge(z["job_ready"], at(lambda j: layer.order[("ct", prev(j))] + 1))
                        sp.dma_start(ctx_sb[:], cs[:, bass.ds(at(b), 1), :, :].rearrange("p b t c -> p (b t) c")
                                     ).then_inc(z["ctx_in"], 16)
                    for c_half, w_key, w_query in ((0, 8, 9), (1, 0, 0)):
                        for group, w_g in (("key", w_key), ("query", w_query)):
                            if w != w_g:
                                continue
                            u = v if c_half == 0 else (lambda j: 2 * j + s // UNIT + 1)
                            if not live(u, layer.units):
                                continue
                            c = lambda j: 2 * u(j) + c_half
                            par = (s // UNIT + (0 if c_half == 0 else 1)) % 2
                            slot = 2 * par + c_half
                            sp.wait_ge(z["split_step"], at(lambda j: 4 * u(j) + (2 if group == "key" else 4)))
                            apart(sp)
                            if group == "key" and some(c, 4):
                                sp.wait_ge(z["qk_done"], at(lambda j: 8 * (c(j) - 3)))
                            for t, (qp, kp) in enumerate(TERMS):
                                src = parts[64 * c_half:64 * c_half + 64, par]
                                dst = stack[8 * t:8 * t + 8, slot]
                                if group == "key" and qp != kp:
                                    sp.dma_start(dst[:, :, 0:NK], src[:, kp, 0:NK]).then_inc(z["stack_in"][slot], 16)
                                if group == "query" and qp == kp:
                                    sp.dma_start(dst[:, :, :], src[:, kp, :]).then_inc(z["stack_in"][slot], 16)
                                if group == "query" and qp != kp:
                                    sp.dma_start(dst[:, :, NK:KQ], src[:, qp, NK:KQ]).then_inc(z["stack_in"][slot], 16)
                    for name, u, no in blk.jobs(s):
                        if name == "mt":
                            slot = (s + M_T) // 8 % 4
                            sp.wait_ge(z["job_taken"], at(lambda j: no(j) + 1))
                            sp.dma_start(stack[MROW:MROW + 3, slot, :, NK:KQ], max_rows[:, slot % 2, :]
                                         ).then_inc(z["mrow_in"][slot % 2], 16)
            run_blocks(sp, layer, emit)

        def att_tensor(pe, layer):
            n, z = layer.n, S[layer.n]

            def job(blk, s, name, u, no):
                at = blk.at
                if name != "first":
                    if blk.some(no, 1):
                        pe.wait_ge(z["job_taken"], at(no))
                if name == "ct":
                    pe.wait_ge(z["ctx_in"], at(lambda j: 16 * (layer.lead_no(u(j)) + 1)))
                    for t in range(KT):
                        ins = nc.tensor.transpose(misc[:, t * P:(t + 1) * P], ctx_sb[:, t, :], ident[:])
                elif name == "k":
                    ins = nc.tensor.matmul(misc, w_all[:, WK[n][s // UNIT], :], ctxT[:], start=True, stop=True)
                elif name == "xt":
                    pe.wait_ge(z["xn_ready"], at(lambda j: 2 * (layer.lead_no(u(j)) + 1)))
                    for t in range(QT):
                        ins = nc.tensor.transpose(misc[:, t * P:(t + 1) * P], xn[:, t, :], ident[:])
                elif name == "q":
                    ins = nc.tensor.matmul(misc[:, 0:NQ], w_all[:, WQ[n][s // UNIT], :], xnT[:], start=True, stop=True)
                elif name == "v":
                    for t in range(KT):
                        ins = nc.tensor.matmul(misc[:, t * P:(t + 1) * P], ctxT[:, t * P:(t + 1) * P],
                                               w_all[:, WV[n], :], start=True, stop=True)
                elif name == "mt":
                    pe.wait_ge(z["mp_step"], at(lambda j: 4 * (u(j) + 1)))
                    for t in range(QT):
                        src = max_parts[:, (s + M_T) // 8 % 2, t].rearrange("p a h -> p (a h)")
                        ins = nc.tensor.transpose(misc_bf[0:3 * HH, t * P:(t + 1) * P], src, identb[:])
                elif name == "ot":
                    pe.wait_ge(z["o_taken"], at(lambda j: u(j) + 1))
                    for t in range(QT):
                        for f in range(2):
                            ins = nc.tensor.transpose(misc[:, (2 * t + f) * P:(2 * t + f + 1) * P],
                                                      outT[:, f, t * P:(t + 1) * P], ident[:])
                elif name == "on":
                    if layer.diff:
                        pe.wait_ge(z["on_ready"], at(lambda j: QT * (layer.lead_no(u(j)) + 1)))
                    for t in range(QT):
                        ins = nc.tensor.transpose(misc[:, t * P:(t + 1) * P], o_norm[:, t, :], ident[:])
                elif name == "proj":
                    for t in range(QT):
                        ins = nc.tensor.matmul(misc[:, t * P:(t + 1) * P], onT[:, t * P:(t + 1) * P],
                                               w_all[:, WO[n], :], start=True, stop=True)
                ins.then_inc(z["job_ready"], 1)

            def emit(blk):
                at, live, some = blk.at, blk.live, blk.some
                for s in range(PAIR):
                    for name, u, no in blk.jobs(s):
                        job(blk, s, name, u, no)
                    g = lambda j: PAIR * j + s
                    if live(g, layer.steps):
                        slot, pp, kt = s // 8, s // 4 % 2, s % 4
                        if s % 8 == 0:
                            pe.wait_ge(z["mrow_in"][slot % 2], at(lambda j: 16 * (2 * j + slot // 2 + 1)))
                        if n == 0 and blk.j == 0 and s in (0, UNIT):
                            pe.wait_ge(ones_done, 2 if s == 0 else 4)
                        if some(g, 2):
                            pe.wait_ge(z["exp_done"], at(lambda j: g(j) - 1))
                        for i in range(4):
                            ins = nc.tensor.matmul(score[s % 2][:, i, :],
                                                   stack[:, slot, 4 * pp + i, kt * P:(kt + 1) * P],
                                                   stack[:, slot, 4 * pp + i, NK:KQ], start=True, stop=True)
                        ins.then_inc(z["qk_done"], 1)
                    gm = lambda j: PAIR * j + s + UNIT
                    if live(gm, layer.steps):
                        slot = (s + UNIT) // 8 % 4
                        if s % 8 == 0:
                            cyc = lambda j: j + (s + UNIT) // PAIR
                            pe.wait_ge(z["stack_in"][slot], at(lambda j: 16 * STACK_DMAS * (cyc(j) + 1)))
                        for t in range(QT):
                            if some(gm, 1):
                                pe.wait_ge(z["mx_taken"], at(lambda j: 2 * gm(j) + t - 1))
                            nc.tensor.matmul(maxs[t], stack[0:MROW, slot, s % 8, NK + t * P:NK + (t + 1) * P],
                                             stack[0:MROW, slot, s % 8, 0:NK], start=True, stop=True
                                             ).then_inc(z["mx_ready"], 1)
                    gp = lambda j: PAIR * j + s - 2
                    if live(gp, layer.steps):
                        sp_ = (s - 2) % PAIR
                        f, pp, kt = sp_ // 8 % 2, sp_ // 4 % 2, sp_ % 4
                        if sp_ % UNIT == 0 and some(gp, 1):
                            pe.wait_ge(z["o_taken"], at(lambda j: gp(j) // UNIT))
                        if sp_ % 8 == 0 and layer.leads(sp_ // UNIT):
                            pe.wait_ge(z["vpad_ready"], at(lambda j: 4 * layer.lead_no(gp(j) // UNIT) + 2 * f + 2))
                        pe.wait_ge(z["exp_done"], at(lambda j: gp(j) + 1))
                        for i in range(4):
                            ins = nc.tensor.matmul(oacc[32 * i:32 * i + 32, f, :], vpad[:, f, pp, kt, i, :],
                                                   probs[:, sp_ % 4, i, :], start=(sp_ % UNIT == 0),
                                                   stop=(sp_ % 8 == 7), skip_group_check=True)
                        ins.then_inc(z["pv_done"], 1)
            run_blocks(pe, layer, emit)

        def att_scalar(act, layer):
            n, z = layer.n, S[layer.n]

            def emit(blk):
                at, live, some = blk.at, blk.live, blk.some
                for s in range(PAIR):
                    for name, u, no in blk.jobs(s):
                        if name in ("v", "ot", "proj"):
                            continue
                        act.wait_ge(z["job_ready"], at(lambda j: no(j) + 1))
                        par = s // UNIT
                        if name == "ct":
                            nc.scalar.copy(ctxT[:], misc).then_inc(z["job_taken"], 1)
                        elif name == "xt":
                            nc.scalar.copy(xnT[:], misc[:, 0:NQ]).then_inc(z["job_taken"], 1)
                        elif name == "on":
                            nc.scalar.copy(onT[:], misc[:, 0:NQ]).then_inc(z["job_taken"], 1)
                        elif name == "mt":
                            q = (s + M_T) // 8 % 2
                            if some(u, 2):
                                act.wait_ge(z["mrow_in"][q], at(lambda j: 16 * (u(j) // 2)))
                            nc.scalar.copy(max_rows[:, q, :], misc_bf[0:3 * HH, 0:NQ]).then_inc(z["job_taken"], 1)
                        else:
                            cols, bias = ((slice(0, NK), bias_k) if name == "k" else (slice(NK, KQ), bias_q))
                            if some(u, 2):
                                for slot in (2 * par, 2 * par + 1):
                                    act.wait_ge(z["stack_in"][slot], at(lambda j: 16 * STACK_DMAS * (u(j) // 2)))
                            nc.scalar.activation(parts[:, par, 0, cols], misc[:, 0:cols.stop - cols.start],
                                                 ACT.Identity, bias=bias[:, n:n + 1]).then_inc(z["a1_done"], 1)
                    uo = lambda j: 2 * j + (s - P_O) // UNIT
                    if (s - P_O) % UNIT == 0 and live(uo, layer.units):
                        act.wait_ge(z["pv_done"], at(lambda j: UNIT * (uo(j) + 1)))
                        if some(uo, 1):
                            act.wait_ge(z["job_ready"], at(lambda j: layer.order[("ot", uo(j) - 1)] + 1))
                        nc.scalar.copy(outT[:], oacc).then_inc(z["o_taken"], 1)
                    g = lambda j: PAIR * j + s
                    if live(g, layer.steps):
                        act.wait_ge(z["qk_done"], at(lambda j: g(j) + 1))
                        if some(g, 4):
                            act.wait_ge(z["pv_done"], at(lambda j: g(j) - 3))
                        elif n == 1:
                            act.wait_ge(Z[0]["mixed"], 8 * (s + 1))
                        nc.scalar.activation(probs[:, s % 4], score[s % 2], ACT.Exp, scale=SCALE
                                             ).then_inc(z["exp_done"], 1)
            run_blocks(act, layer, emit)

        def att_vector(dve, layer):
            n, z = layer.n, S[layer.n]

            def emit(blk):
                at, live, some = blk.at, blk.live, blk.some
                for s in range(PAIR):
                    if n == 1 and blk.j == -1:
                        for b in MIX_AT.get(s, ()):
                            mix(dve, 0, b)
                    if n == 1 and blk.j == 0 and s == 0:
                        mix(dve, 0, B - 1)
                    w, par = s % UNIT, s // UNIT
                    if n == 0 and blk.j == -1 and s in (W_V + 1, W_V + 2):
                        ones_rows(s - W_V + 1)
                    gm = lambda j: PAIR * j + s + UNIT
                    if live(gm, layer.steps):
                        c2 = s // 8 % 2
                        for t in range(QT):
                            dve.wait_ge(z["mx_ready"], at(lambda j: 2 * gm(j) + t + 1))
                            if s % 8 == 0 and t == 0 and some(lambda j: gm(j) // 8, 2):
                                dve.wait_ge(z["mp_step"], at(lambda j: 4 * (gm(j) // 8 - 1)))
                            nc.vector.tensor_reduce(row_max[:, c2, t, s % 8:s % 8 + 1], maxs[t], axis=AX.X,
                                                    op=ALU.max, negate=True).then_inc(z["mx_taken"], 1)
                    for name, u, no in blk.jobs(s):
                        if name in ("k", "q"):
                            cols, bias, rest = ((slice(0, NK), bias_k, rest_k) if name == "k"
                                                else (slice(NK, KQ), bias_q, rest_q))
                            k = 1 if name == "k" else 2
                            dve.wait_ge(z["a1_done"], at(lambda j: 2 * u(j) + k))
                            if some(u, 1):
                                dve.wait_ge(z["split_step"], at(lambda j: 4 * (u(j) - 1) + 2 * k))
                            nc.vector.scalar_tensor_tensor(
                                out=rest[:], in0=misc[:, 0:cols.stop - cols.start], scalar=bias[:, n:n + 1],
                                in1=parts[:, par, 0, cols], op0=ALU.add, op1=ALU.subtract
                            ).then_inc(z["job_taken"], 1)
                        elif name == "v":
                            dve.wait_ge(z["job_ready"], at(lambda j: no(j) + 1))
                            if some(u, 2):
                                dve.wait_ge(z["vpad_ready"], at(lambda j: 4 * (layer.lead_no(u(j) - 2) + 1)))
                            nc.vector.tensor_tensor(vals[:, par], misc.rearrange("p (t c) -> p t c", t=KT),
                                                    bias_v[:, n:n + 1, :].broadcast_to([P, KT, D]), ALU.add
                                                    ).then_inc(z["job_taken"], 1)
                        elif name == "ot":
                            second = layer.diff and layer.ends((s - P_OT) // UNIT)
                            got = misc.rearrange("p (m c) -> p m c", c=16)
                            den = got[:, :, HD:HD + 1].rearrange("p (t m) c -> p t (m c)", t=QT)
                            rd = r_den[:].rearrange("p t m -> p (t m)")
                            dve.wait_ge(z["job_ready"], at(lambda j: no(j) + 1))
                            base = (lambda j: 4 * (u(j) // 2) + (u(j) % 2)) if layer.diff else (lambda j: u(j))
                            nc.vector.reciprocal(r_den[:], den).then_inc(z["den_step"], 1)
                            dve.wait_ge(z["den_step"], at(lambda j: base(j) + 1))
                            if second:
                                nc.vector.tensor_tensor(r_den[:], r_den[:],
                                                        lam[:].rearrange("p (o m) -> p o m", o=1).broadcast_to([P, QT, H]),
                                                        ALU.mult).then_inc(z["den_step"], 1)
                                dve.wait_ge(z["den_step"], at(lambda j: base(j) + 2))
                            dst = o_first if layer.diff and not second else o_second
                            if not layer.diff:
                                dst = o_norm[:].rearrange("p t (m d) -> p (t m) d", d=HD)
                                if some(u, 1):
                                    dve.wait_ge(z["job_ready"], at(lambda j: layer.order[("on", u(j) - 1)] + 1))
                            else:
                                dst = dst[:]
                            ins = nc.vector.tensor_tensor(dst, got[:, :, 0:HD],
                                                          rd.rearrange("p (m o) -> p m o", o=1).broadcast_to([P, QT * H, HD]),
                                                          ALU.mult)
                            ins.then_inc(z["job_taken"], 1)
                        elif name == "proj":
                            b = (lambda j: u(j) // 2) if layer.diff else u
                            dve.wait_ge(z["job_ready"], at(lambda j: no(j) + 1))
                            dve.wait_ge(z["res_ready"], at(lambda j: b(j) + 1))
                            rows = x_all[:, bass.ds(at(lambda j: QT * b(j)), QT), :]
                            nc.vector.tensor_tensor(rows, misc[:, 0:NQ].rearrange("p (t c) -> p t c", t=QT), rows, ALU.add
                                                    ).then_inc(z["job_taken"], 1)
                    v = lambda j: 2 * j + s // UNIT + 2
                    if w in (2, 4) and layer.leads(par) and live(v, layer.units):
                        b = lambda j: layer.lead_no(v(j))
                        row = lambda b, t: x_all[:, bass.ds(at(lambda j: QT * b(j) + t), 1), :].rearrange("p t c -> p (t c)")
                        if w == 2:
                            if n == 0:
                                dve.wait_ge(x_start, 32 if some(b, 1) else 16)
                            else:
                                dve.wait_ge(Z[0]["mixed"], at(lambda j: 4 * (b(j) + 1)))
                            for t in range(QT):
                                nc.vector.bn_stats(x_stat[:, t, :], row(b, t)).then_inc(z["ln_step"], 1)
                            dve.wait_ge(z["ln_step"], at(lambda j: 4 * b(j) + 2))
                            if some(b, 1):
                                dve.wait_ge(z["rstd_step"], at(lambda j: 2 * b(j)))
                            for t in range(QT):
                                apart(dve)
                                nc.vector.bn_aggr(x_mv[:, t, :], x_stat[:, t, :]).then_inc(z["ln_step"], 1)
                        else:
                            dve.wait_ge(z["rstd_step"], at(lambda j: 2 * b(j) + 2))
                            if some(b, 1):
                                prev = lambda j: v(j) - (2 if layer.diff else 1)
                                dve.wait_ge(z["job_ready"], at(lambda j: layer.order[("xt", prev(j))] + 1))
                            for t in range(QT):
                                nc.vector.tensor_scalar(xn[:, t, :], row(b, t), x_mv[:, t, 0:1],
                                                        x_rstd[:, t:t + 1], ALU.subtract, ALU.mult
                                                        ).then_inc(z["xn_ready"], 1)
                    for k in (P_DIFF, P_SUMS):
                        uu = lambda j, k=k: 2 * j + (s - k) // UNIT
                        if (s - k) % UNIT or not layer.diff or not layer.ends((s - k) // UNIT) or not live(uu, layer.units):
                            continue
                        if k == P_DIFF:
                            dve.wait_ge(z["job_taken"], at(lambda j: layer.order[("ot", uu(j))] + 1))
                            if some(uu, 2):
                                dve.wait_ge(z["on_ready"], at(lambda j: QT * (uu(j) // 2)))
                            nc.vector.tensor_tensor(o_diff[:].rearrange("p t (m d) -> p (t m) d", d=HD),
                                                    o_first[:], o_second[:], ALU.subtract).then_inc(z["den_step"], 1)
                        else:
                            dve.wait_ge(z["den_step"], at(lambda j: 4 * (uu(j) // 2) + 4))
                            if some(uu, 2):
                                dve.wait_ge(z["rr_step"], at(lambda j: 2 * (uu(j) // 2)))
                            for t in range(QT):
                                if t or some(uu, 2):
                                    dve.wait_ge(z["ss_step"], at(lambda j: 2 * (uu(j) // 2) + t))
                                nc.vector.tensor_tensor_reduce(out=o_sq[:], in0=o_diff[:, t, :], in1=o_diff[:, t, :],
                                                               scale=1.0, scalar=0.0, op0=ALU.mult, op1=ALU.add,
                                                               accum_out=o_ss[:, t:t + 1]).then_inc(z["ss_step"], 1)
                    if (s - P_NORM) % UNIT == 0 and layer.diff and layer.ends((s - P_NORM) // UNIT):
                        uu = lambda j: 2 * j + (s - P_NORM) // UNIT
                        if live(uu, layer.units):
                            bb = lambda j: uu(j) // 2
                            dve.wait_ge(z["rr_step"], at(lambda j: 2 * bb(j) + 2))
                            if some(bb, 1):
                                dve.wait_ge(z["job_ready"], at(lambda j: layer.order[("on", uu(j) - 2)] + 1))
                            for t in range(QT):
                                nc.vector.tensor_scalar(o_norm[:, t, :], o_diff[:, t, :], o_rr[:, t:t + 1], None,
                                                        ALU.mult).then_inc(z["on_ready"], 1)
            run_blocks(dve, layer, emit)

        def att_gpsimd(pool, layer):
            n, z = layer.n, S[layer.n]

            def emit(blk):
                at, live, some = blk.at, blk.live, blk.some
                for s in range(PAIR):
                    w, par = s % UNIT, s // UNIT
                    if n == 0 and blk.j == -1 and s == 9:
                        late_gpsimd(pool)
                    if n == 1 and blk.j == -1:
                        for b in GATHER_AT.get(s, ()):
                            gather(pool, 0, b)
                    if blk.j == 0 and s % 4 == 0:
                        load_expert(pool, n, s // 4)
                    if n == 0 and blk.j == 0 and s == PAIR - 1:
                        pool.wait_ge(const_step, 3)
                        pool.dma_start(rows_in.rearrange("(s p) c -> p s c", p=P),
                                       zero_row[:].rearrange("p (o c) -> p o c", o=1).broadcast_to([P, SLOTS, D])
                                       ).then_inc(rows_zero, 16)
                    if s % 8 == 1:
                        c = lambda j: 4 * j + (s + 7) // 8
                        q = (s + 7) // 8 % 2
                        if live(c, 2 * layer.units):
                            pool.wait_ge(z["mx_taken"], at(lambda j: 16 * (c(j) + 1)))
                            if some(c, 2):
                                pool.wait_ge(z["job_ready"], at(lambda j: layer.order[("mt", c(j) - 2)] + 1))
                            part = [max_parts[:, q, :, k, :] for k in range(3)]
                            apart(pool)
                            nc.gpsimd.tensor_copy(part[0], row_max[:, q]).then_inc(z["mp_step"], 1)
                            pool.wait_ge(z["mp_step"], at(lambda j: 4 * c(j) + 1))
                            nc.gpsimd.tensor_tensor(max_rest[:], row_max[:, q], part[0], ALU.subtract
                                                    ).then_inc(z["mp_step"], 1)
                            pool.wait_ge(z["mp_step"], at(lambda j: 4 * c(j) + 2))
                            apart(pool)
                            nc.gpsimd.tensor_copy(part[1], max_rest[:]).then_inc(z["mp_step"], 1)
                            pool.wait_ge(z["mp_step"], at(lambda j: 4 * c(j) + 3))
                            nc.gpsimd.tensor_tensor(part[2], max_rest[:], part[1], ALU.subtract
                                                    ).then_inc(z["mp_step"], 1)
                    v = lambda j: 2 * j + s // UNIT + 2
                    if w == 3 and layer.leads(par) and live(v, layer.units):
                        b = lambda j: layer.lead_no(v(j))
                        pool.wait_ge(z["ln_step"], at(lambda j: 4 * b(j) + 4))
                        if some(b, 1):
                            pool.wait_ge(z["xn_ready"], at(lambda j: 2 * b(j)))
                        var = x_mv[:, :, 1:2].rearrange("p t o -> p (t o)")
                        apart(pool)
                        nc.gpsimd.tensor_scalar(x_rstd[:], var, LN_EPS, None, ALU.add).then_inc(z["rstd_step"], 1)
                        pool.wait_ge(z["rstd_step"], at(lambda j: 2 * b(j) + 1))
                        nc.gpsimd.tensor_tensor(x_rstd[:], x_rstd[:], half_neg[:, 0:QT], ALU.pow
                                                ).then_inc(z["rstd_step"], 1)
                    for f, sc in ((0, 11), (1, 3)):
                        vu = lambda j: 2 * j + s // UNIT + (1 if f == 0 else 0)
                        if w == sc and layer.leads(s // UNIT + (1 if f == 0 else 0)) and live(vu, layer.units):
                            pool.wait_ge(z["job_taken"], at(lambda j: layer.order[("v", vu(j))] + 1))
                            if some(vu, 1):
                                pool.wait_ge(z["pv_done"], at(lambda j: UNIT * vu(j) - (8 if f == 0 else 0)))
                            vp = (s // UNIT + (1 if f == 0 else 0)) % 2
                            for pp in range(2):
                                apart(pool)
                                nc.gpsimd.tensor_copy(
                                    vpad[:, f, pp, :, :, 16 * pp:16 * pp + HD],
                                    vals[:, vp, :, 64 * f + 32 * pp:64 * f + 32 * pp + 32].rearrange("p t (i d) -> p t i d", i=4)
                                ).then_inc(z["vpad_ready"], 1)
                    if (s - P_RMS) % UNIT == 0 and layer.diff and layer.ends((s - P_RMS) // UNIT):
                        uu = lambda j: 2 * j + (s - P_RMS) // UNIT
                        if live(uu, layer.units):
                            bb = lambda j: uu(j) // 2
                            pool.wait_ge(z["ss_step"], at(lambda j: 2 * bb(j) + 2))
                            if some(bb, 1):
                                pool.wait_ge(z["on_ready"], at(lambda j: 2 * bb(j)))
                            apart(pool)
                            nc.gpsimd.tensor_scalar(o_rr[:], o_ss[:], 1.0 / D, RMS_EPS, ALU.mult, ALU.add
                                                    ).then_inc(z["rr_step"], 1)
                            pool.wait_ge(z["rr_step"], at(lambda j: 2 * bb(j) + 1))
                            nc.gpsimd.tensor_tensor(o_rr[:], o_rr[:], half_neg[:, 0:QT], ALU.pow
                                                    ).then_inc(z["rr_step"], 1)
                    for name, u, no in blk.jobs(s):
                        if name in ("k", "q"):
                            cols, rest = ((slice(0, NK), rest_k) if name == "k" else (slice(NK, KQ), rest_q))
                            k = 0 if name == "k" else 2
                            pool.wait_ge(z["job_taken"], at(lambda j: no(j) + 1))
                            apart(pool)
                            nc.gpsimd.tensor_copy(parts[:, par, 1, cols], rest[:]).then_inc(z["split_step"], 1)
                            pool.wait_ge(z["split_step"], at(lambda j: 4 * u(j) + k + 1))
                            nc.gpsimd.tensor_tensor(parts[:, par, 2, cols], rest[:], parts[:, par, 1, cols],
                                                    ALU.subtract).then_inc(z["split_step"], 1)
                        if name == "on":
                            b = (lambda j: u(j) // 2) if layer.diff else u
                            if n == 0 and blk.j is not None and blk.j <= 1:
                                pool.wait_ge(bias_in, 16)
                            pool.wait_ge(z["xn_ready"], at(lambda j: QT * (b(j) + 1)))
                            rows = x_all[:, bass.ds(at(lambda j: QT * b(j)), QT), :]
                            nc.gpsimd.tensor_tensor(rows, rows, bias_o[:, n:n + 1, :].broadcast_to([P, QT, D]), ALU.add).then_inc(z["res_ready"], 1)
            run_blocks(pool, layer, emit)

        for n in range(2):
            S[n]["ss_step"] = sem(f"ss_step{n}")

        def ffn_sems(n):
            names = ("stat_step stat_rstd xn_all xt_bank xt_copied scored expd counted route_step "
                     "placed scattered wt_done wt_copied rows_t rows_taken up_done act_done hid_done hid_t "
                     "hidT_taken down_done out_taken mixed stored").split()
            d = {k: sem(f"f_{k}{n}") for k in names}
            d["gathered"] = [sem(f"f_gathered{n}_{i}") for i in range(B)]
            d["rows_in"] = [sem(f"f_rows_in{n}_{i}") for i in range(2)]
            d["rows_out"] = [sem(f"f_rows_out{n}_{i}") for i in range(2)]
            return d

        Z = [ffn_sems(0), ffn_sems(1)]

        class Tiles:
            pairs = SLOTS // 4
            loops = 1

        up_ps = [ps[:, 0, :], ps[:, 1, :]]
        gate_ps = [ps[:, 2, :], ps[:, 3, :]]
        hidT_ps = ps[:, 4, :]
        rowsT_ps = ps[:, 5, 0:P]
        down_ps = [ps[:, 6, 0:D], ps[:, 7, 0:D]]

        def x_tiles(ap):
            return ap.rearrange("b (t p) c -> p (b t) c", p=P)

        def ffn_sync(sp, n):
            z = Z[n]
            if n == 0:
                load_biases(sp)
            sp.wait_ge(z["scattered"], 16 * 2 * TT)
            src = rows_in.rearrange("(s p) c -> p s c", p=P)

            def emit(blk):
                at, live, some = blk.at, blk.live, blk.some
                for q in range(4):
                    t = lambda j: 4 * j + q + 2
                    if live(t, SLOTS):
                        if some(t, 2):
                            sp.wait_ge(z["rows_t"], at(lambda j: t(j) - 1))
                        sp.dma_start(s_rows[:, q % 2:q % 2 + 1, :], src[:, bass.ds(at(t), 1), :]).then_inc(z["rows_in"][q % 2], 16)
            run_blocks(sp, Tiles, emit)
            if n == 0:
                sp.wait_ge(bias_in, 16 * 7)
            else:
                for b in range(0, B, 2):
                    sp.wait_ge(z["mixed"], 4 * (b + 2))
                    sp.dma_start(x_tiles(out)[:, QT * b:QT * b + 4, :], x_all[:, QT * b:QT * b + 4, :]
                                 ).then_inc(z["stored"], 16)
                sp.wait_ge(z["stored"], 16 * B // 2)

        def ffn_gpsimd(pool, n):
            z = Z[n]
            pool.wait_ge(z["stat_step"], 2 * TT)
            nc.gpsimd.tensor_scalar(t_rstd[:], t_mv[:, :, 1:2].rearrange("p t o -> p (t o)"), LN_EPS, None, ALU.add
                                    ).then_inc(z["stat_rstd"], 1)
            pool.wait_ge(z["stat_rstd"], 1)
            nc.gpsimd.tensor_tensor(t_rstd[:], t_rstd[:], half_neg[:], ALU.pow).then_inc(z["stat_rstd"], 1)
            pool.wait_ge(z["placed"], 2)
            pool.wait_ge(z["xn_all"], TT)
            pool.wait_ge(rows_zero, 16)
            for t in range(TT):
                for k in range(2):
                    nc.gpsimd.indirect_dma_start(
                        out=rows_in, out_offset=bass.IndirectOffsetOnAxis(ap=position[:, k, t:t + 1], axis=0),
                        in_=xn_all[:, t, :], in_offset=None).then_inc(z["scattered"], 16)
            dst = rows_out.rearrange("(s p) c -> p s c", p=P)

            def emit(blk):
                at, live = blk.at, blk.live
                for q in range(4):
                    t2 = lambda j: 4 * j + q - 2
                    if live(t2, SLOTS):
                        pool.wait_ge(z["out_taken"], at(lambda j: t2(j) + 1))
                        apart(pool)
                        pool.dma_start(dst[:, bass.ds(at(t2), 1), :], s_out[:, q % 2:q % 2 + 1, :]
                                       ).then_inc(z["rows_out"][q % 2], 16)
            run_blocks(pool, Tiles, emit)
            for q in range(2):
                pool.wait_ge(z["rows_out"][q], 16 * (SLOTS // 2))
            if n == 1:
                for b in range(B):
                    gather(pool, n, b)

        def ffn_scalar(act, n):
            z = Z[n]
            for k in range(TT // 4):
                act.wait_ge(z["xt_bank"], k + 1)
                nc.scalar.copy(xT_all[:, 512 * k:512 * k + 512], ps[:, k, :]).then_inc(z["xt_copied"], 1)
            act.wait_ge(z["route_step"], EXP_AT[n][0])
            if n == 0:
                nc.scalar.activation(rt_b[:], rt_a[:], ACT.Exp, scale=-1.0).then_inc(z["expd"], 1)
                act.wait_ge(z["route_step"], EXP_AT[n][1])
                nc.scalar.activation(rt_b[:], rt_a[:], ACT.Exp, scale=-1.0).then_inc(z["expd"], 1)
            else:
                nc.scalar.activation(rt_k[:], share_d[:], ACT.Exp, scale=-1.0).then_inc(z["expd"], 1)
            if n == 0:
                for k in range(3 * E):
                    act.wait_ge(z["wt_done"], k + 1)
                    nc.scalar.copy(w_exp[:, k // E, k % E, :], ps[:, 6 + k % 2, :]).then_inc(z["wt_copied"], 1)

            def emit(blk):
                at, live, some = blk.at, blk.live, blk.some
                for q in range(4):
                    t = lambda j: 4 * j + q + 1
                    if live(t, SLOTS):
                        act.wait_ge(z["rows_t"], at(lambda j: t(j) + 1))
                        if some(t, 2):
                            act.wait_ge(z["up_done"], at(lambda j: t(j) - 1))
                        nc.scalar.copy(s_rowsT[:, (q + 1) % 2, :], rowsT_ps).then_inc(z["rows_taken"], 1)
                    t1 = lambda j: 4 * j + q - 1
                    if live(t1, SLOTS):
                        act.wait_ge(z["hid_t"], at(lambda j: t1(j) + 1))
                        if some(t1, 2):
                            act.wait_ge(z["down_done"], at(lambda j: t1(j) - 1))
                        nc.scalar.copy(s_hidT[:, (q + 1) % 2, :], hidT_ps).then_inc(z["hidT_taken"], 1)
                    t0 = lambda j: 4 * j + q
                    if live(t0, SLOTS):
                        act.wait_ge(z["up_done"], at(lambda j: t0(j) + 1))
                        if some(t0, 2):
                            act.wait_ge(z["hid_done"], at(lambda j: t0(j) - 1))
                        nc.scalar.activation(s_act[:, q % 2, :], up_ps[q % 2], ACT.Silu).then_inc(z["act_done"], 1)
            run_blocks(act, Tiles, emit)

        def ffn_tensor(pe, n):
            z = Z[n]
            pe.wait_ge(w_exp_in, 16 * W_EXP_DMAS[n])
            if n == 0:
                nc.tensor.transpose(ps[:, 7, 0:E], gate_raw[:], ident[0:E, 0:E]).then_inc(z["counted"], 1)
            for k in range(TT // 4):
                pe.wait_ge(z["xn_all"], 4 * k + 4)
                for i in range(4):
                    ins = nc.tensor.transpose(ps[:, k, i * P:(i + 1) * P], xn_all[:, 4 * k + i, :], ident[:])
                ins.then_inc(z["xt_bank"], 1)
            if n == 0:
                pe.wait_ge(gate_ready, 1)
            for k in range(TT // 4):
                pe.wait_ge(z["xt_copied"], k + 1)
                for i in range(4):
                    t = 4 * k + i
                    ins = nc.tensor.matmul(ps[:, 4, t * E:(t + 1) * E], xT_all[:, t * P:(t + 1) * P], w_gate[:, n, :],
                                           start=True, stop=True)
            ins.then_inc(z["scored"], 1)
            pe.wait_ge(const_step, 3)
            pe.wait_ge(z["route_step"], PICK_AT[n])
            flat = picked[:].rearrange("p t e -> p (t e)")
            nc.tensor.matmul(ps[:, 5, 0:P], tri[:], flat, start=True, stop=True)
            nc.tensor.matmul(ps[:, 5, P:2 * P], ones[:], flat, start=True, stop=True).then_inc(z["counted"], 1)
            if n == 0:
                for k in range(3 * E):
                    if k >= 2:
                        pe.wait_ge(z["wt_copied"], k - 1)
                    for c in range(FC):
                        ins = nc.tensor.transpose(ps[:, 6 + k % 2, c * P:(c + 1) * P],
                                                  w_exp[:, k // E, k % E, c * P:(c + 1) * P], ident[:])
                    ins.then_inc(z["wt_done"], 1)
                pe.wait_ge(z["wt_copied"], 3 * E)
            pe.wait_ge(z["placed"], 2)

            def emit(blk):
                at, live, some = blk.at, blk.live, blk.some
                for q in range(4):
                    t = lambda j: 4 * j + q + 1
                    if live(t, SLOTS):
                        cyc = lambda j: t(j) // 2 + 1
                        pe.wait_ge(z["rows_in"][(q + 1) % 2], at(lambda j: 16 * cyc(j)))
                        if some(t, 1):
                            pe.wait_ge(z["rows_taken"], at(t))
                        nc.tensor.transpose(rowsT_ps, s_rows[:, (q + 1) % 2, :], ident[:]).then_inc(z["rows_t"], 1)
                    t0 = lambda j: 4 * j + q
                    if live(t0, SLOTS):
                        e = pe.value_load(expert_of[0:1, bass.ds(at(t0), 1)], min_val=0, max_val=E - 1)
                        pe.wait_ge(z["rows_taken"], at(lambda j: t0(j) + 1))
                        if some(t0, 2):
                            pe.wait_ge(z["act_done"], at(lambda j: t0(j) - 1))
                            pe.wait_ge(z["hid_done"], at(lambda j: t0(j) - 1))
                        for k, dst in ((0, up_ps[q % 2]), (1, gate_ps[q % 2])):
                            ins = nc.tensor.matmul(dst, s_rowsT[:, q % 2, :],
                                                   w_exp[:, k, bass.ds(e, 1), :].rearrange("p e f -> p (e f)"),
                                                   start=True, stop=True)
                        ins.then_inc(z["up_done"], 1)
                    t1 = lambda j: 4 * j + q - 1
                    if live(t1, SLOTS):
                        pe.wait_ge(z["hid_done"], at(lambda j: t1(j) + 1))
                        if some(t1, 1):
                            pe.wait_ge(z["hidT_taken"], at(t1))
                        for c in range(FC):
                            ins = nc.tensor.transpose(hidT_ps[:, c * P:(c + 1) * P],
                                                      s_hid[:, (q + 1) % 2, c * P:(c + 1) * P], ident[:])
                        ins.then_inc(z["hid_t"], 1)
                    t2 = lambda j: 4 * j + q - 2
                    if live(t2, SLOTS):
                        e = pe.value_load(expert_of[0:1, bass.ds(at(t2), 1)], min_val=0, max_val=E - 1)
                        pe.wait_ge(z["hidT_taken"], at(lambda j: t2(j) + 1))
                        if some(t2, 2):
                            pe.wait_ge(z["out_taken"], at(lambda j: t2(j) - 1))
                        for c in range(FC):
                            ins = nc.tensor.matmul(down_ps[q % 2], s_hidT[:, q % 2, c * P:(c + 1) * P],
                                                   w_exp[:, 2, bass.ds(e, 1), c * P:(c + 1) * P
                                                         ].rearrange("p e f -> p (e f)"),
                                                   start=(c == 0), stop=(c == FC - 1))
                        ins.then_inc(z["down_done"], 1)
            run_blocks(pe, Tiles, emit)

        EXP_AT, PICK_AT = [[None, None], [None]], [None, None]

        def route(dve, n, dry=False):
            z = Z[n]
            count = [0]

            def step(make):
                count[0] += 1
                if not dry:
                    make().then_inc(z["route_step"], 1)
                    dve.wait_ge(z["route_step"], count[0])

            V = nc.vector
            by_token = lambda ap: ap.rearrange("p (t o) -> p t o", o=1).broadcast_to([P, TT, E])
            by_expert = lambda ap: ap.rearrange("p (o e) -> p o e", o=1).broadcast_to([P, TT, E])
            if not dry:
                dve.wait_ge(z["scored"], 1)
            step(lambda: V.tensor_copy(gate_s[:].rearrange("p t e -> p (t e)"), ps[:, 4, 0:TT * E]))
            for k, src in ((0, gate_s), (1, gate_s2)):
                step(lambda: V.tensor_reduce(top[:, k, :], src[:], axis=AX.X, op=ALU.max))
                step(lambda: V.tensor_tensor(rt_a[:], src[:], by_token(top[:, k, :]), ALU.is_equal))
                step(lambda: V.tensor_tensor(rt_a[:], rt_a[:], by_expert(rev[:]), ALU.mult))
                step(lambda: V.tensor_reduce(rt_k[:], rt_a[:], axis=AX.X, op=ALU.max))
                step(lambda: V.tensor_tensor(hot[:, k], by_expert(rev[:]), by_token(rt_k[:]), ALU.is_equal))
                if k == 0:
                    step(lambda: V.scalar_tensor_tensor(out=gate_s2[:], in0=hot[:, 0], scalar=-BIG, in1=gate_s[:],
                                                        op0=ALU.mult, op1=ALU.add))
            step(lambda: V.tensor_tensor(picked[:], hot[:, 0], hot[:, 1], ALU.add))
            PICK_AT[n] = count[0]
            if not dry:
                dve.wait_ge(z["counted"], 2 if n == 0 else 1)
            step(lambda: V.tensor_copy(total[:], ps[:, 5, P:2 * P].rearrange("p (t e) -> p e t", e=E)))
            step(lambda: V.tensor_tensor_scan(upto[:].rearrange("p e t -> p (e t)"), carry[:].rearrange("p e t -> p (e t)"),
                                              total[:].rearrange("p e t -> p (e t)"), 0.0, ALU.mult, ALU.add))
            step(lambda: V.tensor_tensor(more[:], upto[:, :, TT - 1:TT].broadcast_to([P, E, TT]),
                                         full_rows[:].rearrange("p (o t) -> p o t", o=1).broadcast_to([P, E, TT]),
                                         ALU.is_gt))
            step(lambda: V.tensor_reduce(n_tiles[:], more[:], axis=AX.X, op=ALU.add))
            step(lambda: V.tensor_tensor_scan(tile_end[:], carry[:, 0:1, 1:1 + E].rearrange("p o t -> p (o t)"),
                                              n_tiles[:], 0.0, ALU.mult, ALU.add))
            step(lambda: V.tensor_tensor(tile_at[:], tile_end[:], n_tiles[:], ALU.subtract))
            step(lambda: V.tensor_tensor(done_e[:], tile_end[:].rearrange("p (o e) -> p o e", o=1).broadcast_to([P, SLOTS, E]),
                                         slot_no[:].rearrange("p (s o) -> p s o", o=1).broadcast_to([P, SLOTS, E]),
                                         ALU.is_le))
            step(lambda: V.tensor_reduce(tile_e[:], done_e[:], axis=AX.X, op=ALU.add))
            if not dry:
                V.tensor_scalar(expert_of[:], tile_e[:], float(E - 1), None, ALU.min).then_inc(z["placed"], 1)
            step(lambda: V.tensor_tensor(upto[:], upto[:], total[:], ALU.subtract))
            step(lambda: V.tensor_tensor(place[:], ps[:, 5, 0:P].rearrange("p (t e) -> p t e", e=E),
                                         upto[:].rearrange("p e t -> p t e"), ALU.add))
            step(lambda: V.scalar_tensor_tensor(out=place[:], in0=by_expert(tile_at[:]), scalar=float(P), in1=place[:],
                                                op0=ALU.mult, op1=ALU.add))
            step(lambda: V.tensor_tensor(hot[:], hot[:], place[:].rearrange("p (o t) e -> p o t e", o=1
                                                                          ).broadcast_to([P, 2, TT, E]), ALU.mult))
            step(lambda: V.tensor_reduce(place_f[:], hot[:], axis=AX.X, op=ALU.add))
            if not dry:
                V.tensor_copy(position[:], place_f[:]).then_inc(z["placed"], 1)
            if n == 0:
                step(lambda: V.scalar_tensor_tensor(out=gate_abs[:], in0=gate_s[:], scalar=-1.0, in1=gate_s[:],
                                                    op0=ALU.mult, op1=ALU.max))
                for k, src in ((0, gate_s), (1, gate_s2)):
                    step(lambda: V.tensor_tensor(rt_a[:], by_token(top[:, k, :]), src[:], ALU.subtract))
                    EXP_AT[0][k] = count[0]
                    step(lambda: V.tensor_tensor(place[:], gate_abs[:], by_token(top[:, k, :]), ALU.max))
                    step(lambda: V.scalar_tensor_tensor(out=place[:], in0=place[:], scalar=0.02, in1=rt_a[:],
                                                        op0=ALU.mult, op1=ALU.is_ge))
                    if not dry:
                        dve.wait_ge(z["expd"], k + 1)
                    step(lambda: V.tensor_tensor(place[:], place[:], rt_b[:], ALU.mult))
                    step(lambda: V.tensor_reduce(share_d[:], place[:], axis=AX.X, op=ALU.add))
                    step(lambda: V.reciprocal(share[:, k, :], share_d[:]))
            else:
                step(lambda: V.tensor_tensor(share_d[:], top[:, 0, :], top[:, 1, :], ALU.subtract))
                EXP_AT[1][0] = count[0]
                if not dry:
                    dve.wait_ge(z["expd"], 1)
                step(lambda: V.tensor_scalar(share_d[:], rt_k[:], 1.0, None, ALU.add))
                step(lambda: V.reciprocal(share[:, 0, :], share_d[:]))
                step(lambda: V.tensor_tensor(share[:, 1, :], share[:, 0, :], rt_k[:], ALU.mult))

        for n in range(2):
            route(None, n, dry=True)

        def ffn_vector(dve, n):
            z = Z[n]
            for t in range(TT):
                nc.vector.bn_stats(t_stat[:, t, :], x_all[:, t, :]).then_inc(z["stat_step"], 1)
            for t in range(TT):
                dve.wait_ge(z["stat_step"], TT)
                nc.vector.bn_aggr(t_mv[:, t, :], t_stat[:, t, :]).then_inc(z["stat_step"], 1)
            if n == 0:
                dve.wait_ge(z["counted"], 1)
                nc.vector.tensor_copy(w_gate[:, 0, :], ps[:, 7, 0:E]).then_inc(gate_ready, 1)
            dve.wait_ge(z["stat_rstd"], 2)
            for t in range(TT):
                nc.vector.tensor_scalar(xn_all[:, t, :], x_all[:, t, :], t_mv[:, t, 0:1], t_rstd[:, t:t + 1],
                                        ALU.subtract, ALU.mult).then_inc(z["xn_all"], 1)
            route(dve, n)

            def emit(blk):
                at, live, some = blk.at, blk.live, blk.some
                for q in range(4):
                    t0 = lambda j: 4 * j + q
                    t2 = lambda j: 4 * j + q - 2
                    if live(t2, SLOTS):
                        dve.wait_ge(z["down_done"], at(lambda j: t2(j) + 1))
                        if some(t2, 2):
                            dve.wait_ge(z["rows_out"][q % 2], at(lambda j: 16 * (t2(j) // 2)))
                        nc.vector.tensor_copy(s_out[:, q % 2, :], down_ps[q % 2]).then_inc(z["out_taken"], 1)
                    if live(t0, SLOTS):
                        dve.wait_ge(z["act_done"], at(lambda j: t0(j) + 1))
                        if some(t0, 2):
                            dve.wait_ge(z["hid_t"], at(lambda j: t0(j) - 1))
                        nc.vector.tensor_tensor(s_hid[:, q % 2, :], gate_ps[q % 2], s_act[:, q % 2, :], ALU.mult
                                                ).then_inc(z["hid_done"], 1)
            run_blocks(dve, Tiles, emit)
            if n == 1:
                for b in range(B):
                    mix(dve, n, b)

        def next_phase(eng, k):
            eng.drain().then_inc(phase[k], 1)
            eng.wait_ge(phase[k], 5)

        @block.sync
        def _(sp):
            start_sync(sp)
            att_sync(sp, L[0])
            next_phase(sp, 0)
            ffn_sync(sp, 0)
            next_phase(sp, 1)
            att_sync(sp, L[1])
            next_phase(sp, 2)
            ffn_sync(sp, 1)

        @block.gpsimd
        def _(pool):
            start_gpsimd(pool)
            att_gpsimd(pool, L[0])
            next_phase(pool, 0)
            ffn_gpsimd(pool, 0)
            next_phase(pool, 1)
            att_gpsimd(pool, L[1])
            next_phase(pool, 2)
            ffn_gpsimd(pool, 1)

        @block.scalar
        def _(act):
            act.wait_ge(wt_taken, 10)
            act.wait_ge(zero_done, 4)
            act.wait_ge(gp_init, GP_INIT)
            act.wait_ge(w_in, 16 * W_DMAS)
            att_scalar(act, L[0])
            next_phase(act, 0)
            ffn_scalar(act, 0)
            next_phase(act, 1)
            att_scalar(act, L[1])
            next_phase(act, 2)
            ffn_scalar(act, 1)

        @block.vector
        def _(dve):
            start_vector(dve)
            dve.wait_ge(gp_init, GP_INIT)
            att_vector(dve, L[0])
            next_phase(dve, 0)
            ffn_vector(dve, 0)
            next_phase(dve, 1)
            att_vector(dve, L[1])
            next_phase(dve, 2)
            ffn_vector(dve, 1)

        @block.tensor
        def _(pe):
            start_tensor(pe)
            att_tensor(pe, L[0])
            next_phase(pe, 0)
            ffn_tensor(pe, 0)
            next_phase(pe, 1)
            att_tensor(pe, L[1])
            next_phase(pe, 2)
            ffn_tensor(pe, 1)


_INS = ["x", "ctx_1024",
        "L0_xattn_q1_w", "L0_xattn_q2_w", "L0_xattn_kv1_w", "L0_xattn_kv2_w", "L0_xattn_proj_w", "L0_xattn_proj_b",
        "L0_xattn_norm_w", "L0_xattn_lambda_1", "L0_xattn_lambda_2",
        "L0_ffn_gate_w", "L0_ffn_w1", "L0_ffn_w2", "L0_ffn_w3",
        "L1_xattn_W_q", "L1_xattn_b_q", "L1_xattn_W_k", "L1_xattn_b_k", "L1_xattn_W_v", "L1_xattn_b_v",
        "L1_xattn_W_o", "L1_xattn_b_o",
        "L1_ffn_gate_kernel", "L1_ffn_w0", "L1_ffn_w1", "L1_ffn_wo"]


def kernel(**inputs):
    import numpy as np
    import concourse.bacc as bacc
    from concourse.bass_utils import run_bass_kernel_spmd

    nc = bacc.Bacc("TRN2", target_bir_lowering=False, num_devices=1)
    arrays, aps = {}, {}
    for name in _INS:
        x = np.ascontiguousarray(inputs[name])
        arrays[f"in_{name}_dram"] = x
        aps[name] = nc.dram_tensor(f"in_{name}_dram", x.shape, mybir.dt.from_np(x.dtype), kind="ExternalInput").ap()
    out = nc.dram_tensor("out_dram", (B, NQ, D), F32, kind="ExternalOutput").ap()
    build(nc, aps, out)
    return run_bass_kernel_spmd(nc, [arrays], core_ids=[0]).results[0]["out_dram"]
```

```python
from contextlib import ExitStack

import concourse.bass as bass
from concourse import mybir

ALU = mybir.AluOpType
ACT = mybir.ActivationFunctionType
AX = mybir.AxisListType
F32 = mybir.dt.float32
BF16 = mybir.dt.bfloat16
I32 = mybir.dt.int32
U32 = mybir.dt.uint32

P = 128
B, NQ, NK, D = 8, 256, 512, 128
H, HD = 16, 8
HH = H // 2
KT, QT = NK // P, NQ // P
SCALE = HD ** -0.5
LN_EPS, RMS_EPS, LAMBDA_INIT = 1e-5, 1e-6, 0.1
E, F = 8, 512
FC = F // P
TOK = B * NQ
TT = TOK // P
SLOTS = TT * 2 + E - 1
BIG = 3.0e38
TWO_ONES = 1.0 + 0x3F80 / 2.0 ** 23
UNIT = 16
PAIR = 2 * UNIT
KQ = NK + NQ

TERMS = [(0, 0), (1, 1), (0, 1), (1, 0), (0, 2), (2, 0)]
MROW = 96
STACK_DMAS = 10

W_LOAD, W_CT, W_K, W_XT, W_Q, W_V = 0, 2, 3, 6, 7, 11
P_O, P_OT, P_ON, P_PROJ = 18, 25, 31, 33
P_DIFF, P_SUMS, P_RMS = P_OT + 1, P_OT + 2, P_OT + 3
M_T = 3
R_STATS, R_AGGR, R_RSTD, R_ROWS, R_XT, R_SCORE, R_COUNT, R_SCATTER = 34, 35, 35, 38, 44, 46, 56, 63
CHAIN_A, CHAIN_B = 15, 7
CHAIN = CHAIN_A + CHAIN_B - 2
WIDE = D + 2
REGION = TOK
BLOCKS = E * REGION // P + -(-SLOTS // 8) * 8


class Layer:
    loops = 2
    tail = 2

    def __init__(self, n):
        self.n = n
        self.diff = n == 0
        self.units = 2 * B if self.diff else B
        self.pairs = self.units // 2
        self.steps = self.units * UNIT
        self.order = {}
        for g in range(-PAIR, self.steps + 2 * PAIR):
            for job in self.jobs(g):
                if 0 <= job[1] < (2 * self.units if job[0] == "mt" else self.units):
                    self.order[job] = len(self.order)

    def leads(self, u):
        return not self.diff or u % 2 == 0

    def ends(self, u):
        return not self.diff or u % 2 == 1

    def jobs(self, g):
        w = g % UNIT
        v = (g - w) // UNIT + 2
        out = []
        if w == W_CT and self.leads(v):
            out.append(("ct", v))
        if w == W_K:
            out.append(("k", v))
        if w == W_XT and self.leads(v):
            out.append(("xt", v))
        if w == W_Q:
            out.append(("q", v))
        if w == W_V and self.leads(v):
            out.append(("v", v))
        if (g + M_T) % 8 == 0:
            out.append(("mt", (g + M_T) // 8))
        for name, p in (("ot", P_OT), ("on", P_ON), ("proj", P_PROJ), ("rt", R_XT), ("rs", R_SCORE), ("rc", R_COUNT)):
            if (g - p) % UNIT == 0 and (name == "ot" or self.ends((g - p) // UNIT)):
                out.append((name, (g - p) // UNIT))
        return out

    def batch(self, u):
        return u // 2 if self.diff else u

    def par(self, s, p):
        return (s - p) // UNIT % 2

    def lead_no(self, v):
        return v // 2 if self.diff else v


class Block:

    def __init__(self, layer, j=None, it=None):
        self.layer, self.j, self.it = layer, j, it

    def at(self, f):
        if self.it is None:
            return f(self.j)
        j = self.layer.loops
        return f(j) + (f(j + 1) - f(j)) * self.it

    def live(self, f, n):
        return self.it is not None or 0 <= f(self.j) < n

    def some(self, f, least):
        return f(self.layer.loops if self.it is not None else self.j) >= least

    def jobs(self, s):
        j0 = self.layer.loops if self.it is not None else self.j
        out = []
        for name, v in self.layer.jobs(PAIR * j0 + s):
            per = 4 if name == "mt" else 2
            if (name, v) in self.layer.order:
                unit = lambda j, v=v, per=per: v + per * (j - j0)
                out.append((name, unit, lambda j, name=name, unit=unit: self.layer.order[(name, unit(j))]))
        return out


def run_blocks(eng, layer, emit):
    for j in range(-1, layer.loops):
        emit(Block(layer, j=j))
    if layer.pairs - 1 - layer.loops > 1:
        with eng.Fori(0, layer.pairs - 1 - layer.loops) as it:
            emit(Block(layer, it=it))
    else:
        emit(Block(layer, j=layer.loops))
    for j in range(layer.pairs - 1, layer.pairs + layer.tail):
        emit(Block(layer, j=j))


def build(nc, a, out):
    L = [Layer(0), Layer(1)]
    with ExitStack() as ctx:
        def sb(name, shape, dt=F32):
            return ctx.enter_context(nc.sbuf_tensor(name, shape, dt))

        def sem(name):
            return ctx.enter_context(nc.semaphore(name))

        def dram(name, shape, dt=F32):
            return nc.dram_tensor(name, shape, dt).ap()

        rows_in = dram("rows_in", (BLOCKS * P, WIDE))
        results = dram("results", (2 * TOK + SLOTS * P, D))

        ident = sb("ident", [P, P])
        identb = sb("identb", [P, P], BF16)
        stack = sb("stack", [P, 4, HH, KQ], BF16)
        parts = sb("parts", [P, 2, 3, KQ], BF16)
        rest_k = sb("rest_k", [P, NK])
        rest_q = sb("rest_q", [P, NQ])
        probs = sb("probs", [P, 4, 4, NQ])
        vpad = sb("vpad", [P, 2, 2, KT, 4, 32])
        vals = sb("vals", [P, 2, KT, D])
        ctx_sb = sb("ctx_sb", [P, KT, D])
        ctxT = sb("ctxT", [P, NK])
        x_all = sb("x_all", [P, TT, D])
        x_stat = sb("x_stat", [P, QT, 6])
        x_mv = sb("x_mv", [P, QT, 2])
        x_rstd = sb("x_rstd", [P, QT])
        xn = sb("xn", [P, QT, D])
        xnT = sb("xnT", [P, NQ])
        row_max = sb("row_max", [P, 2, QT, HH])
        max_rest = sb("max_rest", [P, QT, HH])
        max_parts = sb("max_parts", [P, 2, QT, 3, HH], BF16)
        max_rows = sb("max_rows", [3 * HH, 2, NQ], BF16)
        outT = sb("outT", [P, 2, NQ])
        r_den = sb("r_den", [P, QT, H])
        o_first = sb("o_first", [P, QT * H, HD])
        o_second = sb("o_second", [P, QT * H, HD])
        o_diff = sb("o_diff", [P, QT, D])
        o_sq = sb("o_sq", [P, D])
        o_ss = sb("o_ss", [P, QT])
        o_rr = sb("o_rr", [P, QT])
        o_norm = sb("o_norm", [P, QT, D])
        onT = sb("onT", [P, NQ])
        half_neg = sb("half_neg", [P, TT])
        raw = sb("raw", [P, 10, D])
        raw_perm = sb("raw_perm", [P, 2, D])
        w_all = sb("w_all", [P, 10, D])
        bias_k = sb("bias_k", [P, 2])
        bias_q = sb("bias_q", [P, 2])
        bias_v = sb("bias_v", [P, 2, D])
        bias_o = sb("bias_o", [P, 2, D])
        norm_col = sb("norm_col", [P, 1])
        lam_in = sb("lam_in", [P, 2, H])
        lam_d = sb("lam_d", [P, H])
        lam = sb("lam", [P, H])

        zero_rows = sb("zero_rows", [P, QT * WIDE])
        w_exp = sb("w_exp", [P, 3, E, F])
        gate_raw = sb("gate_raw", [E, D])
        w_gate = sb("w_gate", [P, 2, E])
        y_all = w_exp[:, 0].rearrange("p e (n c) -> p (e n) c", c=D)
        t_stat = sb("t_stat", [P, QT, 6])
        t_mv = sb("t_mv", [P, QT, 2])
        t_rstd = sb("t_rstd", [P, QT])
        t_rows = sb("t_rows", [P, 2, QT, WIDE])
        t_rowsT = sb("t_rowsT", [P, NQ])
        t_top = sb("t_top", [P, 2, QT])
        t_a = sb("t_a", [P, QT, E])
        t_k = sb("t_k", [P, 2, QT])
        i_token = sb("i_token", [P, TT], I32)
        token_no = sb("token_no", [P, TT])
        t_next = sb("t_next", [P, QT, E])
        t_hot = sb("t_hot", [P, 2, QT, E])
        t_hot_at = sb("t_hot_at", [P, 2, QT, E])
        t_pick = sb("t_pick", [P, QT, E], BF16)
        t_count = sb("t_count", [P, 2, QT, E])
        t_from = sb("t_from", [P, QT, E])
        t_place = sb("t_place", [P, QT, E])
        t_place_f = sb("t_place_f", [P, 2, QT])
        t_pos = sb("t_pos", [P, 2, QT], U32)
        i_region = sb("i_region", [P, E], I32)
        region = sb("region", [P, E])
        tri = sb("tri", [P, P], BF16)
        ones = sb("ones", [P, P], BF16)
        i_rev = sb("i_rev", [P, E], I32)
        rev = sb("rev", [P, E])
        i_slot = sb("i_slot", [P, SLOTS], I32)
        slot_no = sb("slot_no", [P, SLOTS])
        i_full = sb("i_full", [P, TT], I32)
        full_rows = sb("full_rows", [P, TT])
        carry = sb("carry", [P, E, TT])
        gate_s = sb("gate_s", [P, TT, E])
        gate_s2 = sb("gate_s2", [P, TT, E])
        gate_abs = sb("gate_abs", [P, TT, E])
        below = sb("below", [P, 2, TT, E])
        near = sb("near", [P, 2, TT, E])
        exps = sb("exps", [P, 2, TT, E])
        below_2 = sb("below_2", [P, TT])
        exp_2 = sb("exp_2", [P, TT])
        top = sb("top", [P, 2, TT])
        rt_a = sb("rt_a", [P, TT, E])
        rt_k = sb("rt_k", [P, TT])
        hot = sb("hot", [P, 2, TT, E])
        share = sb("share", [P, 2, TT])
        share_d = sb("share_d", [P, 2, TT])
        count_e = sb("count_e", [P, E])
        more = sb("more", [P, E, TT])
        n_tiles = sb("n_tiles", [P, E])
        tile_end = sb("tile_end", [P, E])
        tile_at = sb("tile_at", [P, E])
        shift = sb("shift", [P, E])
        step_e = sb("step_e", [P, E])
        done_e = sb("done_e", [P, SLOTS, E])
        tile_e = sb("tile_e", [P, SLOTS])
        expert_of = sb("expert_of", [P, SLOTS], I32)
        done_step = sb("done_step", [P, SLOTS, E])
        block_f = sb("block_f", [P, SLOTS])
        block_of = sb("block_of", [P, SLOTS], I32)
        tile_mark = sb("tile_mark", [P, SLOTS])
        ends_at = sb("ends_at", [P, E])
        ends_step = sb("ends_step", [P, E])
        row_limit = sb("row_limit", [P, SLOTS])
        row_used = sb("row_used", [P, SLOTS])
        row_spare = sb("row_spare", [P, SLOTS])
        spare_at = sb("spare_at", [P, 1])
        spare_no = sb("spare_no", [P, SLOTS])
        s_dest = sb("s_dest", [P, 4])
        s_place = sb("s_place", [P, 4], U32)
        s_rows = sb("s_rows", [P, 4, WIDE])
        s_rowsT = sb("s_rowsT", [P, 2, P])
        s_act = sb("s_act", [P, 2, F])
        s_hid = sb("s_hid", [P, 2, F])
        s_hidT = sb("s_hidT", [P, 2, F])
        s_out = sb("s_out", [P, 2, D])

        ps = ctx.enter_context(nc.psum_tensor("ps", [P, 8, 512], F32))
        score = [ps[:, 0:2, :].rearrange("p b (i n) -> p (b i) n", i=2),
                 ps[:, 2:4, :].rearrange("p b (i n) -> p (b i) n", i=2)]
        maxs = [ps[:, 4, :], ps[:, 5, :]]
        oacc = ps[:, 6, :].rearrange("p (f n) -> p f n", f=2)
        misc = ps[:, 7, :]
        misc_bf = misc.bitcast(BF16)

        w_first = sem("w_first")
        w_in = sem("w_in")
        bias_in = sem("bias_in")
        x_start = sem("x_start")
        ones_done = sem("ones_done")
        gp_init = sem("gp_init")
        late_init = sem("late_init")
        raw_perm_ready = sem("raw_perm_ready")
        wt_ready = sem("wt_ready")
        wt_taken = sem("wt_taken")
        zero_done = sem("zero_done")
        const_step = sem("const_step")
        rows_zero = sem("rows_zero")
        w_exp_in = sem("w_exp_in")
        lam_step = sem("lam_step")
        gate_ready = sem("gate_ready")
        carrier = sem("carrier")

        WQ = [[0, 1], [6, 6]]
        WK = [[2, 3], [7, 7]]
        WV = [4, 8]
        WO = [5, 9]

        def heads_last(ap):
            return ap.rearrange("p (f h d) -> p f d h", f=2, h=HH)

        block = ctx.enter_context(nc.Block())

        def att_sems(n):
            names = ("ctx_in qk_done exp_done pv_done mx_ready mx_taken job_ready job_taken a1_done "
                     "split_step vpad_ready ln_step rstd_step xn_ready mp_step o_taken den_step on_ready "
                     "rr_step res_ready diffed "
                     "t_stats t_rstds t_rows_ready t_from_set route_step").split()
            d = {k: sem(f"{k}{n}") for k in names}
            d["stack_in"] = [sem(f"stack_in{n}_{i}") for i in range(4)]
            d["scattered"] = [sem(f"scattered{n}_{i}") for i in range(2)]
            d["mrow_in"] = [sem(f"mrow_in{n}_{i}") for i in range(2)]
            return d

        S = [att_sems(0), att_sems(1)]
        phase = [sem(f"phase{i}") for i in range(3)]

        FIRST = 5

        def start_sync(sp):
            sp.dma_start(ctx_sb[:], a["ctx_1024"][0].rearrange("(t p) c -> p t c", p=P)).then_inc(S[0]["ctx_in"], 16)
            xs = a["x"].rearrange("b (t p) c -> p (b t) c", p=P)
            sp.dma_start(x_all[:, 0:QT, :], xs[:, 0:QT, :]).then_inc(x_start, 16)
            for i, src in ((0, a["L0_xattn_q1_w"]), (1, a["L0_xattn_q2_w"]), (2, a["L0_xattn_kv1_w"][0:D, :]),
                           (3, a["L0_xattn_kv2_w"][0:D, :]), (4, a["L0_xattn_kv1_w"][D:2 * D, :]),
                           (5, a["L0_xattn_proj_w"]), (6, a["L1_xattn_W_q"]), (7, a["L1_xattn_W_k"]),
                           (8, a["L1_xattn_W_v"]), (9, a["L1_xattn_W_o"])):
                sp.dma_start(raw[:, i, :], src).then_inc(w_first if i < FIRST else w_in, 16)
            sp.dma_start(gate_raw[:], a["L0_ffn_gate_w"]).then_inc(w_in, 16)
            sp.dma_start(w_gate[:, 1, :], a["L1_ffn_gate_kernel"]).then_inc(w_in, 16)
            for f in range(2):
                r = slice(f * 64, f * 64 + 64)
                for i in range(4):
                    sp.dma_start(norm_col[64 * f + 16 * i:64 * f + 16 * i + 16, :],
                                 a["L0_xattn_norm_w"][r].rearrange("(q i d o) -> i q d o", q=2, i=4, o=1)[i],
                                 allow_slow_non_contiguous=True).then_inc(w_in, 16)
            for i, name in enumerate(("L0_xattn_lambda_1", "L0_xattn_lambda_2")):
                sp.dma_start(lam_in[:, i, :], a[name].rearrange("a h b c -> (a h b c)").partition_broadcast(P)
                             ).then_inc(w_in, 16)
            sp.dma_start(x_all[:, QT:TT, :], xs[:, QT:TT, :]).then_inc(x_start, 16)
            sp.dma_start(bias_o[:, 0, :], a["L0_xattn_proj_b"].partition_broadcast(P)).then_inc(bias_in, 16)

        def load_biases(sp):
            for f in range(2):
                r = slice(f * 64, f * 64 + 64)
                for col, src in ((bias_q, a["L1_xattn_b_q"]), (bias_k, a["L1_xattn_b_k"])):
                    sp.dma_start(col[r, 1:2], src[r].rearrange("(h d o) -> d h o", h=HH, o=1),
                                 allow_slow_non_contiguous=True).then_inc(bias_in, 16)
            for tile, src in ((bias_o[:, 1, :], a["L1_xattn_b_o"]), (bias_v[:, 1, :], a["L1_xattn_b_v"])):
                sp.dma_start(tile, src.partition_broadcast(P)).then_inc(bias_in, 16)

        def load_expert(pool, n, e, k):
            src = a[(("L0_ffn_w1", "L0_ffn_w3", "L0_ffn_w2"), ("L1_ffn_w0", "L1_ffn_w1", "L1_ffn_wo"))[n][k]][e]
            dst = w_exp[:, k, e, :]
            if (n == 0) == (k < 2):
                dst, src = dst.rearrange("p (c h) -> p c h", c=FC), src.rearrange("(c p) h -> p c h", p=P)
            pool.dma_start(dst, src).then_inc(w_exp_in, 16)

        W_EXP_DMAS = [3 * E, 2 * 3 * E]

        W_DMAS = 10 - FIRST + 2 + 2 * 4 + 2

        def zero_view(c):
            return stack[:, c, :, :].bitcast(F32)

        def start_gpsimd(pool):
            for c in range(2, 4):
                nc.gpsimd.memset(zero_view(c), 0.0).then_inc(zero_done, 1)
            nc.gpsimd.memset(ident[:], 1.0).then_inc(gp_init, 1)
            pool.wait_ge(gp_init, 1)
            nc.gpsimd.affine_select(out=ident[:], in_=ident[:], compare_op=ALU.is_equal, fill=0.0, base=0,
                                    pattern=[[-1, P]], channel_multiplier=1).then_inc(gp_init, 1)
            pool.wait_ge(gp_init, 2)
            nc.gpsimd.tensor_copy(identb[:], ident[:]).then_inc(gp_init, 1)
            nc.gpsimd.memset(half_neg[:], -0.5).then_inc(gp_init, 1)
            nc.gpsimd.memset(vpad[:], 0.0).then_inc(gp_init, 1)
            pool.wait_ge(gp_init, 5)
            for pp in range(2):
                nc.gpsimd.memset(vpad[:, :, pp, :, :, 16 * pp + HD:16 * pp + HD + 1], 1.0).then_inc(gp_init, 1)
            nc.gpsimd.memset(bias_k[:, 0:1], 0.0).then_inc(gp_init, 1)
            nc.gpsimd.memset(bias_q[:, 0:1], 0.0).then_inc(gp_init, 1)
            nc.gpsimd.memset(bias_v[:, 0, :], 0.0).then_inc(gp_init, 1)

        GP_INIT = 10

        def ones_rows(c):
            nc.vector.memset(stack[MROW:P, c, :, 0:NK].bitcast(F32), TWO_ONES).then_inc(ones_done, 1)

        def late_gpsimd(pool):
            nc.gpsimd.memset(ones[:], 1.0).then_inc(late_init, 1)
            nc.gpsimd.iota(i_rev[:], pattern=[[-1, E]], base=E, channel_multiplier=0).then_inc(late_init, 1)
            nc.gpsimd.iota(i_slot[:], pattern=[[1, SLOTS]], base=0, channel_multiplier=0).then_inc(late_init, 1)
            nc.gpsimd.iota(i_full[:], pattern=[[P, TT]], base=0, channel_multiplier=0).then_inc(late_init, 1)
            nc.gpsimd.iota(i_region[:], pattern=[[REGION, E]], base=0, channel_multiplier=0).then_inc(late_init, 1)
            nc.gpsimd.iota(i_token[:], pattern=[[P, TT]], base=0, channel_multiplier=1).then_inc(late_init, 1)
            nc.gpsimd.memset(carry[:], 1.0).then_inc(const_step, 1)
            pool.wait_ge(late_init, 6)
            nc.gpsimd.tensor_copy(token_no[:], i_token[:]).then_inc(late_init, 1)
            nc.gpsimd.tensor_copy(region[:], i_region[:]).then_inc(late_init, 1)
            nc.gpsimd.tensor_copy(rev[:], i_rev[:]).then_inc(late_init, 1)
            nc.gpsimd.tensor_copy(slot_no[:], i_slot[:]).then_inc(late_init, 1)
            nc.gpsimd.tensor_copy(full_rows[:], i_full[:]).then_inc(late_init, 1)
            pool.wait_ge(const_step, 1)
            for e in range(E):
                nc.gpsimd.memset(carry[:, e, 0:1], 0.0).then_inc(late_init, 1)
            nc.gpsimd.affine_select(out=tri[:], in_=ones[:], compare_op=ALU.is_gt, fill=0.0, base=0,
                                    pattern=[[1, P]], channel_multiplier=-1).then_inc(const_step, 1)
            nc.gpsimd.memset(zero_rows[:], 0.0).then_inc(const_step, 1)

        LATE_INIT = 6 + 5 + E

        def start_vector(dve):
            for c in range(2):
                nc.vector.memset(zero_view(c), 0.0).then_inc(zero_done, 1)
            transposed(dve, range(FIRST))

        def transposed(dve, which):
            for i in which:
                dve.wait_ge(wt_ready, i + 1)
                src = ps[:, i % 4, 0:D]
                if i in WQ[0] + WK[0] + WQ[1][:1] + WK[1][:1]:
                    ins = nc.vector.tensor_copy(w_all[:, i, :].rearrange("p (f d h) -> p f d h", f=2, d=HD),
                                                heads_last(src))
                elif i == WO[0]:
                    ins = nc.vector.tensor_scalar(w_all[:, i, :], src, norm_col[:, 0:1], None, ALU.mult)
                else:
                    ins = nc.vector.tensor_copy(w_all[:, i, :], src)
                ins.then_inc(wt_taken, 1)

        def late_vector(dve):
            dve.wait_ge(w_in, 16 * W_DMAS)
            for n in range(2):
                for f in range(2):
                    r = slice(f * 64, f * 64 + 64)
                    nc.vector.tensor_copy(raw_perm[:, n, r].rearrange("p (i q d) -> p q i d", i=4, q=2),
                                          raw[:, WO[n], r].rearrange("p (q i d) -> p q i d", q=2, i=4)
                                          ).then_inc(raw_perm_ready, 1)
            nc.vector.tensor_tensor(lam_d[:], lam_in[:, 0, :], lam_in[:, 1, :], ALU.subtract).then_inc(lam_step, 1)
            dve.wait_ge(lam_step, 1)
            for f in range(2):
                nc.vector.tensor_scalar(lam[:, f * 8:f * 8 + 8].rearrange("p (i q) -> p q i", i=4),
                                        lam_d[:, f * 8:f * 8 + 8].rearrange("p (q i) -> p q i", q=2),
                                        LAMBDA_INIT, None, ALU.add).then_inc(lam_step, 1)
            transposed(dve, range(FIRST, 10))
            dve.wait_ge(gate_ready, 1)
            nc.vector.tensor_copy(w_gate[:, 0, :], ps[:, 2, 0:E]).then_inc(gate_ready, 1)
            dve.wait_ge(zero_done, 4)
            for c in range(4):
                ones_rows(c)

        def start_tensor(pe):
            pe.wait_ge(gp_init, GP_INIT)
            pe.wait_ge(w_first, 16 * FIRST)
            transpose_weights(pe, range(FIRST))
            pe.wait_ge(wt_taken, FIRST)
            pe.wait_ge(zero_done, 4)

        def transpose_weights(pe, which):
            for i in which:
                if i >= 4:
                    pe.wait_ge(wt_taken, i - 3)
                nc.tensor.transpose(ps[:, i % 4, 0:D], raw_perm[:, WO.index(i), :] if i in WO else raw[:, i, :],
                                    ident[:]).then_inc(wt_ready, 1)

        def late_tensor(pe):
            pe.wait_ge(w_in, 16 * W_DMAS)
            pe.wait_ge(raw_perm_ready, 4)
            transpose_weights(pe, range(FIRST, 10))
            pe.wait_ge(wt_taken, 7)
            nc.tensor.transpose(ps[:, 2, 0:E], gate_raw[:], ident[0:E, 0:E]).then_inc(gate_ready, 1)
            pe.wait_ge(wt_taken, 10)
            pe.wait_ge(gate_ready, 2)

        def apart(eng):
            eng.sem_inc(carrier, 1)

        MIX_AT = {1: 0, 9: 1, 10: 2, 11: 3, 12: 4, 13: 5, 14: 6, 15: 7}

        BEYOND = BLOCKS - E * REGION // P
        assert BEYOND % 8 == 0
        ZERO_DMAS = BEYOND // 8
        ZERO_AT = 29

        WT_AT = 3

        def mix(dve, n, b):
            dve.wait_ge(Z[n]["result_in"][b], 16 * 2)
            for e in range(2):
                if e:
                    dve.wait_ge(Z[n]["mixed"], 4 * b + 2)
                for t in range(QT * b, QT * b + QT):
                    nc.vector.scalar_tensor_tensor(out=x_all[:, t, :], in0=y_all[:, 2 * QT * b + QT * e + t - QT * b, :],
                                                   scalar=share[:, e, t:t + 1], in1=x_all[:, t, :],
                                                   op0=ALU.mult, op1=ALU.add).then_inc(Z[n]["mixed"], 1)

        def att_sync(sp, layer):
            n, z = layer.n, S[layer.n]
            cs = a["ctx_1024"].rearrange("b (t p) c -> p b t c", p=P)

            def emit(blk):
                at, live, some = blk.at, blk.live, blk.some
                for s in range(PAIR):
                    w = s % UNIT
                    v = lambda j: 2 * j + s // UNIT + 2
                    lead = layer.leads(s // UNIT)
                    first = blk.j == -1 and s == 0
                    if w == W_LOAD and lead and live(v, layer.units) and not first:
                        b = lambda j: layer.lead_no(v(j))
                        if some(b, 1):
                            prev = lambda j: v(j) - (2 if layer.diff else 1)
                            sp.wait_ge(z["job_ready"], at(lambda j: layer.order[("ct", prev(j))] + 1))
                        sp.dma_start(ctx_sb[:], cs[:, bass.ds(at(b), 1), :, :].rearrange("p b t c -> p (b t) c")
                                     ).then_inc(z["ctx_in"], 16)
                    for c_half, w_key, w_query in ((0, 8, 9), (1, 0, 0)):
                        for group, w_g in (("key", w_key), ("query", w_query)):
                            if w != w_g:
                                continue
                            u = v if c_half == 0 else (lambda j: 2 * j + s // UNIT + 1)
                            if not live(u, layer.units):
                                continue
                            c = lambda j: 2 * u(j) + c_half
                            par = (s // UNIT + (0 if c_half == 0 else 1)) % 2
                            slot = 2 * par + c_half
                            sp.wait_ge(z["split_step"], at(lambda j: 6 * u(j) + (3 if group == "key" else 6)))
                            apart(sp)
                            if group == "key" and some(c, 4):
                                sp.wait_ge(z["qk_done"], at(lambda j: 8 * (c(j) - 3)))
                            for t, (qp, kp) in enumerate(TERMS):
                                src = parts[64 * c_half:64 * c_half + 64, par]
                                dst = stack[8 * t:8 * t + 8, slot]
                                if group == "key" and qp != kp:
                                    sp.dma_start(dst[:, :, 0:NK], src[:, kp, 0:NK]).then_inc(z["stack_in"][slot], 16)
                                if group == "query" and qp == kp:
                                    sp.dma_start(dst[:, :, :], src[:, kp, :]).then_inc(z["stack_in"][slot], 16)
                                if group == "query" and qp != kp:
                                    sp.dma_start(dst[:, :, NK:KQ], src[:, qp, NK:KQ]).then_inc(z["stack_in"][slot], 16)
                    for name, u, no in blk.jobs(s):
                        if name == "mt":
                            slot = (s + M_T) // 8 % 4
                            sp.wait_ge(z["job_taken"], at(lambda j: no(j) + 1))
                            sp.dma_start(stack[MROW:MROW + 3, slot, :, NK:KQ], max_rows[:, slot % 2, :]
                                         ).then_inc(z["mrow_in"][slot % 2], 16)
                if n == 0 and blk.j == layer.pairs:
                    load_biases(sp)
            run_blocks(sp, layer, emit)

        def att_tensor(pe, layer):
            n, z = layer.n, S[layer.n]

            def job(blk, s, name, u, no):
                at = blk.at
                if name != "first":
                    if blk.some(no, 1):
                        pe.wait_ge(z["job_taken"], at(no))
                if name == "ct":
                    pe.wait_ge(z["ctx_in"], at(lambda j: 16 * (layer.lead_no(u(j)) + 1)))
                    for t in range(KT):
                        ins = nc.tensor.transpose(misc[:, t * P:(t + 1) * P], ctx_sb[:, t, :], ident[:])
                elif name == "k":
                    ins = nc.tensor.matmul(misc, w_all[:, WK[n][s // UNIT], :], ctxT[:], start=True, stop=True)
                elif name == "xt":
                    pe.wait_ge(z["xn_ready"], at(lambda j: 2 * (layer.lead_no(u(j)) + 1)))
                    for t in range(QT):
                        ins = nc.tensor.transpose(misc[:, t * P:(t + 1) * P], xn[:, t, :], ident[:])
                elif name == "q":
                    ins = nc.tensor.matmul(misc[:, 0:NQ], w_all[:, WQ[n][s // UNIT], :], xnT[:], start=True, stop=True)
                elif name == "v":
                    for t in range(KT):
                        ins = nc.tensor.matmul(misc[:, t * P:(t + 1) * P], ctxT[:, t * P:(t + 1) * P],
                                               w_all[:, WV[n], :], start=True, stop=True)
                elif name == "mt":
                    pe.wait_ge(z["mp_step"], at(lambda j: 4 * (u(j) + 1)))
                    for t in range(QT):
                        src = max_parts[:, (s + M_T) // 8 % 2, t].rearrange("p a h -> p (a h)")
                        ins = nc.tensor.transpose(misc_bf[0:3 * HH, t * P:(t + 1) * P], src, identb[:])
                elif name == "ot":
                    pe.wait_ge(z["o_taken"], at(lambda j: u(j) + 1))
                    for t in range(QT):
                        for f in range(2):
                            ins = nc.tensor.transpose(misc[:, (2 * t + f) * P:(2 * t + f + 1) * P],
                                                      outT[:, f, t * P:(t + 1) * P], ident[:])
                elif name == "on":
                    if layer.diff:
                        pe.wait_ge(z["on_ready"], at(lambda j: QT * (layer.lead_no(u(j)) + 1)))
                    for t in range(QT):
                        ins = nc.tensor.transpose(misc[:, t * P:(t + 1) * P], o_norm[:, t, :], ident[:])
                elif name == "proj":
                    for t in range(QT):
                        ins = nc.tensor.matmul(misc[:, t * P:(t + 1) * P], onT[:, t * P:(t + 1) * P],
                                               w_all[:, WO[n], :], start=True, stop=True)
                elif name == "rt":
                    pe.wait_ge(z["t_rows_ready"], at(lambda j: QT * (layer.batch(u(j)) + 1)))
                    for t in range(QT):
                        ins = nc.tensor.transpose(misc[:, t * P:(t + 1) * P], t_rows[:, layer.par(s, R_XT), t, 0:D], ident[:])
                elif name == "rs":
                    for t in range(QT):
                        ins = nc.tensor.matmul(misc[:, t * E:(t + 1) * E], t_rowsT[:, t * P:(t + 1) * P], w_gate[:, n, :],
                                               start=True, stop=True)
                elif name == "rc":
                    pe.wait_ge(z["route_step"], at(lambda j: CHAIN * layer.batch(u(j)) + CHAIN_A - 1))
                    for k, m in enumerate((tri, ones)):
                        ins = nc.tensor.matmul(misc[:, k * QT * E:(k + 1) * QT * E], m[:],
                                               t_pick[:].rearrange("p t e -> p (t e)"), start=True, stop=True)
                ins.then_inc(z["job_ready"], 1)

            def emit(blk):
                at, live, some = blk.at, blk.live, blk.some
                for s in range(PAIR):
                    if n == 0 and blk.j == -1 and s == W_V + 1:
                        late_tensor(pe)
                    k = s - WT_AT
                    if n == 0 and blk.j == layer.pairs and 0 <= k < 3 * E:
                        if k == 0:
                            pe.wait_ge(w_exp_in, 16 * W_EXP_DMAS[0])
                            pe.wait_ge(z["exp_done"], layer.steps)
                        if k >= 4:
                            pe.wait_ge(Z[0]["wt_copied"], k - 3)
                        for c in range(FC):
                            ins = nc.tensor.transpose(ps[:, k % 4, c * P:(c + 1) * P],
                                                      w_exp[:, k // E, k % E, c * P:(c + 1) * P], ident[:])
                        ins.then_inc(Z[0]["wt_done"], 1)
                    g = lambda j: PAIR * j + s
                    if live(g, layer.steps):
                        slot, pp, kt = s // 8, s // 4 % 2, s % 4
                        if s % 8 == 0:
                            pe.wait_ge(z["mrow_in"][slot % 2], at(lambda j: 16 * (2 * j + slot // 2 + 1)))
                        if n == 0 and blk.j == 0 and s in (0, UNIT):
                            pe.wait_ge(ones_done, 2 if s == 0 else 4)
                        if some(g, 2):
                            pe.wait_ge(z["exp_done"], at(lambda j: g(j) - 1))
                        for i in range(4):
                            ins = nc.tensor.matmul(score[s % 2][:, i, :],
                                                   stack[:, slot, 4 * pp + i, kt * P:(kt + 1) * P],
                                                   stack[:, slot, 4 * pp + i, NK:KQ], start=True, stop=True)
                        ins.then_inc(z["qk_done"], 1)
                    gm = lambda j: PAIR * j + s + UNIT
                    if live(gm, layer.steps):
                        slot = (s + UNIT) // 8 % 4
                        if s % 8 == 0:
                            cyc = lambda j: j + (s + UNIT) // PAIR
                            pe.wait_ge(z["stack_in"][slot], at(lambda j: 16 * STACK_DMAS * (cyc(j) + 1)))
                        for t in range(QT):
                            if some(gm, 1):
                                pe.wait_ge(z["mx_taken"], at(lambda j: 2 * gm(j) + t - 1))
                            nc.tensor.matmul(maxs[t], stack[0:MROW, slot, s % 8, NK + t * P:NK + (t + 1) * P],
                                             stack[0:MROW, slot, s % 8, 0:NK], start=True, stop=True
                                             ).then_inc(z["mx_ready"], 1)
                    for name, u, no in blk.jobs(s):
                        job(blk, s, name, u, no)
                    gp = lambda j: PAIR * j + s - 2
                    if live(gp, layer.steps):
                        sp_ = (s - 2) % PAIR
                        f, pp, kt = sp_ // 8 % 2, sp_ // 4 % 2, sp_ % 4
                        if sp_ % UNIT == 0 and some(gp, 1):
                            pe.wait_ge(z["o_taken"], at(lambda j: gp(j) // UNIT))
                        if sp_ % 8 == 0 and layer.leads(sp_ // UNIT):
                            pe.wait_ge(z["vpad_ready"], at(lambda j: 4 * layer.lead_no(gp(j) // UNIT) + 2 * f + 2))
                        pe.wait_ge(z["exp_done"], at(lambda j: gp(j) + 1))
                        for i in range(4):
                            ins = nc.tensor.matmul(oacc[32 * i:32 * i + 32, f, :], vpad[:, f, pp, kt, i, :],
                                                   probs[:, sp_ % 4, i, :], start=(sp_ % UNIT == 0),
                                                   stop=(sp_ % 8 == 7), skip_group_check=True)
                        ins.then_inc(z["pv_done"], 1)
            run_blocks(pe, layer, emit)

        def att_scalar(act, layer):
            n, z = layer.n, S[layer.n]

            def emit(blk):
                at, live, some = blk.at, blk.live, blk.some
                for s in range(PAIR):
                    uo = lambda j: 2 * j + (s - P_O) // UNIT
                    if (s - P_O) % UNIT == 0 and live(uo, layer.units):
                        act.wait_ge(z["pv_done"], at(lambda j: UNIT * (uo(j) + 1)))
                        if some(uo, 1):
                            act.wait_ge(z["job_ready"], at(lambda j: layer.order[("ot", uo(j) - 1)] + 1))
                        nc.scalar.copy(outT[:], oacc).then_inc(z["o_taken"], 1)
                    g = lambda j: PAIR * j + s
                    if live(g, layer.steps):
                        act.wait_ge(z["qk_done"], at(lambda j: g(j) + 1))
                        if some(g, 4):
                            act.wait_ge(z["pv_done"], at(lambda j: g(j) - 3))
                        nc.scalar.activation(probs[:, s % 4], score[s % 2], ACT.Exp, scale=SCALE
                                             ).then_inc(z["exp_done"], 1)
                    for name, u, no in blk.jobs(s):
                        if name in ("v", "ot", "proj", "rs", "rc"):
                            continue
                        act.wait_ge(z["job_ready"], at(lambda j: no(j) + 1))
                        par = s // UNIT
                        if name == "ct":
                            nc.scalar.copy(ctxT[:], misc).then_inc(z["job_taken"], 1)
                        elif name == "xt":
                            nc.scalar.copy(xnT[:], misc[:, 0:NQ]).then_inc(z["job_taken"], 1)
                        elif name == "rt":
                            nc.scalar.copy(t_rowsT[:], misc[:, 0:NQ]).then_inc(z["job_taken"], 1)
                        elif name == "on":
                            nc.scalar.copy(onT[:], misc[:, 0:NQ]).then_inc(z["job_taken"], 1)
                        elif name == "mt":
                            q = (s + M_T) // 8 % 2
                            if some(u, 2):
                                act.wait_ge(z["mrow_in"][q], at(lambda j: 16 * (u(j) // 2)))
                            nc.scalar.copy(max_rows[:, q, :], misc_bf[0:3 * HH, 0:NQ]).then_inc(z["job_taken"], 1)
                        else:
                            cols, bias = ((slice(0, NK), bias_k) if name == "k" else (slice(NK, KQ), bias_q))
                            if some(u, 2):
                                for slot in (2 * par, 2 * par + 1):
                                    act.wait_ge(z["stack_in"][slot], at(lambda j: 16 * STACK_DMAS * (u(j) // 2)))
                            nc.scalar.activation(parts[:, par, 0, cols], misc[:, 0:cols.stop - cols.start],
                                                 ACT.Identity, bias=bias[:, n:n + 1]).then_inc(z["a1_done"], 1)
                    for name, u, no in blk.jobs(s):
                        if name in ("k", "q"):
                            rest, bias, k = (rest_k, bias_k, 1) if name == "k" else (rest_q, bias_q, 2)
                            if some(u, 1):
                                act.wait_ge(z["split_step"], at(lambda j: 6 * (u(j) - 1) + 3 * k))
                            nc.scalar.activation(rest[:], misc[:, 0:NK if name == "k" else NQ], ACT.Identity,
                                                 bias=bias[:, n:n + 1]).then_inc(z["job_taken"], 1)
                        elif name == "v":
                            act.wait_ge(z["job_ready"], at(lambda j: no(j) + 1))
                            if some(u, 2):
                                act.wait_ge(z["vpad_ready"], at(lambda j: 4 * (layer.lead_no(u(j) - 2) + 1)))
                            nc.scalar.copy(vals[:, s // UNIT].rearrange("p t c -> p (t c)"), misc
                                           ).then_inc(z["job_taken"], 1)
                    k = s - WT_AT
                    if n == 0 and blk.j == layer.pairs and 0 <= k < 3 * E:
                        act.wait_ge(Z[0]["wt_done"], k + 1)
                        nc.scalar.copy(w_exp[:, k // E, k % E, :], ps[:, k % 4, :]).then_inc(Z[0]["wt_copied"], 1)
            run_blocks(act, layer, emit)

        def att_vector(dve, layer):
            n, z = layer.n, S[layer.n]

            def chain(blk, s, half):
                for base, first in ((R_SCORE, 0), (R_COUNT, CHAIN_A)):
                    for p in range(base, base + 8):
                        i = first + 2 * (p - base) + half - 1
                        u = lambda j, p=p: 2 * j + (s - p) // UNIT
                        if not first <= i < (CHAIN_A if first == 0 else CHAIN_A + CHAIN_B):
                            continue
                        if (s - p) % UNIT == 0 and layer.ends((s - p) // UNIT) and blk.live(u, layer.units):
                            chain_op(blk, u, lambda j, u=u: layer.batch(u(j)), i, layer.par(s, p))

            def chain_op(blk, u, b, i, par):
                at, some, V = blk.at, blk.some, nc.vector
                order = layer.order
                done = i - 1 if i <= CHAIN_A else i - 2
                G = gate_s[:, bass.ds(at(lambda j: QT * b(j)), QT), :]
                by_token = lambda ap: ap.rearrange("p (t o) -> p t o", o=1).broadcast_to([P, QT, E])
                by_expert = lambda ap: ap.rearrange("p (o e) -> p o e", o=1).broadcast_to([P, QT, E])
                if i == 0:
                    dve.wait_ge(z["job_ready"], at(lambda j: order[("rs", u(j))] + 1))
                elif i == CHAIN_A:
                    dve.wait_ge(z["job_ready"], at(lambda j: order[("rc", u(j))] + 1))
                else:
                    if i == 1:
                        dve.wait_ge(z["job_taken"], at(lambda j: order[("rs", u(j))] + 1))
                    if i == CHAIN_A + 1:
                        dve.wait_ge(z["job_taken"], at(lambda j: order[("rc", u(j))] + 1))
                    if i == CHAIN_A + 1 and not some(b, 1):
                        dve.wait_ge(z["t_from_set"], 1)
                    if done or some(b, 1):
                        dve.wait_ge(z["route_step"], at(lambda j: CHAIN * b(j) + done))
                if i == 0:
                    V.tensor_copy(G, misc[:, 0:QT * E].rearrange("p (t e) -> p t e", e=E)).then_inc(z["job_taken"], 1)
                    return
                if i == CHAIN_A:
                    V.tensor_copy(t_count[:].rearrange("p k t e -> p (k t e)"), misc[:, 0:2 * QT * E]
                                  ).then_inc(z["job_taken"], 1)
                    return
                if i < 12:
                    k = 0 if i <= 6 else 1
                    src = G if k == 0 else t_next[:]
                if i in (1, 7):
                    apart(dve)
                    ins = V.tensor_reduce(t_top[:, k, :], src, axis=AX.X, op=ALU.max)
                elif i in (2, 8):
                    ins = V.tensor_tensor(t_a[:], src, by_token(t_top[:, k, :]), ALU.is_equal)
                elif i in (3, 9):
                    ins = V.tensor_tensor(t_a[:], t_a[:], by_expert(rev[:]), ALU.mult)
                elif i in (4, 10):
                    ins = V.tensor_reduce(t_k[:, k, :], t_a[:], axis=AX.X, op=ALU.max)
                elif i in (5, 11):
                    ins = V.tensor_tensor(t_hot[:, k], by_expert(rev[:]), by_token(t_k[:, k, :]), ALU.is_equal)
                elif i == 6:
                    ins = V.scalar_tensor_tensor(out=t_next[:], in0=t_hot[:, 0], scalar=-BIG, in1=G,
                                                 op0=ALU.mult, op1=ALU.add)
                elif i == 12:
                    ins = V.tensor_tensor(t_pick[:], t_hot[:, 0], t_hot[:, 1], ALU.add)
                elif i == 13:
                    numbers = token_no[:, bass.ds(at(lambda j: QT * b(j)), QT)]
                    ins = V.tensor_copy(t_rows[:, par, :, D:D + 1].rearrange("p t o -> p (t o)"), numbers)
                elif i == 14:
                    ins = V.tensor_copy(t_rows[:, par, :, D + 1:D + 2].rearrange("p t o -> p (t o)"), t_k[:, 0, :])
                elif i == CHAIN_A + 1:
                    ins = V.tensor_tensor(t_from[:, 1, :], t_from[:, 0, :], t_count[:, 1, 0, :], ALU.add)
                elif i == CHAIN_A + 2:
                    ins = V.tensor_tensor(t_place[:], t_count[:, 0], t_from[:], ALU.add)
                elif i == CHAIN_A + 3:
                    ins = V.tensor_tensor(t_from[:, 0, :], t_from[:, 1, :], t_count[:, 1, 1, :], ALU.add)
                elif i == CHAIN_A + 4:
                    ins = V.tensor_tensor(t_hot_at[:], t_hot[:], t_place[:].rearrange("p (o t) e -> p o t e", o=1
                                                                                    ).broadcast_to([P, 2, QT, E]), ALU.mult)
                elif i == CHAIN_A + 5:
                    ins = V.tensor_reduce(t_place_f[:], t_hot_at[:], axis=AX.X, op=ALU.add)
                else:
                    if some(b, 1):
                        last = 1 if layer.diff else 0
                        if layer.diff:
                            dve.wait_ge(z["scattered"][1], at(lambda j: 64 * b(j)))
                        else:
                            for par in range(2):
                                dve.wait_ge(z["scattered"][par], at(lambda j: 64 * ((b(j) + 1 - par) // 2)))
                    ins = V.tensor_copy(t_pos[:], t_place_f[:])
                ins.then_inc(z["route_step"], 1)

            def emit(blk):
                at, live, some = blk.at, blk.live, blk.some
                for s in range(PAIR):
                    if blk.j == 0 and s == 1:
                        dve.wait_ge(late_init, LATE_INIT)
                        nc.vector.tensor_copy(t_from[:, 0, :], region[:]).then_inc(z["t_from_set"], 1)
                    if n == 1 and blk.j == -1 and s in MIX_AT:
                        mix(dve, 0, MIX_AT[s])
                    w, par = s % UNIT, s // UNIT
                    if n == 0 and blk.j == -1 and s == W_V + 1:
                        late_vector(dve)
                    gm = lambda j: PAIR * j + s + UNIT
                    c2 = s // 8 % 2
                    for t in range(QT):
                        if live(gm, layer.steps):
                            dve.wait_ge(z["mx_ready"], at(lambda j: 2 * gm(j) + t + 1))
                            if s % 8 == 0 and t == 0 and some(lambda j: gm(j) // 8, 2):
                                dve.wait_ge(z["mp_step"], at(lambda j: 4 * (gm(j) // 8 - 1)))
                            nc.vector.tensor_reduce(row_max[:, c2, t, s % 8:s % 8 + 1], maxs[t], axis=AX.X,
                                                    op=ALU.max, negate=True).then_inc(z["mx_taken"], 1)
                        if t == 0:
                            chain(blk, s, 0)
                    for name, u, no in blk.jobs(s):
                        if name == "ot":
                            second = layer.diff and layer.ends((s - P_OT) // UNIT)
                            got = misc.rearrange("p (m c) -> p m c", c=16)
                            den = got[:, :, HD:HD + 1].rearrange("p (t m) c -> p t (m c)", t=QT)
                            rd = r_den[:].rearrange("p t m -> p (t m)")
                            dve.wait_ge(z["job_ready"], at(lambda j: no(j) + 1))
                            base = (lambda j: 3 * (u(j) // 2) + (u(j) % 2)) if layer.diff else (lambda j: u(j))
                            nc.vector.reciprocal(r_den[:], den).then_inc(z["den_step"], 1)
                            dve.wait_ge(z["den_step"], at(lambda j: base(j) + 1))
                            if second:
                                nc.vector.tensor_tensor(r_den[:], r_den[:],
                                                        lam[:].rearrange("p (o m) -> p o m", o=1).broadcast_to([P, QT, H]),
                                                        ALU.mult).then_inc(z["den_step"], 1)
                                dve.wait_ge(z["den_step"], at(lambda j: base(j) + 2))
                            dst = o_first if layer.diff and not second else o_second
                            if layer.diff and some(u, 2):
                                dve.wait_ge(z["diffed"], at(lambda j: u(j) // 2))
                            if not layer.diff:
                                dst = o_norm[:].rearrange("p t (m d) -> p (t m) d", d=HD)
                                if some(u, 1):
                                    dve.wait_ge(z["job_ready"], at(lambda j: layer.order[("on", u(j) - 1)] + 1))
                            else:
                                dst = dst[:]
                            ins = nc.vector.tensor_tensor(dst, got[:, :, 0:HD],
                                                          rd.rearrange("p (m o) -> p m o", o=1).broadcast_to([P, QT * H, HD]),
                                                          ALU.mult)
                            ins.then_inc(z["job_taken"], 1)
                        elif name == "proj":
                            b = (lambda j: u(j) // 2) if layer.diff else u
                            dve.wait_ge(z["job_ready"], at(lambda j: no(j) + 1))
                            dve.wait_ge(z["res_ready"], at(lambda j: b(j) + 1))
                            rows = x_all[:, bass.ds(at(lambda j: QT * b(j)), QT), :]
                            nc.vector.tensor_tensor(rows, misc[:, 0:NQ].rearrange("p (t c) -> p t c", t=QT), rows, ALU.add
                                                    ).then_inc(z["job_taken"], 1)
                    v = lambda j: 2 * j + s // UNIT + 2
                    if w == 2 and layer.leads(par) and live(v, layer.units):
                        b = lambda j: layer.lead_no(v(j))
                        row = lambda b, t: x_all[:, bass.ds(at(lambda j: QT * b(j) + t), 1), :].rearrange("p t c -> p (t c)")
                        if n == 0:
                            dve.wait_ge(x_start, 32 if some(b, 1) else 16)
                        else:
                            dve.wait_ge(Z[0]["mixed"], at(lambda j: 4 * (b(j) + 1)))
                        for t in range(QT):
                            nc.vector.bn_stats(x_stat[:, t, :], row(b, t)).then_inc(z["ln_step"], 1)
                        dve.wait_ge(z["ln_step"], at(lambda j: 4 * b(j) + 2))
                        if some(b, 1):
                            dve.wait_ge(z["rstd_step"], at(lambda j: 2 * b(j)))
                        for t in range(QT):
                            apart(dve)
                            nc.vector.bn_aggr(x_mv[:, t, :], x_stat[:, t, :]).then_inc(z["ln_step"], 1)
                    if w == 4 and layer.leads(par) and live(v, layer.units):
                        b = lambda j: layer.lead_no(v(j))
                        dve.wait_ge(z["rstd_step"], at(lambda j: 2 * b(j) + 2))
                        if some(b, 1):
                            prev = lambda j: v(j) - (2 if layer.diff else 1)
                            dve.wait_ge(z["job_ready"], at(lambda j: layer.order[("xt", prev(j))] + 1))
                        for t in range(QT):
                            nc.vector.tensor_scalar(xn[:, t, :], x_all[:, bass.ds(at(lambda j: QT * b(j) + t), 1), :
                                                                       ].rearrange("p t c -> p (t c)"),
                                                    x_mv[:, t, 0:1], x_rstd[:, t:t + 1], ALU.subtract, ALU.mult
                                                    ).then_inc(z["xn_ready"], 1)
                    if (s - P_SUMS) % UNIT == 0 and layer.diff and layer.ends((s - P_SUMS) // UNIT):
                        uu = lambda j: 2 * j + (s - P_SUMS) // UNIT
                        if live(uu, layer.units):
                            dve.wait_ge(z["diffed"], at(lambda j: uu(j) // 2 + 1))
                            if some(uu, 2):
                                dve.wait_ge(z["rr_step"], at(lambda j: 2 * (uu(j) // 2)))
                            for t in range(QT):
                                if t or some(uu, 2):
                                    dve.wait_ge(z["ss_step"], at(lambda j: 2 * (uu(j) // 2) + t))
                                nc.vector.tensor_tensor_reduce(out=o_sq[:], in0=o_diff[:, t, :], in1=o_diff[:, t, :],
                                                               scale=1.0, scalar=0.0, op0=ALU.mult, op1=ALU.add,
                                                               accum_out=o_ss[:, t:t + 1]).then_inc(z["ss_step"], 1)
                    for p in (R_STATS, R_AGGR, R_ROWS):
                        u = lambda j, p=p: 2 * j + (s - p) // UNIT
                        b = lambda j, u=u: layer.batch(u(j))
                        if (s - p) % UNIT or not layer.ends((s - p) // UNIT) or not live(u, layer.units):
                            continue
                        row = lambda t, b=b: x_all[:, bass.ds(at(lambda j: QT * b(j) + t), 1), :].rearrange("p t c -> p (t c)")
                        if p == R_STATS:
                            dve.wait_ge(z["job_taken"], at(lambda j: layer.order[("proj", u(j))] + 1))
                            if some(b, 1):
                                dve.wait_ge(z["t_stats"], at(lambda j: 4 * b(j)))
                            apart(dve)
                            for t in range(QT):
                                nc.vector.bn_stats(t_stat[:, t, :], row(t)).then_inc(z["t_stats"], 1)
                        elif p == R_AGGR:
                            dve.wait_ge(z["t_stats"], at(lambda j: 4 * b(j) + 2))
                            if some(b, 1):
                                dve.wait_ge(z["t_rstds"], at(lambda j: 2 * b(j)))
                            for t in range(QT):
                                apart(dve)
                                nc.vector.bn_aggr(t_mv[:, t, :], t_stat[:, t, :]).then_inc(z["t_stats"], 1)
                        else:
                            dve.wait_ge(z["t_rstds"], at(lambda j: 2 * b(j) + 2))
                            par = layer.par(s, p)
                            if some(u, 2):
                                dve.wait_ge(z["scattered"][par], at(lambda j: 64 * (u(j) // 2)))
                                dve.wait_ge(z["job_ready"], at(lambda j: layer.order[("rt", u(j) - 2)] + 1))
                            for t in range(QT):
                                nc.vector.tensor_scalar(t_rows[:, par, t, 0:D], row(t), t_mv[:, t, 0:1],
                                                        t_rstd[:, t:t + 1], ALU.subtract, ALU.mult
                                                        ).then_inc(z["t_rows_ready"], 1)
                    chain(blk, s, 1)
            run_blocks(dve, layer, emit)

        def att_gpsimd(pool, layer):
            n, z = layer.n, S[layer.n]

            def split(blk, s, name, u, no):
                at, par = blk.at, s // UNIT
                cols, rest = ((slice(0, NK), rest_k) if name == "k" else (slice(NK, KQ), rest_q))
                k = 0 if name == "k" else 1
                part = [parts[:, par, i, cols] for i in range(3)]
                pool.wait_ge(z["a1_done"], at(lambda j: 2 * u(j) + k + 1))
                pool.wait_ge(z["job_taken"], at(lambda j: no(j) + 1))
                nc.gpsimd.tensor_tensor(rest[:], rest[:], part[0], ALU.subtract).then_inc(z["split_step"], 1)
                pool.wait_ge(z["split_step"], at(lambda j: 6 * u(j) + 3 * k + 1))
                apart(pool)
                nc.gpsimd.tensor_copy(part[1], rest[:]).then_inc(z["split_step"], 1)
                pool.wait_ge(z["split_step"], at(lambda j: 6 * u(j) + 3 * k + 2))
                nc.gpsimd.tensor_tensor(part[2], rest[:], part[1], ALU.subtract).then_inc(z["split_step"], 1)

            def emit(blk):
                at, live, some = blk.at, blk.live, blk.some
                for s in range(PAIR):
                    w, par = s % UNIT, s // UNIT
                    if n == 0 and blk.j == -1 and s == 9:
                        late_gpsimd(pool)
                    if blk.j in (n, n + 1) and s % 8 in (2, 4, 6):
                        e = 4 * (blk.j - n) + s // 8
                        if n == 1 and s % 8 == 2:
                            pool.wait_ge(Z[0]["mixed"], 4 * (e + 1))
                        load_expert(pool, n, e, s % 8 // 2 - 1)
                    if n == 0 and blk.j == 0 and s % 4 == 2 and s < 4 * ZERO_DMAS:
                        if s == 2:
                            pool.wait_ge(const_step, 3)
                        first = E * REGION + s // 4 * 8 * P
                        pool.dma_start(rows_in[first:first + 8 * P].rearrange("(s p q) c -> p s (q c)", p=P, q=QT),
                                       zero_rows[:].rearrange("p (o c) -> p o c", o=1).broadcast_to([P, 8 // QT, QT * WIDE])
                                       ).then_inc(rows_zero, 16)
                    bz = lambda j: j - 1
                    if n == 0 and s in (ZERO_AT, ZERO_AT + 1) and live(bz, B):
                        half = s - ZERO_AT
                        if half == 0 and some(bz, 1):
                            pool.wait_ge(z["scattered"][1], at(lambda j: 64 * bz(j)))
                            apart(pool)
                        dst = rows_in[half * 4 * REGION:(half + 1) * 4 * REGION].rearrange(
                            "(e b p s) c -> p e b (s c)", e=4, b=B, p=P)
                        pool.dma_start(dst[:, :, bass.ds(at(bz), 1), :].rearrange("p e b c -> p (e b) c"),
                                       zero_rows[:].rearrange("p (o c) -> p o c", o=1
                                                              ).broadcast_to([P, 4, QT * WIDE])
                                       ).then_inc(rows_zero, 16)
                    u = lambda j: 2 * j + (s - R_RSTD) // UNIT
                    b = lambda j, u=u: layer.batch(u(j))
                    if (s - R_RSTD) % UNIT == 0 and layer.ends((s - R_RSTD) // UNIT) and live(u, layer.units):
                        pool.wait_ge(z["t_stats"], at(lambda j: 4 * b(j) + 4))
                        if some(b, 1):
                            pool.wait_ge(z["t_rows_ready"], at(lambda j: QT * b(j)))
                        apart(pool)
                        nc.gpsimd.tensor_scalar(t_rstd[:], t_mv[:, :, 1:2].rearrange("p t o -> p (t o)"), LN_EPS,
                                                None, ALU.add).then_inc(z["t_rstds"], 1)
                        pool.wait_ge(z["t_rstds"], at(lambda j: 2 * b(j) + 1))
                        nc.gpsimd.tensor_tensor(t_rstd[:], t_rstd[:], half_neg[:, 0:QT], ALU.pow
                                                ).then_inc(z["t_rstds"], 1)
                    if s % 8 == 1:
                        c = lambda j: 4 * j + (s + 7) // 8
                        q = (s + 7) // 8 % 2
                        if live(c, 2 * layer.units):
                            pool.wait_ge(z["mx_taken"], at(lambda j: 16 * (c(j) + 1)))
                            if some(c, 2):
                                pool.wait_ge(z["job_ready"], at(lambda j: layer.order[("mt", c(j) - 2)] + 1))
                            part = [max_parts[:, q, :, k, :] for k in range(3)]
                            apart(pool)
                            nc.gpsimd.tensor_copy(part[0], row_max[:, q]).then_inc(z["mp_step"], 1)
                            pool.wait_ge(z["mp_step"], at(lambda j: 4 * c(j) + 1))
                            nc.gpsimd.tensor_tensor(max_rest[:], row_max[:, q], part[0], ALU.subtract
                                                    ).then_inc(z["mp_step"], 1)
                            pool.wait_ge(z["mp_step"], at(lambda j: 4 * c(j) + 2))
                            apart(pool)
                            nc.gpsimd.tensor_copy(part[1], max_rest[:]).then_inc(z["mp_step"], 1)
                            pool.wait_ge(z["mp_step"], at(lambda j: 4 * c(j) + 3))
                            nc.gpsimd.tensor_tensor(part[2], max_rest[:], part[1], ALU.subtract
                                                    ).then_inc(z["mp_step"], 1)
                    v = lambda j: 2 * j + s // UNIT + 2
                    if w == 3 and layer.leads(par) and live(v, layer.units):
                        b = lambda j: layer.lead_no(v(j))
                        pool.wait_ge(z["ln_step"], at(lambda j: 4 * b(j) + 4))
                        if some(b, 1):
                            pool.wait_ge(z["xn_ready"], at(lambda j: 2 * b(j)))
                        var = x_mv[:, :, 1:2].rearrange("p t o -> p (t o)")
                        apart(pool)
                        nc.gpsimd.tensor_scalar(x_rstd[:], var, LN_EPS, None, ALU.add).then_inc(z["rstd_step"], 1)
                        pool.wait_ge(z["rstd_step"], at(lambda j: 2 * b(j) + 1))
                        nc.gpsimd.tensor_tensor(x_rstd[:], x_rstd[:], half_neg[:, 0:QT], ALU.pow
                                                ).then_inc(z["rstd_step"], 1)
                    for f, sc in ((0, 11), (1, 3)):
                        vu = lambda j: 2 * j + s // UNIT + (1 if f == 0 else 0)
                        if w == sc and layer.leads(s // UNIT + (1 if f == 0 else 0)) and live(vu, layer.units):
                            pool.wait_ge(z["job_taken"], at(lambda j: layer.order[("v", vu(j))] + 1))
                            if some(vu, 1):
                                pool.wait_ge(z["pv_done"], at(lambda j: UNIT * vu(j) - (8 if f == 0 else 0)))
                            vp = (s // UNIT + (1 if f == 0 else 0)) % 2
                            for pp in range(2):
                                cols = slice(64 * f + 32 * pp, 64 * f + 32 * pp + 32)
                                dst = vpad[:, f, pp, :, :, 16 * pp:16 * pp + HD]
                                src = vals[:, vp, :, cols].rearrange("p t (i d) -> p t i d", i=4)
                                apart(pool)
                                if n == 0:
                                    ins = nc.gpsimd.tensor_copy(dst, src)
                                else:
                                    bias = bias_v[:, 1:2, cols].rearrange("p o (i d) -> p o i d", i=4)
                                    ins = nc.gpsimd.tensor_tensor(dst, src, bias.broadcast_to([P, KT, 4, HD]), ALU.add)
                                ins.then_inc(z["vpad_ready"], 1)
                    if (s - P_DIFF) % UNIT == 0 and layer.diff and layer.ends((s - P_DIFF) // UNIT):
                        uu = lambda j: 2 * j + (s - P_DIFF) // UNIT
                        if live(uu, layer.units):
                            pool.wait_ge(z["job_taken"], at(lambda j: layer.order[("ot", uu(j))] + 1))
                            if some(uu, 2):
                                pool.wait_ge(z["on_ready"], at(lambda j: QT * (uu(j) // 2)))
                                pool.wait_ge(z["ss_step"], at(lambda j: QT * (uu(j) // 2)))
                            nc.gpsimd.tensor_tensor(o_diff[:].rearrange("p t (m d) -> p (t m) d", d=HD),
                                                    o_first[:], o_second[:], ALU.subtract).then_inc(z["diffed"], 1)
                    if (s - P_RMS) % UNIT == 0 and layer.diff and layer.ends((s - P_RMS) // UNIT):
                        uu = lambda j: 2 * j + (s - P_RMS) // UNIT
                        if live(uu, layer.units):
                            bb = lambda j: uu(j) // 2
                            pool.wait_ge(z["ss_step"], at(lambda j: 2 * bb(j) + 2))
                            if some(bb, 1):
                                pool.wait_ge(z["on_ready"], at(lambda j: 2 * bb(j)))
                            apart(pool)
                            nc.gpsimd.tensor_scalar(o_rr[:], o_ss[:], 1.0 / D, RMS_EPS, ALU.mult, ALU.add
                                                    ).then_inc(z["rr_step"], 1)
                            pool.wait_ge(z["rr_step"], at(lambda j: 2 * bb(j) + 1))
                            nc.gpsimd.tensor_tensor(o_rr[:], o_rr[:], half_neg[:, 0:QT], ALU.pow
                                                    ).then_inc(z["rr_step"], 1)
                            pool.wait_ge(z["rr_step"], at(lambda j: 2 * bb(j) + 2))
                            if some(bb, 1):
                                pool.wait_ge(z["job_ready"], at(lambda j: layer.order[("on", uu(j) - 2)] + 1))
                            for t in range(QT):
                                apart(pool)
                                nc.gpsimd.tensor_scalar(o_norm[:, t, :], o_diff[:, t, :], o_rr[:, t:t + 1], None,
                                                        ALU.mult).then_inc(z["on_ready"], 1)
                    for name, u, no in blk.jobs(s):
                        if name in ("k", "q"):
                            split(blk, s, name, u, no)
                        if name == "on":
                            b = (lambda j: u(j) // 2) if layer.diff else u
                            if n == 0 and blk.j is not None and blk.j <= 1:
                                pool.wait_ge(bias_in, 16)
                            pool.wait_ge(z["xn_ready"], at(lambda j: QT * (b(j) + 1)))
                            rows = x_all[:, bass.ds(at(lambda j: QT * b(j)), QT), :]
                            nc.gpsimd.tensor_tensor(rows, rows, bias_o[:, n:n + 1, :].broadcast_to([P, QT, D]),
                                                    ALU.add).then_inc(z["res_ready"], 1)
                    u = lambda j: 2 * j + (s - R_SCATTER) // UNIT
                    b = lambda j, u=u: layer.batch(u(j))
                    if (s - R_SCATTER) % UNIT == 0 and layer.ends((s - R_SCATTER) // UNIT) and live(u, layer.units):
                        if n == 0:
                            pool.wait_ge(rows_zero, at(lambda j: 16 * (ZERO_DMAS + 2 * (b(j) + 1))))
                            apart(pool)
                        par = layer.par(s, R_SCATTER)
                        pool.wait_ge(z["route_step"], at(lambda j: CHAIN * b(j) + CHAIN))
                        apart(pool)
                        for t in range(QT):
                            for k in range(2):
                                nc.gpsimd.indirect_dma_start(
                                    out=rows_in, out_offset=bass.IndirectOffsetOnAxis(ap=t_pos[:, k, t:t + 1], axis=0),
                                    in_=t_rows[:, par, t, :], in_offset=None).then_inc(z["scattered"][par], 16)
            run_blocks(pool, layer, emit)

        for n in range(2):
            S[n]["ss_step"] = sem(f"ss_step{n}")

        def ffn_sems(n):
            names = ("expd route_step placed wt_done wt_copied rows_t rows_taken up_done act_done hid_done hid_t "
                     "hidT_taken down_done out_taken dest_step mixed stored").split()
            d = {k: sem(f"f_{k}{n}") for k in names}
            d["result_in"] = [sem(f"f_result_in{n}_{i}") for i in range(B)]
            d["rows_in"] = [sem(f"f_rows_in{n}_{i}") for i in range(4)]
            d["rows_out"] = [sem(f"f_rows_out{n}_{i}") for i in range(2)]
            return d

        Z = [ffn_sems(0), ffn_sems(1)]

        class Tiles:
            pairs = -(-SLOTS // 4)
            loops = 1
            tail = 1

        up_ps = [ps[:, 0, :], ps[:, 1, :]]
        gate_ps = [ps[:, 2, :], ps[:, 3, :]]
        hidT_ps = ps[:, 4, :]
        rowsT_ps = ps[:, 5, 0:P]
        down_ps = [ps[:, 6, 0:D], ps[:, 7, 0:D]]

        def x_tiles(ap):
            return ap.rearrange("b (t p) c -> p (b t) c", p=P)

        def ffn_sync(sp, n):
            z = Z[n]
            sp.wait_ge(S[n]["scattered"][1], 16 * 2 * TT // (1 if n == 0 else 2))
            if n == 1:
                sp.wait_ge(S[n]["scattered"][0], 16 * TT)
            sp.wait_ge(z["placed"], 2)
            src = rows_in.rearrange("(s p) c -> p s c", p=P)

            def emit(blk):
                at, live, some = blk.at, blk.live, blk.some
                for q in range(4):
                    t = lambda j: 4 * j + q + 2
                    if live(t, SLOTS):
                        i = (q + 2) % 4
                        if some(t, 4):
                            sp.wait_ge(z["rows_t"], at(lambda j: t(j) - 3))
                            apart(sp)
                            sp.wait_ge(z["dest_step"], at(lambda j: 4 * (t(j) - 3)))
                            apart(sp)
                        k = sp.value_load(block_of[0:1, bass.ds(at(t), 1)], min_val=0, max_val=BLOCKS - 1)
                        sp.dma_start(s_rows[:, i:i + 1, :], src[:, bass.ds(k, 1), :]).then_inc(z["rows_in"][i], 16)
            run_blocks(sp, Tiles, emit)
            for q in range(2):
                sp.wait_ge(z["rows_out"][q], 16 * ((SLOTS + 1 - q) // 2))
            for b in range(B):
                for k in range(2):
                    first = k * TOK + b * NQ
                    sp.dma_start(y_all[:, QT * (2 * b + k):QT * (2 * b + k + 1), :],
                                 results[first:first + NQ].rearrange("(t p) c -> p t c", p=P)
                                 ).then_inc(z["result_in"][b], 16)
                if n == 0 and b == 0:
                    sp.dma_start(ctx_sb[:], a["ctx_1024"][0].rearrange("(t p) c -> p t c", p=P)
                                 ).then_inc(S[1]["ctx_in"], 16)
            if n == 0:
                sp.wait_ge(bias_in, 16 * 7)
            else:
                for b in range(0, B, 2):
                    sp.wait_ge(z["mixed"], 4 * (b + 2))
                    sp.dma_start(x_tiles(out)[:, QT * b:QT * b + 4, :], x_all[:, QT * b:QT * b + 4, :]
                                 ).then_inc(z["stored"], 16)
                sp.wait_ge(z["stored"], 16 * B // 2)

        def ffn_gpsimd(pool, n):
            z = Z[n]

            def emit(blk):
                at, live = blk.at, blk.live
                for q in range(4):
                    t2 = lambda j: 4 * j + q - 2
                    if live(t2, SLOTS):
                        pool.wait_ge(z["dest_step"], at(lambda j: 4 * (t2(j) + 1)))
                        pool.wait_ge(z["out_taken"], at(lambda j: t2(j) + 1))
                        apart(pool)
                        i = (q - 2) % 4
                        nc.gpsimd.indirect_dma_start(
                            out=results, out_offset=bass.IndirectOffsetOnAxis(ap=s_place[:, i:i + 1], axis=0),
                            in_=s_out[:, q % 2, :], in_offset=None).then_inc(z["rows_out"][q % 2], 16)
            run_blocks(pool, Tiles, emit)
            for q in range(2):
                pool.wait_ge(z["rows_out"][q], 16 * ((SLOTS + 1 - q) // 2))

        def ffn_scalar(act, n):
            z = Z[n]
            def emit(blk):
                at, live, some = blk.at, blk.live, blk.some
                for q in range(4):
                    t = lambda j: 4 * j + q + 1
                    if live(t, SLOTS):
                        act.wait_ge(z["rows_t"], at(lambda j: t(j) + 1))
                        if some(t, 2):
                            act.wait_ge(z["up_done"], at(lambda j: t(j) - 1))
                        nc.scalar.copy(s_rowsT[:, (q + 1) % 2, :], rowsT_ps).then_inc(z["rows_taken"], 1)
                    t1 = lambda j: 4 * j + q - 1
                    if live(t1, SLOTS):
                        act.wait_ge(z["hid_t"], at(lambda j: t1(j) + 1))
                        if some(t1, 2):
                            act.wait_ge(z["down_done"], at(lambda j: t1(j) - 1))
                        nc.scalar.copy(s_hidT[:, (q + 1) % 2, :], hidT_ps).then_inc(z["hidT_taken"], 1)
                    t0 = lambda j: 4 * j + q
                    if live(t0, SLOTS):
                        act.wait_ge(z["up_done"], at(lambda j: t0(j) + 1))
                        if some(t0, 2):
                            act.wait_ge(z["hid_done"], at(lambda j: t0(j) - 1))
                        nc.scalar.activation(s_act[:, q % 2, :], up_ps[q % 2], ACT.Silu).then_inc(z["act_done"], 1)
            run_blocks(act, Tiles, emit)
            act.wait_ge(z["route_step"], EXP_AT[n])
            if n == 0:
                nc.scalar.activation(exps[:], below[:], ACT.Exp, scale=-1.0).then_inc(z["expd"], 1)
            else:
                nc.scalar.activation(exp_2[:], below_2[:], ACT.Exp, scale=-1.0).then_inc(z["expd"], 1)

        def ffn_tensor(pe, n):
            z = Z[n]
            pe.wait_ge(w_exp_in, 16 * W_EXP_DMAS[n])
            pe.wait_ge(z["placed"], 2)

            def emit(blk):
                at, live, some = blk.at, blk.live, blk.some
                for q in range(4):
                    t = lambda j: 4 * j + q + 1
                    if live(t, SLOTS):
                        cyc = lambda j: t(j) // 4 + 1
                        pe.wait_ge(z["rows_in"][(q + 1) % 4], at(lambda j: 16 * cyc(j)))
                        if some(t, 1):
                            pe.wait_ge(z["rows_taken"], at(t))
                        nc.tensor.transpose(rowsT_ps, s_rows[:, (q + 1) % 4, 0:D], ident[:]).then_inc(z["rows_t"], 1)
                    t0 = lambda j: 4 * j + q
                    if live(t0, SLOTS):
                        e = pe.value_load(expert_of[0:1, bass.ds(at(t0), 1)], min_val=0, max_val=E - 1)
                        pe.wait_ge(z["rows_taken"], at(lambda j: t0(j) + 1))
                        if some(t0, 2):
                            pe.wait_ge(z["act_done"], at(lambda j: t0(j) - 1))
                            pe.wait_ge(z["hid_done"], at(lambda j: t0(j) - 1))
                        for k, dst in ((0, up_ps[q % 2]), (1, gate_ps[q % 2])):
                            ins = nc.tensor.matmul(dst, s_rowsT[:, q % 2, :],
                                                   w_exp[:, k, bass.ds(e, 1), :].rearrange("p e f -> p (e f)"),
                                                   start=True, stop=True)
                        ins.then_inc(z["up_done"], 1)
                    t1 = lambda j: 4 * j + q - 1
                    if live(t1, SLOTS):
                        pe.wait_ge(z["hid_done"], at(lambda j: t1(j) + 1))
                        if some(t1, 1):
                            pe.wait_ge(z["hidT_taken"], at(t1))
                        for c in range(FC):
                            ins = nc.tensor.transpose(hidT_ps[:, c * P:(c + 1) * P],
                                                      s_hid[:, (q + 1) % 2, c * P:(c + 1) * P], ident[:])
                        ins.then_inc(z["hid_t"], 1)
                    t2 = lambda j: 4 * j + q - 2
                    if live(t2, SLOTS):
                        e = pe.value_load(expert_of[0:1, bass.ds(at(t2), 1)], min_val=0, max_val=E - 1)
                        pe.wait_ge(z["hidT_taken"], at(lambda j: t2(j) + 1))
                        if some(t2, 2):
                            pe.wait_ge(z["out_taken"], at(lambda j: t2(j) - 1))
                        for c in range(FC):
                            ins = nc.tensor.matmul(down_ps[q % 2], s_hidT[:, q % 2, c * P:(c + 1) * P],
                                                   w_exp[:, 2, bass.ds(e, 1), c * P:(c + 1) * P
                                                         ].rearrange("p e f -> p (e f)"),
                                                   start=(c == 0), stop=(c == FC - 1))
                        ins.then_inc(z["down_done"], 1)
            run_blocks(pe, Tiles, emit)

        EXP_AT = [None, None]

        def route(dve, n, part, dry=False):
            z = Z[n]
            count = [0]

            now = [0]

            def step(make):
                count[0] += 1
                if not dry and now[0] == part:
                    make().then_inc(z["route_step"], 1)
                    dve.wait_ge(z["route_step"], count[0])

            V = nc.vector
            by_token = lambda ap: ap.rearrange("p (t o) -> p t o", o=1).broadcast_to([P, TT, E])
            by_expert = lambda ap: ap.rearrange("p (o e) -> p o e", o=1).broadcast_to([P, TT, E])
            by_slot = lambda ap: ap.rearrange("p (o e) -> p o e", o=1).broadcast_to([P, SLOTS, E])
            step(lambda: V.tensor_tensor(count_e[:], t_from[:, 0, :], region[:], ALU.subtract))
            step(lambda: V.tensor_tensor(more[:], count_e[:].rearrange("p (e o) -> p e o", o=1).broadcast_to([P, E, TT]),
                                         full_rows[:].rearrange("p (o t) -> p o t", o=1).broadcast_to([P, E, TT]),
                                         ALU.is_gt))
            step(lambda: V.tensor_reduce(n_tiles[:], more[:], axis=AX.X, op=ALU.add))
            step(lambda: V.tensor_tensor_scan(tile_end[:], carry[:, 0:1, 1:1 + E].rearrange("p o t -> p (o t)"),
                                              n_tiles[:], 0.0, ALU.mult, ALU.add))
            step(lambda: V.tensor_tensor(tile_at[:], tile_end[:], n_tiles[:], ALU.subtract))
            step(lambda: V.tensor_tensor(done_e[:], by_slot(tile_end[:]),
                                         slot_no[:].rearrange("p (s o) -> p s o", o=1).broadcast_to([P, SLOTS, E]),
                                         ALU.is_le))
            step(lambda: V.tensor_reduce(tile_e[:], done_e[:], axis=AX.X, op=ALU.add))
            if not dry and part == 0:
                V.tensor_scalar(expert_of[:], tile_e[:], float(E - 1), None, ALU.min).then_inc(z["placed"], 1)
            step(lambda: V.scalar_tensor_tensor(out=shift[:], in0=region[:], scalar=1.0 / P, in1=tile_at[:],
                                                op0=ALU.mult, op1=ALU.subtract))
            step(lambda: V.memset(step_e[:], 0.0))
            step(lambda: V.tensor_tensor(step_e[:, 0:E - 1], shift[:, 1:E], shift[:, 0:E - 1], ALU.subtract))
            step(lambda: V.tensor_tensor(done_step[:], done_e[:], by_slot(step_e[:]), ALU.mult))
            step(lambda: V.tensor_reduce(block_f[:], done_step[:], axis=AX.X, op=ALU.add))
            if not dry and part == 0:
                V.tensor_tensor(block_of[:], block_f[:], slot_no[:], ALU.add).then_inc(z["placed"], 1)
            now[0] = 1
            step(lambda: V.tensor_scalar(tile_mark[:], tile_e[:], -1.0, float(E), ALU.mult, ALU.add))
            step(lambda: V.scalar_tensor_tensor(out=ends_at[:], in0=tile_at[:], scalar=float(P), in1=count_e[:],
                                                op0=ALU.mult, op1=ALU.add))
            step(lambda: V.memset(ends_step[:], 0.0))
            step(lambda: V.tensor_tensor(ends_step[:, 0:E - 1], ends_at[:, 1:E], ends_at[:, 0:E - 1], ALU.subtract))
            step(lambda: V.tensor_tensor(done_step[:], done_e[:], by_slot(ends_step[:]), ALU.mult))
            step(lambda: V.tensor_reduce(row_limit[:], done_step[:], axis=AX.X, op=ALU.add))
            step(lambda: V.tensor_scalar(row_limit[:], row_limit[:], ends_at[:, 0:1], None, ALU.add))
            step(lambda: V.scalar_tensor_tensor(out=row_limit[:], in0=slot_no[:], scalar=-float(P), in1=row_limit[:],
                                                op0=ALU.mult, op1=ALU.add))
            step(lambda: V.tensor_scalar(row_used[:], row_limit[:], token_no[:, 0:1], None, ALU.is_gt))
            step(lambda: V.tensor_scalar(row_spare[:], row_used[:], -1.0, 1.0, ALU.mult, ALU.add))
            step(lambda: V.tensor_scalar(spare_at[:], token_no[:, 0:1], float(2 * TOK), None, ALU.add))
            step(lambda: V.tensor_scalar(spare_no[:], slot_no[:], float(P), spare_at[:, 0:1], ALU.mult, ALU.add))
            step(lambda: V.tensor_tensor(row_spare[:], row_spare[:], spare_no[:], ALU.mult))
            for k, src in ((0, gate_s), (1, gate_s2)):
                step(lambda: V.tensor_reduce(top[:, k, :], src[:], axis=AX.X, op=ALU.max))
                if k == 0:
                    step(lambda: V.tensor_tensor(rt_a[:], src[:], by_token(top[:, k, :]), ALU.is_equal))
                    step(lambda: V.tensor_tensor(rt_a[:], rt_a[:], by_expert(rev[:]), ALU.mult))
                    step(lambda: V.tensor_reduce(rt_k[:], rt_a[:], axis=AX.X, op=ALU.max))
                    step(lambda: V.tensor_tensor(hot[:, k], by_expert(rev[:]), by_token(rt_k[:]), ALU.is_equal))
                    step(lambda: V.scalar_tensor_tensor(out=gate_s2[:], in0=hot[:, 0], scalar=-BIG, in1=gate_s[:],
                                                        op0=ALU.mult, op1=ALU.add))
            if n == 0:
                step(lambda: V.scalar_tensor_tensor(out=gate_abs[:], in0=gate_s[:], scalar=-1.0, in1=gate_s[:],
                                                    op0=ALU.mult, op1=ALU.max))
                for k, src in ((0, gate_s), (1, gate_s2)):
                    step(lambda: V.tensor_tensor(below[:, k], by_token(top[:, k, :]), src[:], ALU.subtract))
                    step(lambda: V.tensor_tensor(near[:, k], gate_abs[:], by_token(top[:, k, :]), ALU.max))
                    step(lambda: V.scalar_tensor_tensor(out=near[:, k], in0=near[:, k], scalar=0.02, in1=below[:, k],
                                                        op0=ALU.mult, op1=ALU.is_ge))
            else:
                step(lambda: V.tensor_tensor(below_2[:], top[:, 0, :], top[:, 1, :], ALU.subtract))
            EXP_AT[n] = count[0]
            now[0] = 2
            if not dry and part == 2:
                dve.wait_ge(z["expd"], 1)
            if n == 0:
                step(lambda: V.tensor_tensor(near[:], near[:], exps[:], ALU.mult))
                step(lambda: V.tensor_reduce(share_d[:], near[:], axis=AX.X, op=ALU.add))
                step(lambda: V.reciprocal(share[:], share_d[:]))
            else:
                step(lambda: V.tensor_scalar(share_d[:, 0, :], exp_2[:], 1.0, None, ALU.add))
                step(lambda: V.reciprocal(share[:, 0, :], share_d[:, 0, :]))
                step(lambda: V.tensor_tensor(share[:, 1, :], share[:, 0, :], exp_2[:], ALU.mult))

        for n in range(2):
            route(None, n, 0, dry=True)

        def ffn_vector(dve, n):
            z = Z[n]
            route(dve, n, 1)

            def emit(blk):
                at, live, some = blk.at, blk.live, blk.some
                for q in range(4):
                    t0 = lambda j: 4 * j + q
                    t2 = lambda j: 4 * j + q - 2
                    if live(t2, SLOTS):
                        dve.wait_ge(z["down_done"], at(lambda j: t2(j) + 1))
                        if some(t2, 2):
                            dve.wait_ge(z["rows_out"][q % 2], at(lambda j: 16 * (t2(j) // 2)))
                        nc.vector.tensor_copy(s_out[:, q % 2, :], down_ps[q % 2]).then_inc(z["out_taken"], 1)
                    if live(t0, SLOTS):
                        dve.wait_ge(z["act_done"], at(lambda j: t0(j) + 1))
                        if some(t0, 2):
                            dve.wait_ge(z["hid_t"], at(lambda j: t0(j) - 1))
                        nc.vector.tensor_tensor(s_hid[:, q % 2, :], gate_ps[q % 2], s_act[:, q % 2, :], ALU.mult
                                                ).then_inc(z["hid_done"], 1)
                        number, mark = s_rows[:, q, D:D + 1], s_rows[:, q, D + 1:D + 2]
                        dest, tile = s_dest[:, q:q + 1], bass.ds(at(t0), 1)
                        dve.wait_ge(z["rows_in"][q], at(lambda j: 16 * (t0(j) // 4 + 1)))
                        nc.vector.tensor_tensor(dest, mark, tile_mark[:, tile], ALU.not_equal).then_inc(z["dest_step"], 1)
                        dve.wait_ge(z["dest_step"], at(lambda j: 4 * t0(j) + 1))
                        nc.vector.scalar_tensor_tensor(out=dest, in0=dest, scalar=float(TOK), in1=number,
                                                       op0=ALU.mult, op1=ALU.add).then_inc(z["dest_step"], 1)
                        dve.wait_ge(z["dest_step"], at(lambda j: 4 * t0(j) + 2))
                        nc.vector.tensor_tensor(dest, dest, row_used[:, tile], ALU.mult).then_inc(z["dest_step"], 1)
                        dve.wait_ge(z["dest_step"], at(lambda j: 4 * t0(j) + 3))
                        if some(t0, 4):
                            dve.wait_ge(z["rows_out"][q % 2], at(lambda j: 16 * (t0(j) // 2 - 1)))
                        nc.vector.tensor_tensor(s_place[:, q:q + 1], dest, row_spare[:, tile], ALU.add
                                                ).then_inc(z["dest_step"], 1)
            run_blocks(dve, Tiles, emit)
            route(dve, n, 2)
            if n == 1:
                for b in range(B):
                    mix(dve, n, b)

        def next_phase(eng, k):
            eng.drain().then_inc(phase[k], 1)
            eng.wait_ge(phase[k], 5)

        @block.sync
        def _(sp):
            start_sync(sp)
            att_sync(sp, L[0])
            next_phase(sp, 0)
            ffn_sync(sp, 0)
            next_phase(sp, 1)
            att_sync(sp, L[1])
            next_phase(sp, 2)
            ffn_sync(sp, 1)

        @block.gpsimd
        def _(pool):
            start_gpsimd(pool)
            att_gpsimd(pool, L[0])
            next_phase(pool, 0)
            ffn_gpsimd(pool, 0)
            next_phase(pool, 1)
            att_gpsimd(pool, L[1])
            next_phase(pool, 2)
            ffn_gpsimd(pool, 1)

        @block.scalar
        def _(act):
            act.wait_ge(zero_done, 4)
            act.wait_ge(gp_init, GP_INIT)
            att_scalar(act, L[0])
            next_phase(act, 0)
            ffn_scalar(act, 0)
            next_phase(act, 1)
            att_scalar(act, L[1])
            next_phase(act, 2)
            ffn_scalar(act, 1)

        @block.vector
        def _(dve):
            start_vector(dve)
            dve.wait_ge(gp_init, GP_INIT)
            att_vector(dve, L[0])
            route(dve, 0, 0)
            next_phase(dve, 0)
            ffn_vector(dve, 0)
            next_phase(dve, 1)
            att_vector(dve, L[1])
            route(dve, 1, 0)
            next_phase(dve, 2)
            ffn_vector(dve, 1)

        @block.tensor
        def _(pe):
            start_tensor(pe)
            att_tensor(pe, L[0])
            next_phase(pe, 0)
            ffn_tensor(pe, 0)
            next_phase(pe, 1)
            att_tensor(pe, L[1])
            next_phase(pe, 2)
            ffn_tensor(pe, 1)


_INS = ["x", "ctx_1024",
        "L0_xattn_q1_w", "L0_xattn_q2_w", "L0_xattn_kv1_w", "L0_xattn_kv2_w", "L0_xattn_proj_w", "L0_xattn_proj_b",
        "L0_xattn_norm_w", "L0_xattn_lambda_1", "L0_xattn_lambda_2",
        "L0_ffn_gate_w", "L0_ffn_w1", "L0_ffn_w2", "L0_ffn_w3",
        "L1_xattn_W_q", "L1_xattn_b_q", "L1_xattn_W_k", "L1_xattn_b_k", "L1_xattn_W_v", "L1_xattn_b_v",
        "L1_xattn_W_o", "L1_xattn_b_o",
        "L1_ffn_gate_kernel", "L1_ffn_w0", "L1_ffn_w1", "L1_ffn_wo"]


def kernel(**inputs):
    import numpy as np
    import concourse.bacc as bacc
    from concourse.bass_utils import run_bass_kernel_spmd

    nc = bacc.Bacc("TRN2", target_bir_lowering=False, num_devices=1)
    arrays, aps = {}, {}
    for name in _INS:
        x = np.ascontiguousarray(inputs[name])
        arrays[f"in_{name}_dram"] = x
        aps[name] = nc.dram_tensor(f"in_{name}_dram", x.shape, mybir.dt.from_np(x.dtype), kind="ExternalInput").ap()
    out = nc.dram_tensor("out_dram", (B, NQ, D), F32, kind="ExternalOutput").ap()
    build(nc, aps, out)
    return run_bass_kernel_spmd(nc, [arrays], core_ids=[0]).results[0]["out_dram"]
```
